# Optimizing a Trainium2 kernel written in Bass

```python
import numpy as np
import jax
import jax.numpy as jnp

def _softmax(x, axis=-1):
    return jax.nn.softmax(x, axis=axis)

def _gelu(x):
    return jax.nn.gelu(x, approximate=True)

def _silu(x):
    return jax.nn.silu(x)

def _sigmoid(x):
    return jax.nn.sigmoid(x)

def _layernorm(x, axis=-1, eps=1e-05):
    m = jnp.mean(x, axis=axis, keepdims=True)
    v = jnp.var(x, axis=axis, keepdims=True)
    return (x - m) / jnp.sqrt(v + eps)

def _scatter_add(tgt, idx, src, axis=0):
    return tgt.at[idx].add(src)

def _segment_sum(src, seg, n):
    return jax.ops.segment_sum(src, seg, n)
kernel_name = 'mk_adj_ffn_d4_adj_r2_189101'

def setup_inputs(seed: int=0):
    np.random.seed(seed)
    _w = jnp.asarray

    def _rec_inputs():
        import jax
        import jax.numpy as jnp
        _gk = jax.random.key(seed)
        x = -0.0002928 + 1 * jax.random.normal(jax.random.fold_in(_gk, 1), (64, 128, 128), jnp.float32)
        _w = (1.0 + jnp.arange(128, dtype=jnp.float32)) ** (-0.5)
        _w = _w / _w.mean()
        _pij = jnp.clip(0.03125 * _w[:, None] * _w[None, :], 0.0, 1.0)
        _a = jax.random.uniform(jax.random.fold_in(_gk, 2), (128, 128)) < _pij
        _af = _a.astype(jnp.float32)
        adj = _af
        return (x, adj)
    x, adj = _rec_inputs()

    def _L0_gnn_setup():
        import jax, jax.numpy as jnp
        import numpy as np
        B, N, C, D = (8, 1024, 128, 128)
        NEG = -1e+16
        key = jax.random.key(seed)
        k1, k2, k3, k4, k5 = jax.random.split(key, 5)
        inputs = jax.random.normal(k1, (B, N, C), dtype=jnp.float32)
        graph = jax.random.bernoulli(k2, 0.5, (N, N)).astype(jnp.float32)
        W = jax.random.normal(k3, (C, D), dtype=jnp.float32) * (1.0 / np.sqrt(C))
        b_lin = jax.random.normal(k4, (D,), dtype=jnp.float32) * 0.02
        b = jax.random.normal(k5, (D,), dtype=jnp.float32)
        return {'inputs': inputs, 'graph': graph, 'W': W, 'b_lin': b_lin, 'b': b}
    _L0_gnn_all = _L0_gnn_setup()
    _L0_gnn_in = {k: v for k, v in _L0_gnn_all.items() if k in ('W', 'b_lin', 'b')}
    del _L0_gnn_all

    def _L0_ffn_setup():
        import jax, jax.numpy as jnp
        import numpy as np
        B, S, D, H, E, K = (8, 4096, 128, 512, 8, 2)
        key = jax.random.key(seed)
        ks = jax.random.split(key, 7)
        s_in = 1.0 / np.sqrt(D)
        s_hid = 1.0 / np.sqrt(H)
        return {'x': jax.random.normal(ks[0], (B, S, D), dtype=jnp.float32), 'Wg': jax.random.uniform(ks[1], (E, D), jnp.float32, -s_in, s_in), 'bg': jax.random.uniform(ks[2], (E,), jnp.float32, -s_in, s_in), 'W1': jax.random.uniform(ks[3], (E, H, D), jnp.float32, -s_in, s_in), 'b1': jax.random.uniform(ks[4], (E, H), jnp.float32, -s_in, s_in), 'W2': jax.random.uniform(ks[5], (E, D, H), jnp.float32, -s_hid, s_hid), 'b2': jax.random.uniform(ks[6], (E, D), jnp.float32, -s_hid, s_hid)}
    _L0_ffn_all = _L0_ffn_setup()
    _L0_ffn_in = {k: v for k, v in _L0_ffn_all.items() if k in ('Wg', 'bg', 'W1', 'b1', 'W2', 'b2')}
    del _L0_ffn_all

    def _L1_gnn_setup():
        import jax, jax.numpy as jnp
        import numpy as np
        B, T, D, H = (64, 1024, 128, 128)
        MAX_SKIP = 4

        def _lstm_last(Wih, Whh, bih, bhh, xs):
            N, _, Hd = xs.shape
            bias = bih + bhh

            def step(carry, x_t):
                h, c = carry
                g = x_t @ Wih.T + h @ Whh.T + bias
                i, f, gg, o = jnp.split(g, 4, axis=-1)
                c = jax.nn.sigmoid(f) * c + jax.nn.sigmoid(i) * jnp.tanh(gg)
                h = jax.nn.sigmoid(o) * jnp.tanh(c)
                return ((h, c), None)
            init = (jnp.zeros((N, Hd), xs.dtype), jnp.zeros((N, Hd), xs.dtype))
            (h_last, _), _ = jax.lax.scan(step, init, jnp.swapaxes(xs, 0, 1))
            return h_last
        key = jax.random.key(seed)
        ks = jax.random.split(key, 8)
        s = 0.05
        x = jax.random.normal(ks[0], (B, T, D), jnp.float32)
        adj = jax.random.uniform(ks[1], (T, T), jnp.float32) / T
        Wg0 = jax.random.normal(ks[2], (D, H), jnp.float32) * s
        bg0 = jnp.zeros((H,), jnp.float32)
        Wg1 = jax.random.normal(ks[3], (H, H), jnp.float32) * s
        bg1 = jnp.zeros((H,), jnp.float32)
        Wih = jax.random.normal(ks[4], (MAX_SKIP, 4 * H, H), jnp.float32) * s
        Whh = jax.random.normal(ks[5], (MAX_SKIP, 4 * H, H), jnp.float32) * s
        bih = jax.random.normal(ks[6], (MAX_SKIP, 4 * H), jnp.float32) * s
        bhh = jax.random.normal(ks[7], (MAX_SKIP, 4 * H), jnp.float32) * s
        return dict(x=x, adj=adj, Wg0=Wg0, bg0=bg0, Wg1=Wg1, bg1=bg1, Wih=Wih, Whh=Whh, bih=bih, bhh=bhh)
    _L1_gnn_all = _L1_gnn_setup()
    _L1_gnn_in = {k: v for k, v in _L1_gnn_all.items() if k in ('Wg0', 'bg0', 'Wg1', 'bg1', 'Wih', 'Whh', 'bih', 'bhh')}
    del _L1_gnn_all

    def _L1_ffn_setup():
        import jax, jax.numpy as jnp
        import numpy as np
        NUM_EXPERTS = 8
        TOP_K = 2
        B, S, D = (8, 4096, 128)

        def _moe(tokens, router_w, w1, b1, w2, b2):
            N = tokens.shape[0]
            E = router_w.shape[0]
            logits = tokens.astype(jnp.float32) @ router_w.astype(jnp.float32).T
            probs = jax.nn.softmax(logits, axis=-1)
            rw, re = jax.lax.top_k(probs, TOP_K)
            if TOP_K > 1:
                rw = rw / jnp.maximum(rw.sum(-1, keepdims=True), 1e-12)
            rw = rw.astype(tokens.dtype)
            combine = jnp.zeros((N, E), tokens.dtype).at[jnp.arange(N)[:, None], re].set(rw)
            out = tokens
            for e in range(E):
                h = jax.nn.gelu(tokens @ w1[e] + b1[e], approximate=False)
                y = h @ w2[e] + b2[e]
                out = out + combine[:, e:e + 1] * y
            return out
        key = jax.random.key(seed)
        ks = jax.random.split(key, 4)
        scale = 1.0 / np.sqrt(D).astype(np.float32)
        return {'input_embeddings': jax.random.normal(ks[0], (B, S, D), jnp.float32), 'router_w': jax.random.normal(ks[1], (NUM_EXPERTS, D), jnp.float32) * scale, 'w1': jax.random.normal(ks[2], (NUM_EXPERTS, D, D), jnp.float32) * scale, 'b1': jnp.zeros((NUM_EXPERTS, D), jnp.float32), 'w2': jax.random.normal(ks[3], (NUM_EXPERTS, D, D), jnp.float32) * scale, 'b2': jnp.zeros((NUM_EXPERTS, D), jnp.float32)}
    _L1_ffn_all = _L1_ffn_setup()
    _L1_ffn_in = {k: v for k, v in _L1_ffn_all.items() if k in ('router_w', 'w1', 'b1', 'w2', 'b2')}
    del _L1_ffn_all

    def _L2_gnn_setup():
        import jax, jax.numpy as jnp
        import numpy as np
        BT, N, D, HEADS, E = (512, 64, 128, 4, 256)
        LRELU_SLOPE = 0.2
        EPS = 1e-08
        key = jax.random.key(seed)
        ks = jax.random.split(key, 8)
        d = D
        return {'H': jax.random.normal(ks[0], (BT, N, d), jnp.float32), 'W_lin': jax.random.normal(ks[1], (d, d), jnp.float32) / np.sqrt(d).astype(np.float32), 'W_val': jax.random.normal(ks[2], (d, d), jnp.float32) / np.sqrt(d).astype(np.float32), 'a': jax.random.normal(ks[3], (HEADS, d // HEADS), jnp.float32), 'W_out': jax.random.normal(ks[4], (d, d), jnp.float32) / np.sqrt(d).astype(np.float32), 'A0': jax.random.uniform(ks[5], (N, N), jnp.float32), 'src': jax.random.randint(ks[6], (E,), 0, N, jnp.int32), 'dst': jax.random.randint(ks[7], (E,), 0, N, jnp.int32)}
    _L2_gnn_all = _L2_gnn_setup()
    _L2_gnn_in = {k: v for k, v in _L2_gnn_all.items() if k in ('W_lin', 'W_val', 'a', 'W_out', 'src', 'dst')}
    del _L2_gnn_all

    def _L2_ffn_setup():
        import jax, jax.numpy as jnp
        import numpy as np
        B, S, H, F, E, K = (8, 2048, 128, 256, 16, 2)
        EPS = 1e-05
        key = jax.random.key(seed)
        ks = jax.random.split(key, 9)
        sc = 0.02
        return {'x': jax.random.normal(ks[0], (B, S, H), dtype=jnp.float32), 'gate_w': jax.random.normal(ks[1], (H, E), dtype=jnp.float32) * sc, 'gate_b': jnp.zeros((E,), dtype=jnp.float32), 'w1': jax.random.normal(ks[2], (E, H, F), dtype=jnp.float32) * sc, 'b1': jnp.zeros((E, F), dtype=jnp.float32), 'w2': jax.random.normal(ks[3], (E, F, H), dtype=jnp.float32) * sc, 'b2': jnp.zeros((E, H), dtype=jnp.float32), 'gamma': jnp.ones((H,), dtype=jnp.float32), 'beta': jnp.zeros((H,), dtype=jnp.float32)}
    _L2_ffn_all = _L2_ffn_setup()
    _L2_ffn_in = {k: v for k, v in _L2_ffn_all.items() if k in ('gate_w', 'gate_b', 'w1', 'b1', 'w2', 'b2', 'gamma', 'beta')}
    del _L2_ffn_all

    def _L3_gnn_setup():
        import jax, jax.numpy as jnp
        import numpy as np
        B, J, F_IN, F_OUT = (8192, 17, 128, 128)
        key = jax.random.key(seed)
        k1, k2, k3, k4 = jax.random.split(key, 4)
        gain = 1.414
        bound = gain * np.sqrt(6.0 / (F_IN + F_OUT))
        W = jax.random.uniform(k2, (3, F_IN, F_OUT), dtype=jnp.float32, minval=-bound, maxval=bound)
        stdv = 1.0 / np.sqrt(F_OUT)
        bias = jax.random.uniform(k4, (F_OUT,), dtype=jnp.float32, minval=-stdv, maxval=stdv)
        return {'x': jax.random.normal(k1, (B, J, F_IN), dtype=jnp.float32), 'W': W, 'adj': jax.random.uniform(k3, (J, J), dtype=jnp.float32), 'bias': bias}
    _L3_gnn_all = _L3_gnn_setup()
    _L3_gnn_in = {k: v for k, v in _L3_gnn_all.items() if k in ('W', 'bias')}
    del _L3_gnn_all

    def _L3_ffn_setup():
        import jax, jax.numpy as jnp
        import numpy as np
        B, T, D, H, E = (16, 2048, 128, 256, 8)
        key = jax.random.key(seed)
        ks = jax.random.split(key, 5)
        x = jax.random.normal(ks[0], (B, T, D), dtype=jnp.float32)
        gate_w = jax.random.normal(ks[1], (D, E), dtype=jnp.float32) * 0.02
        gate_b = jnp.zeros((E,), dtype=jnp.float32)
        W1 = jax.random.normal(ks[2], (E, D, H), dtype=jnp.float32) * 0.02
        b1 = jnp.zeros((E, H), dtype=jnp.float32)
        W2 = jax.random.normal(ks[3], (E, H, D), dtype=jnp.float32) * 0.02
        b2 = jnp.zeros((E, D), dtype=jnp.float32)
        return {'x': x, 'gate_w': gate_w, 'gate_b': gate_b, 'W1': W1, 'b1': b1, 'W2': W2, 'b2': b2}
    _L3_ffn_all = _L3_ffn_setup()
    _L3_ffn_in = {k: v for k, v in _L3_ffn_all.items() if k in ('gate_w', 'gate_b', 'W1', 'b1', 'W2', 'b2')}
    del _L3_ffn_all
    return {'x': x, 'adj': adj, 'L0_gnn_W': _L0_gnn_in['W'], 'L0_gnn_b_lin': _L0_gnn_in['b_lin'], 'L0_gnn_b': _L0_gnn_in['b'], 'L0_ffn_Wg': _L0_ffn_in['Wg'], 'L0_ffn_bg': _L0_ffn_in['bg'], 'L0_ffn_W1': _L0_ffn_in['W1'], 'L0_ffn_b1': _L0_ffn_in['b1'], 'L0_ffn_W2': _L0_ffn_in['W2'], 'L0_ffn_b2': _L0_ffn_in['b2'], 'L1_gnn_Wg0': _L1_gnn_in['Wg0'], 'L1_gnn_bg0': _L1_gnn_in['bg0'], 'L1_gnn_Wg1': _L1_gnn_in['Wg1'], 'L1_gnn_bg1': _L1_gnn_in['bg1'], 'L1_gnn_Wih': _L1_gnn_in['Wih'], 'L1_gnn_Whh': _L1_gnn_in['Whh'], 'L1_gnn_bih': _L1_gnn_in['bih'], 'L1_gnn_bhh': _L1_gnn_in['bhh'], 'L1_ffn_router_w': _L1_ffn_in['router_w'], 'L1_ffn_w1': _L1_ffn_in['w1'], 'L1_ffn_b1': _L1_ffn_in['b1'], 'L1_ffn_w2': _L1_ffn_in['w2'], 'L1_ffn_b2': _L1_ffn_in['b2'], 'L2_gnn_W_lin': _L2_gnn_in['W_lin'], 'L2_gnn_W_val': _L2_gnn_in['W_val'], 'L2_gnn_a': _L2_gnn_in['a'], 'L2_gnn_W_out': _L2_gnn_in['W_out'], 'L2_gnn_src': _L2_gnn_in['src'], 'L2_gnn_dst': _L2_gnn_in['dst'], 'L2_ffn_gate_w': _L2_ffn_in['gate_w'], 'L2_ffn_gate_b': _L2_ffn_in['gate_b'], 'L2_ffn_w1': _L2_ffn_in['w1'], 'L2_ffn_b1': _L2_ffn_in['b1'], 'L2_ffn_w2': _L2_ffn_in['w2'], 'L2_ffn_b2': _L2_ffn_in['b2'], 'L2_ffn_gamma': _L2_ffn_in['gamma'], 'L2_ffn_beta': _L2_ffn_in['beta'], 'L3_gnn_W': _L3_gnn_in['W'], 'L3_gnn_bias': _L3_gnn_in['bias'], 'L3_ffn_gate_w': _L3_ffn_in['gate_w'], 'L3_ffn_gate_b': _L3_ffn_in['gate_b'], 'L3_ffn_W1': _L3_ffn_in['W1'], 'L3_ffn_b1': _L3_ffn_in['b1'], 'L3_ffn_W2': _L3_ffn_in['W2'], 'L3_ffn_b2': _L3_ffn_in['b2']}

def reference(x, adj, L0_gnn_W, L0_gnn_b_lin, L0_gnn_b, L0_ffn_Wg, L0_ffn_bg, L0_ffn_W1, L0_ffn_b1, L0_ffn_W2, L0_ffn_b2, L1_gnn_Wg0, L1_gnn_bg0, L1_gnn_Wg1, L1_gnn_bg1, L1_gnn_Wih, L1_gnn_Whh, L1_gnn_bih, L1_gnn_bhh, L1_ffn_router_w, L1_ffn_w1, L1_ffn_b1, L1_ffn_w2, L1_ffn_b2, L2_gnn_W_lin, L2_gnn_W_val, L2_gnn_a, L2_gnn_W_out, L2_gnn_src, L2_gnn_dst, L2_ffn_gate_w, L2_ffn_gate_b, L2_ffn_w1, L2_ffn_b1, L2_ffn_w2, L2_ffn_b2, L2_ffn_gamma, L2_ffn_beta, L3_gnn_W, L3_gnn_bias, L3_ffn_gate_w, L3_ffn_gate_b, L3_ffn_W1, L3_ffn_b1, L3_ffn_W2, L3_ffn_b2):
    import jax
    import jax.numpy as jnp

    def _L0_gnn_ref(inputs, graph, W, b_lin, b):
        import jax, jax.numpy as jnp
        import numpy as np
        B, N, C, D = (8, 1024, 128, 128)
        NEG = -1e+16
        h = jnp.einsum('bnc,cd->bnd', inputs, W) + b_lin
        scores = jnp.einsum('bnd,bmd->bnm', h, h) * graph[None, :, :]
        scores = jnp.where(scores == 0.0, NEG, scores)
        attention = jax.nn.softmax(scores, axis=2)
        return jnp.einsum('bnm,bmd->bnd', attention, h) + b

    def _L0_ffn_ref(x, Wg, bg, W1, b1, W2, b2):
        import jax, jax.numpy as jnp
        import numpy as np
        B, S, D, H, E, K = (8, 4096, 128, 512, 8, 2)
        gate_scores = jnp.einsum('bsd,ed->bse', x, Wg) + bg
        topk_scores, topk_idx = jax.lax.top_k(gate_scores, K)
        topk_probs = jax.nn.softmax(topk_scores, axis=-1)
        combine = jnp.sum(topk_probs[..., None] * jax.nn.one_hot(topk_idx, E, dtype=x.dtype), axis=-2)
        out = jnp.zeros_like(x)
        for e in range(E):
            h = jax.nn.relu(jnp.einsum('bsd,hd->bsh', x, W1[e]) + b1[e])
            y = jnp.einsum('bsh,dh->bsd', h, W2[e]) + b2[e]
            out = out + combine[..., e:e + 1] * y
        return out

    def _L1_gnn_ref(x, adj, Wg0, bg0, Wg1, bg1, Wih, Whh, bih, bhh):
        import jax, jax.numpy as jnp
        import numpy as np
        B, T, D, H = (64, 1024, 128, 128)
        MAX_SKIP = 4

        def _lstm_last(Wih, Whh, bih, bhh, xs):
            N, _, Hd = xs.shape
            bias = bih + bhh

            def step(carry, x_t):
                h, c = carry
                g = x_t @ Wih.T + h @ Whh.T + bias
                i, f, gg, o = jnp.split(g, 4, axis=-1)
                c = jax.nn.sigmoid(f) * c + jax.nn.sigmoid(i) * jnp.tanh(gg)
                h = jax.nn.sigmoid(o) * jnp.tanh(c)
                return ((h, c), None)
            init = (jnp.zeros((N, Hd), xs.dtype), jnp.zeros((N, Hd), xs.dtype))
            (h_last, _), _ = jax.lax.scan(step, init, jnp.swapaxes(xs, 0, 1))
            return h_last
        h = jax.nn.relu(jnp.einsum('ts,bsh->bth', adj, x @ Wg0 + bg0))
        h = jax.nn.relu(jnp.einsum('ts,bsh->bth', adj, h @ Wg1 + bg1))
        Bv, Tv, Hd = h.shape
        for p in range(1, MAX_SKIP + 1):
            nw = Tv // p
            wins = h[:, :nw * p, :].reshape(Bv * nw, p, Hd)
            last = _lstm_last(Wih[p - 1], Whh[p - 1], bih[p - 1], bhh[p - 1], wins)
            idx = jnp.arange(nw) * p + (p - 1)
            h = h.at[:, idx, :].set(last.reshape(Bv, nw, Hd))
        return h

    def _L1_ffn_ref(input_embeddings, router_w, w1, b1, w2, b2):
        import jax, jax.numpy as jnp
        import numpy as np
        NUM_EXPERTS = 8
        TOP_K = 2
        B, S, D = (8, 4096, 128)

        def _moe(tokens, router_w, w1, b1, w2, b2):
            N = tokens.shape[0]
            E = router_w.shape[0]
            logits = tokens.astype(jnp.float32) @ router_w.astype(jnp.float32).T
            probs = jax.nn.softmax(logits, axis=-1)
            rw, re = jax.lax.top_k(probs, TOP_K)
            if TOP_K > 1:
                rw = rw / jnp.maximum(rw.sum(-1, keepdims=True), 1e-12)
            rw = rw.astype(tokens.dtype)
            combine = jnp.zeros((N, E), tokens.dtype).at[jnp.arange(N)[:, None], re].set(rw)
            out = tokens
            for e in range(E):
                h = jax.nn.gelu(tokens @ w1[e] + b1[e], approximate=False)
                y = h @ w2[e] + b2[e]
                out = out + combine[:, e:e + 1] * y
            return out
        b, s, d = input_embeddings.shape
        tokens = input_embeddings.reshape(b * s, d)
        return _moe(tokens, router_w, w1, b1, w2, b2).reshape(b, s, d)

    def _L2_gnn_ref(H, W_lin, W_val, a, W_out, A0, src, dst):
        import jax, jax.numpy as jnp
        import numpy as np
        BT, N, D, HEADS, E = (512, 64, 128, 4, 256)
        LRELU_SLOPE = 0.2
        EPS = 1e-08
        bt, n, d = H.shape
        h, dh = a.shape
        Xq = (H @ W_lin.T).reshape(bt, n, h, dh)
        Xv = (H @ W_val.T).reshape(bt, n, h, dh)
        Qs = Xq[:, src]
        Kt = Xq[:, dst]
        e = jnp.einsum('behd,hd->beh', jax.nn.leaky_relu(Qs + Kt, LRELU_SLOPE), a)
        e = e + jnp.log(A0[src, dst] + EPS)[None, :, None]
        e_t = e.transpose(1, 0, 2)
        m = jax.ops.segment_max(e_t, src, num_segments=n)
        ex = jnp.exp(e_t - m[src])
        denom = jax.ops.segment_sum(ex, src, num_segments=n)
        attn = ex / denom[src]
        Vt = Xv[:, dst].transpose(1, 0, 2, 3)
        Y = jax.ops.segment_sum(attn[..., None] * Vt, src, num_segments=n)
        Y = Y.transpose(1, 0, 2, 3).reshape(bt, n, d)
        return Y @ W_out.T

    def _L2_ffn_ref(x, gate_w, gate_b, w1, b1, w2, b2, gamma, beta):
        import jax, jax.numpy as jnp
        import numpy as np
        B, S, H, F, E, K = (8, 2048, 128, 256, 16, 2)
        EPS = 1e-05
        gate_logits = x @ gate_w + gate_b
        topk_vals, topk_idx = jax.lax.top_k(gate_logits, K)
        topk_w = jax.nn.softmax(topk_vals, axis=-1)
        h = jax.nn.relu(jnp.einsum('bsh,ehf->bsef', x, w1) + b1)
        expert_out = jnp.einsum('bsef,efh->bseh', h, w2) + b2
        sel = jnp.take_along_axis(expert_out, topk_idx[:, :, :, None], axis=2)
        moe = jnp.sum(topk_w[..., None] * sel, axis=2)
        y = x + moe
        mu = jnp.mean(y, axis=-1, keepdims=True)
        var = jnp.var(y, axis=-1, keepdims=True)
        return (y - mu) / jnp.sqrt(var + EPS) * gamma + beta

    def _L3_gnn_ref(x, W, adj, bias):
        import jax, jax.numpy as jnp
        import numpy as np
        B, J, F_IN, F_OUT = (8192, 17, 128, 128)
        adj_0 = jnp.diag(jnp.diagonal(adj))
        adj_1 = jnp.triu(adj, k=1)
        adj_2 = jnp.tril(adj, k=-1)
        h = jnp.einsum('bjf,kfo->kbjo', x, W)
        out = jnp.einsum('ij,bjo->bio', adj_0, h[0]) + jnp.einsum('ij,bjo->bio', adj_1, h[1]) + jnp.einsum('ij,bjo->bio', adj_2, h[2])
        return out + bias[None, None, :]

    def _L3_ffn_ref(x, gate_w, gate_b, W1, b1, W2, b2):
        import jax, jax.numpy as jnp
        import numpy as np
        B, T, D, H, E = (16, 2048, 128, 256, 8)
        Bb, Tt, Dd = x.shape
        Ee = gate_w.shape[1]
        xf = x.reshape(-1, Dd)
        N = xf.shape[0]
        logits = xf @ gate_w + gate_b
        probs = jax.nn.softmax(logits, axis=-1)
        top2_vals, top2_idx = jax.lax.top_k(probs, 2)
        cw = jnp.zeros((N, Ee), dtype=xf.dtype).at[jnp.arange(N)[:, None], top2_idx].add(top2_vals)

        def step(acc, params):
            w1, bb1, w2, bb2, we = params
            h = jax.nn.gelu(xf @ w1 + bb1, approximate=False)
            y = h @ w2 + bb2
            return (acc + we[:, None] * y, None)
        out, _ = jax.lax.scan(step, jnp.zeros_like(xf), (W1, b1, W2, b2, cw.T))
        return out.reshape(Bb, Tt, Dd)
    x = x + _L0_gnn_ref(_layernorm(x, axis=-1), adj, L0_gnn_W, L0_gnn_b_lin, L0_gnn_b)
    x = x + _L0_ffn_ref(_layernorm(x, axis=-1), L0_ffn_Wg, L0_ffn_bg, L0_ffn_W1, L0_ffn_b1, L0_ffn_W2, L0_ffn_b2)
    x = x + _L1_gnn_ref(_layernorm(x, axis=-1), adj, L1_gnn_Wg0, L1_gnn_bg0, L1_gnn_Wg1, L1_gnn_bg1, L1_gnn_Wih, L1_gnn_Whh, L1_gnn_bih, L1_gnn_bhh)
    x = x + _L1_ffn_ref(_layernorm(x, axis=-1), L1_ffn_router_w, L1_ffn_w1, L1_ffn_b1, L1_ffn_w2, L1_ffn_b2)
    x = x + _L2_gnn_ref(_layernorm(x, axis=-1), L2_gnn_W_lin, L2_gnn_W_val, L2_gnn_a, L2_gnn_W_out, adj, L2_gnn_src, L2_gnn_dst)
    x = x + _L2_ffn_ref(_layernorm(x, axis=-1), L2_ffn_gate_w, L2_ffn_gate_b, L2_ffn_w1, L2_ffn_b1, L2_ffn_w2, L2_ffn_b2, L2_ffn_gamma, L2_ffn_beta)
    x = x + _L3_gnn_ref(_layernorm(x, axis=-1), L3_gnn_W, adj, L3_gnn_bias)
    x = x + _L3_ffn_ref(_layernorm(x, axis=-1), L3_ffn_gate_w, L3_ffn_gate_b, L3_ffn_W1, L3_ffn_b1, L3_ffn_W2, L3_ffn_b2)
    return x

_drawn_inputs = setup_inputs


def setup_inputs(seed=0):
    import zlib

    import numpy as np

    out = dict(_drawn_inputs(seed))
    spreads = {'L1_gnn_bg0': (0.0, 0.27),
     'L1_gnn_bg1': (0.0, 0.518),
     'L1_ffn_b1': (0.0, 0.461),
     'L1_ffn_b2': (0.0, 0.302),
     'L2_ffn_gate_b': (0.0, 0.566),
     'L2_ffn_b1': (0.0, 0.8),
     'L2_ffn_b2': (0.0, 0.405),
     'L2_ffn_gamma': (1.0, 0.2),
     'L2_ffn_beta': (0.0, 0.1),
     'L3_ffn_gate_b': (0.0, 0.8),
     'L3_ffn_b1': (0.0, 0.8),
     'L3_ffn_b2': (0.0, 0.8)}
    factors = {'L0_ffn_b1': 4.598,
     'L0_ffn_b2': 3.585,
     'L1_gnn_Whh': 8.0,
     'L1_gnn_bih': 3.751,
     'L1_gnn_bhh': 3.971,
     'L2_ffn_gate_w': 2.967,
     'L2_ffn_w1': 7.951,
     'L2_ffn_w2': 5.675,
     'L3_gnn_bias': 6.629,
     'L3_ffn_gate_w': 8.0,
     'L3_ffn_W1': 8.0,
     'L3_ffn_W2': 8.0}
    for name, (base, spread) in spreads.items():
        noise = np.random.default_rng([zlib.crc32(name.encode()), seed]).standard_normal(out[name].shape)
        drawn = base * np.exp(spread * noise) if base else spread * noise
        out[name] = jnp.asarray(drawn.astype(out[name].dtype))
    for name, factor in factors.items():
        out[name] = (out[name] * factor).astype(out[name].dtype)
    return out
```

```python
from contextlib import ExitStack

import concourse.bass as bass
from concourse import mybir

P = 128
NB = 64
GB = 4
NG = NB // GB
COLS = GB * P
EPS = 1e-5

ALU = mybir.AluOpType
ACT = mybir.ActivationFunctionType
AX = mybir.AxisListType
F32 = mybir.dt.float32
F32R = mybir.dt.float32r
BF16 = mybir.dt.bfloat16
U32 = mybir.dt.uint32
I32 = mybir.dt.int32


class Group:

    def __init__(self, n, odd, least):
        self.n, self.odd, self.least = n, odd, least

    def __mul__(self, k):
        return self.n * k

    def __add__(self, k):
        return self.n + k

    def __sub__(self, k):
        return self.n - k

    def next(self):
        return Group(self.n + 1, 1 - self.odd, self.least + 1)

    def last(self):
        return Group(self.n - 1, 1 - self.odd, self.least - 1)


def group_number(n):
    return Group(n, n % 2, n)


def over_groups(engine, group, count=NG):
    first, end = group_number(0), group_number(count - 1)
    group(first, None, first.next())
    with engine.Fori(0, (count - 2) // 2) as i:
        g = Group(i * 2 + 1, 1, 1)
        group(g, g.last(), g.next())
        g = g.next()
        group(g, g.last(), g.next())
    group(end, end.last(), None)


def over_groups_wide(engine, group, count=NG):
    for n in (0, 1):
        group(group_number(n), group_number(n - 1) if n else None, group_number(n + 1))
    with engine.Fori(0, (count - 4) // 2) as i:
        g = Group(i * 2 + 2, 0, 2)
        group(g, g.last(), g.next())
        g = g.next()
        group(g, g.last(), g.next())
    for n in (count - 2, count - 1):
        group(group_number(n), group_number(n - 1), group_number(n + 1) if n < count - 1 else None)


def wait_apart(dve, sem, value, scratch):
    dve.wait_ge(sem, value)
    dve.memset(scratch[:, 0:1], 0.0)


def tile_of(buf, b):
    return buf[:, b * P:(b + 1) * P]


def graph_of(x, g, b):
    return x[:, bass.ds((g * GB + b) * P, P)]


def group_of(x, g):
    return x[:, bass.ds(g * COLS, COLS)]


def by_graph(ap):
    return ap.rearrange("p (b d) -> p b d", b=GB)


class Phase:

    def __init__(self, nc, tag):
        self.nc, self.tag, self.sems = nc, tag, []

    def __enter__(self):
        self.ctx = ExitStack()
        return self

    def sem(self, name):
        s = self.ctx.enter_context(self.nc.semaphore(f"{self.tag}_{name}"))
        self.sems.append(s)
        return s

    def sb(self, name, shape, dt=F32):
        return self.ctx.enter_context(self.nc.sbuf_tensor(f"{self.tag}_{name}", shape, dt))

    def bank(self, name):
        return self.ctx.enter_context(self.nc.psum_tensor(f"{self.tag}_{name}", [P, COLS], F32))

    def __exit__(self, *failed):
        if failed[0] is None:
            for s in self.sems:
                self.nc.gpsimd.sem_clear(s)
            self.nc.all_engine_barrier()
        self.ctx.close()

class Norm:

    def __init__(self, ph, chip):
        self.x, self.minus_half, self.eps = chip.x, chip.minus_half, chip.eps
        self.scratch = ph.sb("scratch", [P, 1])
        self.stats = ph.sb("stats", [P, GB, 6])
        self.means = ph.sb("means", [P, GB, 2])
        self.var_eps = ph.sb("var_eps", [P, GB])
        self.rstd = ph.sb("rstd", [P, GB])
        self.xn = [ph.sb(f"xn{i}", [P, COLS]) for i in range(2)]
        self.stats_step = ph.sem("stats_step")
        self.rstd_step = ph.sem("rstd_step")
        self.xn_ready = ph.sem("xn_ready")

    def moments(self, dve, h):
        if h.least:
            dve.wait_ge(self.rstd_step, h * 2)
        for b in range(GB):
            op = dve.bn_stats(self.stats[:, b, :], graph_of(self.x, h, b))
        op.then_inc(self.stats_step, 1)
        wait_apart(dve, self.stats_step, h * 2 + 1, self.scratch)
        for b in range(GB):
            op = dve.bn_aggr(self.means[:, b, :], self.stats[:, b, :])
        op.then_inc(self.stats_step, 1)

    def deviation(self, pool, h):
        if h.least:
            pool.wait_ge(self.xn_ready, h.n)
        pool.wait_ge(self.stats_step, h * 2 + 2)
        pool.tensor_tensor(self.var_eps[:, :], self.means[:, :, 1], self.eps[:, :], ALU.add)\
            .then_inc(self.rstd_step, 1)
        pool.wait_ge(self.rstd_step, h * 2 + 1)
        pool.tensor_tensor(self.rstd[:, :], self.var_eps[:, :], self.minus_half[:, :], ALU.pow)\
            .then_inc(self.rstd_step, 1)

    def normalise(self, dve, h):
        dve.wait_ge(self.rstd_step, h * 2 + 2)
        for b in range(GB):
            op = dve.tensor_scalar(tile_of(self.xn[h.odd], b), graph_of(self.x, h, b), self.means[:, b, 0:1],
                                   self.rstd[:, b:b + 1], ALU.subtract, ALU.mult)
        op.then_inc(self.xn_ready, 1)


NEVER = -1e16


def attention(nc, chip, ins, load_next):
    with Phase(nc, "att") as ph:
        norm = Norm(ph, chip)
        x, xn = chip.x, norm.xn
        weight = ph.sb("weight", [P, P])
        xt = ph.sb("xt", [P, COLS])
        ht = [ph.sb(f"ht{i}", [P, COLS]) for i in range(2)]
        hn = [ph.sb(f"hn{i}", [P, COLS]) for i in range(2)]
        product = ph.sb("product", [P, COLS])
        barred = ph.sb("barred", [P, COLS])
        score = [ph.sb(f"score{i}", [P, COLS]) for i in range(2)]
        minus_max = [ph.sb(f"minus_max{i}", [P, GB]) for i in range(2)]
        prob = ph.sb("prob", [P, COLS])
        total = ph.sb("total", [P, GB])
        inverse = ph.sb("inverse", [P, GB])
        prob_t = ph.sb("prob_t", [P, COLS])
        turn, project, turn_h, scores, turn_p, mix = (ph.bank(n) for n in
                                                      ("turn", "project", "turn_h", "scores", "turn_p", "mix"))
        loaded = ph.sem("loaded")
        turn_ready = ph.sem("turn_ready")
        xt_ready = ph.sem("xt_ready")
        project_ready = ph.sem("project_ready")
        ht_ready = ph.sem("ht_ready")
        turn_h_ready = ph.sem("turn_h_ready")
        hn_ready = ph.sem("hn_ready")
        scores_ready = ph.sem("scores_ready")
        mask_step = ph.sem("mask_step")
        prob_ready = ph.sem("prob_ready")
        turn_p_ready = ph.sem("turn_p_ready")
        prob_t_ready = ph.sem("prob_t_ready")
        mix_ready = ph.sem("mix_ready")
        inverse_ready = ph.sem("inverse_ready")
        added = ph.sem("added")
        bias_added = ph.sem("bias_added")
        block = nc.Block()
        block.__enter__()

        @block.sync
        def _(sp):
            sp.dma_start(weight[:, :], ins["L0_gnn_W"]).then_inc(loaded, 16)
            load_next(sp)

        @block.tensor
        def _(pe):
            def turn_tokens(h):
                pe.wait_ge(norm.xn_ready, h + 1)
                if h.least:
                    pe.wait_ge(xt_ready, h.n)
                for b in range(GB):
                    mm = pe.transpose(tile_of(turn, b), tile_of(xn[h.odd], b), chip.ident[:, :])
                mm.then_inc(turn_ready, 1)

            def projection(h):
                pe.wait_ge(xt_ready, h + 1)
                if h.least:
                    pe.wait_ge(ht_ready, h.n)
                pe.matmul(project[:, :], weight[:, :], xt[:, :], start=True, stop=True).then_inc(project_ready, 1)

            def h_and_scores(h):
                pe.wait_ge(ht_ready, h + 1)
                if h.least:
                    pe.wait_ge(hn_ready, h.n)
                for b in range(GB):
                    mm = pe.transpose(tile_of(turn_h, b), tile_of(ht[h.odd], b), chip.ident[:, :])
                mm.then_inc(turn_h_ready, 1)
                if h.least:
                    pe.wait_ge(mask_step, h * 4 - 3)
                for b in range(GB):
                    hb = tile_of(ht[h.odd], b)
                    mm = pe.matmul(tile_of(scores, b), hb, hb, start=True, stop=True)
                mm.then_inc(scores_ready, 1)

            def turn_probs(g):
                pe.wait_ge(prob_ready, g + 1)
                if g.least:
                    pe.wait_ge(prob_t_ready, g.n)
                for b in range(GB):
                    mm = pe.transpose(tile_of(turn_p, b), tile_of(prob, b), chip.ident[:, :])
                mm.then_inc(turn_p_ready, 1)

            def mixture_of_h(g):
                pe.wait_ge(prob_t_ready, g + 1)
                pe.wait_ge(hn_ready, g + 1)
                if g.least:
                    pe.wait_ge(added, g.n)
                for b in range(GB):
                    mm = pe.matmul(tile_of(mix, b), tile_of(prob_t, b), tile_of(hn[g.odd], b), start=True, stop=True)
                mm.then_inc(mix_ready, 1)

            def group(g, behind, ahead):
                if ahead is not None:
                    turn_tokens(ahead)
                    projection(ahead)
                turn_probs(g)
                if ahead is not None:
                    h_and_scores(ahead)
                mixture_of_h(g)

            pe.wait_ge(loaded, 16)
            turn_tokens(group_number(0))
            projection(group_number(0))
            h_and_scores(group_number(0))
            over_groups(pe, group)

        @block.scalar
        def _(scalar):
            def take_turned(h):
                scalar.wait_ge(turn_ready, h + 1)
                if h.least:
                    scalar.wait_ge(project_ready, h.n)
                scalar.activation(xt[:, :], turn[:, :], ACT.Copy).then_inc(xt_ready, 1)

            def take_h(h):
                scalar.wait_ge(project_ready, h + 1)
                if h.least >= 2:
                    scalar.wait_ge(scores_ready, h - 1)
                scalar.activation(ht[h.odd][:, :], project[:, :], ACT.Identity, bias=chip.b_lin).then_inc(ht_ready, 1)

            def take_turned_h(h):
                scalar.wait_ge(turn_h_ready, h + 1)
                if h.least >= 2:
                    scalar.wait_ge(mix_ready, h - 1)
                scalar.activation(hn[h.odd][:, :], turn_h[:, :], ACT.Copy).then_inc(hn_ready, 1)

            def exponentials(g):
                scalar.wait_ge(mask_step, g * 4 + 4)
                if g.least:
                    scalar.wait_ge(turn_p_ready, g.n)
                    scalar.wait_ge(inverse_ready, g.n)
                for b in range(GB):
                    op = scalar.activation(tile_of(prob, b), tile_of(score[g.odd], b), ACT.Exp,
                                           bias=minus_max[g.odd][:, b:b + 1], accum_out=total[:, b:b + 1])
                op.then_inc(prob_ready, 1)

            def take_probs(g):
                scalar.wait_ge(turn_p_ready, g + 1)
                if g.least:
                    scalar.wait_ge(mix_ready, g.n)
                scalar.activation(prob_t[:, :], turn_p[:, :], ACT.Copy).then_inc(prob_t_ready, 1)

            def group(g, behind, ahead):
                exponentials(g)
                if ahead is not None:
                    take_turned(ahead)
                    take_h(ahead)
                take_probs(g)
                if ahead is not None:
                    take_turned_h(ahead)

            take_turned(group_number(0))
            take_h(group_number(0))
            take_turned_h(group_number(0))
            over_groups(scalar, group)

        @block.vector
        def _(dve):
            every_graph = chip.adj[:, :].unsqueeze(1).to_broadcast([P, GB, P])

            def mask(h):
                dve.wait_ge(scores_ready, h + 1)
                if h.least:
                    dve.wait_ge(mask_step, h * 4)
                dve.tensor_tensor(by_graph(product[:, :]), by_graph(scores[:, :]), every_graph, ALU.mult)\
                    .then_inc(mask_step, 1)
                dve.wait_ge(mask_step, h * 4 + 1)
                dve.tensor_scalar(barred[:, :], product[:, :], 0.0, NEVER, ALU.is_equal, ALU.mult)\
                    .then_inc(mask_step, 1)
                dve.wait_ge(mask_step, h * 4 + 2)
                if h.least >= 2:
                    dve.wait_ge(prob_ready, h - 1)
                dve.tensor_tensor(score[h.odd][:, :], product[:, :], barred[:, :], ALU.add).then_inc(mask_step, 1)
                dve.wait_ge(mask_step, h * 4 + 3)
                dve.tensor_reduce(minus_max[h.odd][:, :], by_graph(score[h.odd][:, :]), AX.X, ALU.max, negate=True)\
                    .then_inc(mask_step, 1)

            def add(g):
                dve.wait_ge(prob_ready, g + 1)
                if g.least:
                    dve.wait_ge(added, g.n)
                dve.reciprocal(inverse[:, :], total[:, :]).then_inc(inverse_ready, 1)
                dve.wait_ge(inverse_ready, g + 1)
                dve.wait_ge(mix_ready, g + 1)
                dve.wait_ge(bias_added, g + 1)
                for b in range(GB):
                    xb = graph_of(x, g, b)
                    op = dve.scalar_tensor_tensor(out=xb, in0=tile_of(mix, b), scalar=inverse[:, b:b + 1], in1=xb,
                                                  op0=ALU.mult, op1=ALU.add)
                op.then_inc(added, 1)

            def front(h):
                norm.moments(dve, h)
                if h.least >= 2:
                    dve.wait_ge(turn_ready, h - 1)
                norm.normalise(dve, h)

            def group(g, behind, ahead):
                if ahead is not None:
                    front(ahead)
                add(g)
                if ahead is not None:
                    mask(ahead)

            front(group_number(0))
            mask(group_number(0))
            over_groups(dve, group)

        @block.gpsimd
        def _(pool):
            def bias(g):
                pool.wait_ge(norm.xn_ready, g + 1)
                pool.tensor_tensor(by_graph(group_of(x, g)), by_graph(group_of(x, g)),
                                   chip.tables["L2"]["L0_b"].unsqueeze(1).to_broadcast([P, GB, P]), ALU.add)\
                    .then_inc(bias_added, 1)

            def group(g, behind, ahead):
                if ahead is not None:
                    norm.deviation(pool, ahead)
                bias(g)

            norm.deviation(pool, group_number(0))
            over_groups(pool, group)

        block.__exit__(None, None, None)


def three_hops(nc, chip, ins, load_next):
    with Phase(nc, "hops") as ph:
        norm = Norm(ph, chip)
        x, xn = chip.x, norm.xn
        weight = ph.sb("weight", [P, 3 * P])
        parts = ph.sb("parts", [P, 3 * P])
        near = [ph.sb(f"near{b}", [P, 3 * P]) for b in range(GB)]
        gather = [ph.bank(f"gather{b}") for b in range(GB)]
        out = [ph.bank(f"out{i}") for i in range(2)]
        loaded = ph.sem("loaded")
        parts_step = ph.sem("parts_step")
        gather_ready = ph.sem("gather_ready")
        near_ready = ph.sem("near_ready")
        near_ready_v = ph.sem("near_ready_v")
        out_ready = ph.sem("out_ready")
        added = ph.sem("added")
        bias_added = ph.sem("bias_added")
        block = nc.Block()
        block.__enter__()

        @block.sync
        def _(sp):
            sp.dma_start(weight[:, :].rearrange("f (k o) -> f k o", k=3), ins["L3_gnn_W"].rearrange("k f o -> f k o"))\
                .then_inc(loaded, 16)
            load_next(sp)

        @block.tensor
        def _(pe):
            def gathers(h):
                pe.wait_ge(norm.xn_ready, h + 1)
                for b in range(GB):
                    if h.least:
                        pe.wait_ge(near_ready_v if b % 2 else near_ready, h * 2 + b // 2 - 1)
                    pe.matmul(gather[b][:, 0:3 * P], tile_of(xn[h.odd], b), parts[:, :], start=True, stop=True)\
                        .then_inc(gather_ready, 1)

            def outs(g):
                if g.least >= 2:
                    pe.wait_ge(added, g - 1)
                for b in range(GB):
                    pe.wait_ge(near_ready_v if b % 2 else near_ready, g * 2 + b // 2 + 1)
                    for k in range(3):
                        mm = pe.matmul(tile_of(out[g.odd], b), near[b][:, k * P:(k + 1) * P],
                                       weight[:, k * P:(k + 1) * P], start=(k == 0), stop=(k == 2))
                    mm.then_inc(out_ready, 1)

            def group(g, behind, ahead):
                if ahead is not None:
                    gathers(ahead)
                outs(g)

            pe.wait_ge(loaded, 16)
            pe.wait_ge(parts_step, 3)
            gathers(group_number(0))
            over_groups(pe, group)

        def take(engine, copy, done, g, b):
            engine.wait_ge(gather_ready, g * GB + b + 1)
            if g.least:
                engine.wait_ge(out_ready, g * GB - GB + b + 1)
            copy(near[b][:, :], gather[b][:, 0:3 * P]).then_inc(done, 1)

        @block.scalar
        def _(scalar):
            def group(g, behind, ahead):
                for b in (0, 2):
                    take(scalar, lambda o, i: scalar.activation(o, i, ACT.Copy), near_ready, g, b)

            over_groups(scalar, group)

        @block.vector
        def _(dve):
            def front(h):
                norm.moments(dve, h)
                if h.least >= 2:
                    dve.wait_ge(gather_ready, h * GB - GB)
                norm.normalise(dve, h)

            def add(g):
                dve.wait_ge(out_ready, g * GB + GB)
                dve.wait_ge(bias_added, g + 1)
                dve.tensor_tensor(group_of(x, g), group_of(x, g), out[g.odd][:, :], ALU.add).then_inc(added, 1)

            def group(g, behind, ahead):
                for b in (1, 3):
                    take(dve, dve.tensor_copy, near_ready_v, g, b)
                if ahead is not None:
                    front(ahead)
                add(g)

            front(group_number(0))
            over_groups(dve, group)

        @block.gpsimd
        def _(pool):
            done = 0
            for k, compare, sign in ((0, ALU.is_equal, 1), (1, ALU.is_gt, 1), (2, ALU.is_gt, -1)):
                pool.affine_select(out=parts[:, k * P:(k + 1) * P], in_=chip.adj_t[:, :], compare_op=compare, fill=0.0,
                                   base=0, pattern=[[-sign, P]], channel_multiplier=sign).then_inc(parts_step, 1)

            def bias(g):
                pool.wait_ge(norm.xn_ready, g + 1)
                pool.tensor_tensor(by_graph(group_of(x, g)), by_graph(group_of(x, g)),
                                   chip.tables["L2"]["L3_b"].unsqueeze(1).to_broadcast([P, GB, P]), ALU.add)\
                    .then_inc(bias_added, 1)

            def group(g, behind, ahead):
                if ahead is not None:
                    norm.deviation(pool, ahead)
                bias(g)

            norm.deviation(pool, group_number(0))
            over_groups(pool, group)

        block.__exit__(None, None, None)



def recurrent(nc, chip, ins, load_next):
    with ExitStack() as keep:
        hidden = keep.enter_context(nc.sbuf_tensor("hidden", [P, NB * P], F32))
        lstm_w = keep.enter_context(nc.sbuf_tensor("lstm_w", [P, 2 * 16 * P], F32))
        lstm_loaded = keep.enter_context(nc.semaphore("lstm_loaded"))
        convolutions(nc, chip, ins, hidden, lstm_w, lstm_loaded)
        lstms(nc, chip, hidden, lstm_w, lstm_loaded, load_next)
        add_hidden(nc, chip, hidden)


def convolutions(nc, chip, ins, hidden, lstm_w, lstm_loaded):
    with Phase(nc, "conv") as ph:
        norm = Norm(ph, chip)
        x, xn = chip.x, norm.xn
        w0, w1 = ph.sb("w0", [P, P]), ph.sb("w1", [P, P])
        ones = ph.sb("ones", [P, P])
        bias0 = ph.sb("bias0", [P, P])
        near = ph.sb("near", [P, COLS])
        first_sum = ph.sb("first_sum", [P, COLS])
        first = ph.sb("first", [P, COLS])
        second = ph.sb("second", [P, COLS])
        gather, project0, project1, gather1, sums = (ph.bank(n) for n in
                                                     ("gather", "project0", "project1", "gather1", "sums"))
        loaded = ph.sem("loaded")
        ones_set = ph.sem("ones_set")
        sums_ready = ph.sem("sums_ready")
        bias0_ready = ph.sem("bias0_ready")
        gather_ready = ph.sem("gather_ready")
        near_ready = ph.sem("near_ready")
        project0_ready = ph.sem("project0_ready")
        sum0_ready = ph.sem("sum0_ready")
        first_ready = ph.sem("first_ready")
        project1_ready = ph.sem("project1_ready")
        second_ready = ph.sem("second_ready")
        gather1_ready = ph.sem("gather1_ready")
        hidden_ready = ph.sem("hidden_ready")
        block = nc.Block()
        block.__enter__()

        @block.sync
        def _(sp):
            sp.dma_start(w0[:, :], ins["L1_gnn_Wg0"]).then_inc(loaded, 16)
            sp.dma_start(w1[:, :], ins["L1_gnn_Wg1"]).then_inc(loaded, 16)
            for n, name in enumerate(("L1_gnn_Wih", "L1_gnn_Whh")):
                sp.dma_start(lstm_w[:, n * 16 * P:(n + 1) * 16 * P].rearrange("h (r d) -> h r d", d=P),
                             ins[name].rearrange("p (t h) d -> h (p t) d", h=P)).then_inc(lstm_loaded, 16)

        @block.gpsimd
        def _(pool):
            pool.memset(ones[:, :], 1.0).then_inc(ones_set, 1)
            norm.deviation(pool, group_number(0))

            def group(g, behind, ahead):
                if ahead is not None:
                    norm.deviation(pool, ahead)

            over_groups(pool, group)

        @block.tensor
        def _(pe):
            def gathers(h):
                pe.wait_ge(norm.xn_ready, h + 1)
                if h.least:
                    pe.wait_ge(near_ready, h.n)
                for b in range(GB):
                    mm = pe.matmul(tile_of(gather, b), tile_of(xn[h.odd], b), chip.adj_t[:, :], start=True, stop=True)
                mm.then_inc(gather_ready, 1)

            def first_projection(h):
                pe.wait_ge(near_ready, h + 1)
                if h.least:
                    pe.wait_ge(sum0_ready, h.n)
                pe.matmul(project0[:, :], w0[:, :], near[:, :], start=True, stop=True).then_inc(project0_ready, 1)

            def second_projection(g):
                pe.wait_ge(first_ready, g + 1)
                if g.least:
                    pe.wait_ge(second_ready, g.n)
                for b in range(GB):
                    mm = pe.matmul(tile_of(project1, b), tile_of(first, b), w1[:, :], start=True, stop=True)
                mm.then_inc(project1_ready, 1)

            def second_gathers(g):
                pe.wait_ge(second_ready, g + 1)
                if g.least:
                    pe.wait_ge(hidden_ready, g.n)
                for b in range(GB):
                    mm = pe.matmul(tile_of(gather1, b), tile_of(second, b), chip.adj_t[:, :], start=True, stop=True)
                mm.then_inc(gather1_ready, 1)

            def group(g, behind, ahead):
                if ahead is not None:
                    gathers(ahead)
                second_projection(g)
                if ahead is not None:
                    first_projection(ahead)
                second_gathers(g)

            pe.wait_ge(loaded, 32)
            pe.wait_ge(ones_set, 1)
            pe.matmul(sums[:, 0:P], ones[:, :], chip.adj_t[:, :], start=True, stop=True).then_inc(sums_ready, 1)
            gathers(group_number(0))
            first_projection(group_number(0))
            over_groups(pe, group)

        @block.scalar
        def _(scalar):
            def take_near(h):
                scalar.wait_ge(gather_ready, h + 1)
                if h.least:
                    scalar.wait_ge(project0_ready, h.n)
                scalar.activation(near[:, :], gather[:, :], ACT.Copy).then_inc(near_ready, 1)

            def take_first(h):
                scalar.wait_ge(sum0_ready, h + 1)
                if h.least:
                    scalar.wait_ge(project1_ready, h.n)
                scalar.activation(first[:, :], first_sum[:, :], ACT.Relu).then_inc(first_ready, 1)

            def take_hidden(g):
                scalar.wait_ge(gather1_ready, g + 1)
                scalar.activation(group_of(hidden, g), gather1[:, :], ACT.Relu).then_inc(hidden_ready, 1)

            def group(g, behind, ahead):
                if ahead is not None:
                    take_near(ahead)
                    take_first(ahead)
                take_hidden(g)

            take_near(group_number(0))
            take_first(group_number(0))
            over_groups(scalar, group)

        @block.vector
        def _(dve):
            def front(h):
                norm.moments(dve, h)
                if h.least >= 2:
                    dve.wait_ge(gather_ready, h - 1)
                norm.normalise(dve, h)

            def add_bias0(h):
                dve.wait_ge(project0_ready, h + 1)
                if h.least:
                    dve.wait_ge(first_ready, h.n)
                dve.tensor_tensor(by_graph(first_sum[:, :]), by_graph(project0[:, :]),
                                  bias0[:, :].unsqueeze(1).to_broadcast([P, GB, P]), ALU.add).then_inc(sum0_ready, 1)

            def add_bias1(g):
                dve.wait_ge(project1_ready, g + 1)
                if g.least:
                    dve.wait_ge(gather1_ready, g.n)
                dve.tensor_tensor(by_graph(second[:, :]), by_graph(project1[:, :]),
                                  chip.tables["L2"]["bg1"].unsqueeze(1).to_broadcast([P, GB, P]), ALU.add)\
                    .then_inc(second_ready, 1)

            def group(g, behind, ahead):
                add_bias1(g)
                if ahead is not None:
                    add_bias0(ahead)
                    if ahead.least < NG - 1:
                        front(ahead.next())

            dve.wait_ge(sums_ready, 1)
            dve.tensor_scalar(bias0[:, :], sums[:, 0:P], chip.bg0, None, ALU.mult).then_inc(bias0_ready, 1)
            front(group_number(0))
            front(group_number(1))
            dve.wait_ge(bias0_ready, 1)
            add_bias0(group_number(0))
            over_groups_wide(dve, group)

        block.__exit__(None, None, None)


LSTMS = ((1, 4), (2, 8), (3, 8), (4, 16))


def lstms(nc, chip, hidden, lstm_w, lstm_loaded, load_next):
    with Phase(nc, "lstm") as ph:
        weight = ph.sb("weight", [P, 2 * 16 * P])
        gates = [[ph.bank(f"gate{c}_{j}") for j in range(4)] for c in range(2)]
        value = [[ph.sb(f"value{c}_{j}", [P, COLS]) for j in range(4)] for c in range(2)]
        cell = [ph.sb(f"cell{c}", [P, COLS]) for c in range(2)]
        kept = [ph.sb(f"kept{c}", [P, COLS]) for c in range(2)]
        cell_tanh = [ph.sb(f"cell_tanh{c}", [P, COLS]) for c in range(2)]
        state = [ph.sb(f"state{c}", [P, COLS]) for c in range(2)]
        turned = ph.sem("turned")
        weights_ready = ph.sem("weights_ready")
        gate_ready = ph.sem("gate_ready")
        gate_done = ph.sem("gate_done")
        kept_step = ph.sem("kept_step")
        cell_ready = ph.sem("cell_ready")
        tanh_ready = ph.sem("tanh_ready")
        state_ready = ph.sem("state_ready")
        block = nc.Block()
        block.__enter__()
        ORDER = (0, 2, 1, 3)

        def gates_of(s):
            return [j for j in ORDER if s or j != 1]

        def over_units(engine, unit):
            units = later = gates_before = 0
            for p, graphs in LSTMS:
                pairs = NB // graphs // 2
                per_pair = 2 * sum(len(gates_of(s)) for s in range(p))

                def two(pair, opening):
                    u, at = pair * (2 * p) + units, pair * per_pair + gates_before
                    more = pair * (2 * p - 2) + later
                    n = 0
                    for s in range(p):
                        for c in range(2):
                            unit(p, graphs, pair, s, c, u + (2 * s + c), more + (2 * s - 2 + c), at + n,
                                 opening and s == 0)
                            n += len(gates_of(s))

                two(0, True)
                with engine.Fori(1, pairs) as pair:
                    two(pair, False)
                units += pairs * 2 * p
                later += pairs * 2 * (p - 1)
                gates_before += pairs * per_pair

        def windows(p, graphs, pair, c, s):
            n = P // p
            chunk = hidden[:, bass.ds((pair * 2 + c) * (graphs * P), graphs * P)].rearrange("h (b t) -> h b t", t=P)
            return chunk[:, :, s:s + p * (n - 1) + 1:p]

        def columns(buf, p, graphs):
            return buf[:, 0:graphs * (P // p)]

        def as_windows(buf, p, graphs):
            return columns(buf, p, graphs).rearrange("h (b w) -> h b w", b=graphs)

        @block.sync
        def _(sp):
            load_next(sp)

        @block.tensor
        def _(pe):
            pe.wait_ge(lstm_loaded, 32)
            for c in range(8):
                if c >= 8:
                    pe.wait_ge(weights_ready, c - 7)
                for b in range(GB):
                    mm = pe.transpose(tile_of(gates[c // 4][c % 4], b), tile_of(lstm_w[:, c * COLS:(c + 1) * COLS], b),
                                      chip.ident[:, :])
                mm.then_inc(turned, 1)
            pe.wait_ge(weights_ready, 8)

            def unit(p, graphs, pair, s, c, units, later, gates_before, opening):
                if not (p == 1 and opening):
                    behind = gates_before_last(p, s, c, opening)
                    pe.wait_ge(gate_done, gates_before - behind)
                if opening and p > 1 and c == 0:
                    pe.wait_ge(state_ready, units)
                for j in gates_of(s):
                    mm = pe.matmul(as_windows(gates[c][j], p, graphs), weight[:, ((p - 1) * 4 + j) * P:((p - 1) * 4 + j + 1) * P],
                                   windows(p, graphs, pair, c, s), start=True, stop=(s == 0))
                    if s == 0:
                        mm.then_inc(gate_ready, 1)
                if s:
                    pe.wait_ge(state_ready, units - 1)
                    for j in gates_of(s):
                        at = (16 + (p - 1) * 4 + j) * P
                        pe.matmul(columns(gates[c][j], p, graphs), weight[:, at:at + P], columns(state[c], p, graphs),
                                  start=False, stop=True).then_inc(gate_ready, 1)

            def gates_before_last(p, s, c, opening):
                if c == 1:
                    return len(gates_of(s))
                if s:
                    return len(gates_of(s - 1))
                return len(gates_of((p - 1) if not opening else (p - 2)))

            over_units(pe, unit)

        @block.scalar
        def _(scalar):
            for c in range(8):
                scalar.wait_ge(turned, c + 1)
                scalar.activation(weight[:, c * COLS:(c + 1) * COLS], gates[c // 4][c % 4][:, :], ACT.Copy)\
                    .then_inc(weights_ready, 1)

            def unit(p, graphs, pair, s, c, units, later, gates_before, opening):
                if not (p == 1 and opening):
                    scalar.wait_ge(state_ready, units - 1)
                for n, j in enumerate(gates_of(s)):
                    scalar.wait_ge(gate_ready, gates_before + (n + 1))
                    scalar.activation(columns(value[c][j], p, graphs), columns(gates[c][j], p, graphs),
                                      ACT.Tanh if j == 2 else ACT.Sigmoid,
                                      bias=chip.lstm_bias[:, (p - 1) * 4 + j:(p - 1) * 4 + j + 1]).then_inc(gate_done, 1)
                scalar.wait_ge(cell_ready, units + 1)
                scalar.activation(columns(cell_tanh[c], p, graphs), columns(cell[c], p, graphs), ACT.Tanh)\
                    .then_inc(tanh_ready, 1)

            over_units(scalar, unit)

        @block.vector
        def _(dve):
            def unit(p, graphs, pair, s, c, units, later, gates_before, opening):
                def cols(buf):
                    return columns(buf, p, graphs)

                i, f, g, o = (cols(value[c][j]) for j in range(4))
                if not (p == 1 and opening):
                    dve.wait_ge(cell_ready, units - 1)
                    dve.wait_ge(tanh_ready, units - 1)
                if s == 0:
                    dve.wait_ge(gate_done, gates_before + 2)
                    dve.tensor_tensor(cols(cell[c]), i, g, ALU.mult).then_inc(cell_ready, 1)
                else:
                    dve.wait_ge(gate_done, gates_before + 2)
                    dve.tensor_tensor(cols(kept[c]), i, g, ALU.mult).then_inc(kept_step, 1)
                    dve.wait_ge(gate_done, gates_before + 3)
                    dve.tensor_tensor(cols(cell[c]), cols(cell[c]), f, ALU.mult).then_inc(kept_step, 1)
                    dve.wait_ge(kept_step, later * 2 + 2)
                    dve.tensor_tensor(cols(cell[c]), cols(cell[c]), cols(kept[c]), ALU.add).then_inc(cell_ready, 1)
                dve.wait_ge(tanh_ready, units + 1)
                if s < p - 1:
                    dve.tensor_tensor(cols(state[c]), o, cols(cell_tanh[c]), ALU.mult).then_inc(state_ready, 1)
                else:
                    dve.tensor_tensor(windows(p, graphs, pair, c, s), as_windows(value[c][3], p, graphs),
                                      as_windows(cell_tanh[c], p, graphs), ALU.mult).then_inc(state_ready, 1)

            over_units(dve, unit)

        block.__exit__(None, None, None)


def add_hidden(nc, chip, hidden):
    with Phase(nc, "fold") as ph:
        copy = [ph.sb(f"copy{i}", [P, COLS]) for i in range(2)]
        turn = [ph.bank(f"turn{i}") for i in range(2)]
        copy_ready = ph.sem("copy_ready")
        turn_ready = ph.sem("turn_ready")
        added = ph.sem("added")
        block = nc.Block()
        block.__enter__()

        @block.scalar
        def _(scalar):
            def group(g, behind, ahead):
                if g.least >= 2:
                    scalar.wait_ge(turn_ready, g - 1)
                scalar.activation(copy[g.odd][:, :], group_of(hidden, g), ACT.Copy).then_inc(copy_ready, 1)

            over_groups_wide(scalar, group)

        @block.tensor
        def _(pe):
            def group(g, behind, ahead):
                pe.wait_ge(copy_ready, g + 1)
                if g.least >= 2:
                    pe.wait_ge(added, g - 1)
                for b in range(GB):
                    mm = pe.transpose(tile_of(turn[g.odd], b), tile_of(copy[g.odd], b), chip.ident[:, :])
                mm.then_inc(turn_ready, 1)

            over_groups_wide(pe, group)

        @block.vector
        def _(dve):
            def group(g, behind, ahead):
                dve.wait_ge(turn_ready, g + 1)
                dve.tensor_tensor(group_of(chip.x, g), group_of(chip.x, g), turn[g.odd][:, :], ALU.add)\
                    .then_inc(added, 1)

            over_groups_wide(dve, group)

        block.__exit__(None, None, None)



HEADS = 4
EDGES = 256
ET = EDGES // P
ROWS = NB * HEADS
LRELU = 0.2
EDGE_EPS = 1e-8
FAR = -1e30


def edges(nc, chip, ins, load_next):
    with ExitStack() as keep:
        def kept(name, shape):
            return keep.enter_context(nc.sbuf_tensor(f"edge_{name}", shape, F32))

        t = Chip()
        t.loaded = keep.enter_context(nc.semaphore("edge_loaded"))
        t.at_src = kept("at_src", [P, EDGES])
        t.at_dst = kept("at_dst", [P, EDGES])
        t.at_both = kept("at_both", [P, EDGES])
        t.src_t = kept("src_t", [P, ET, P])
        t.last_t = kept("last_t", [P, ET, P])
        t.restart = kept("restart", [P, EDGES])
        t.log_adj = kept("log_adj", [P, ET])
        t.heads = kept("heads", [P, HEADS])
        t.weights = kept("weights", [P, 3 * P])
        t.values = kept("values", [P, NB * P])
        t.score = kept("score", [P, ET, ROWS])
        edge_tables(nc, chip, ins, t)
        edge_scores(nc, chip, t, load_next)
        edge_softmax(nc, chip, t)
        edge_sums(nc, chip, t)


def edge_tables(nc, chip, ins, t):
    with Phase(nc, "etab") as ph:
        ends = ph.sb("ends", [1, 2 * EDGES], I32)
        endsf = ph.sb("endsf", [1, 2 * EDGES])
        key = ph.sb("key", [1, EDGES])
        ones = ph.sb("ones", [P, P])
        count = ph.sb("count", [P, EDGES])
        own = ph.sb("own", [P, 1])
        heads_at = ph.sb("heads_at", [P, HEADS])
        a_col = ph.sb("a_col", [P, 1])
        raw_w = ph.sb("raw_w", [P, 3 * P])
        key_all = ph.sb("key_all", [P, EDGES])
        key_col = ph.sb("key_col", [P, 3 * ET])
        below = ph.sb("below", [P, ET, EDGES])
        rank = ph.sb("rank", [P, ET])
        perm = ph.sb("perm", [P, ET, EDGES])
        spread = ph.sb("spread", [P, 2 * ET, P])
        sorted_ends = ph.sb("sorted_ends", [P, 2, EDGES])
        is_last = ph.sb("is_last", [P, EDGES])
        dst_t = ph.sb("dst_t", [P, ET, P])
        last_of = ph.sb("last_of", [P, EDGES])
        adj_at = ph.sb("adj_at", [P, ET, P])
        adj_sum = ph.sb("adj_sum", [P, ET])
        banks = [ph.bank(f"bank{i}") for i in range(8)]
        loaded = ph.sem("loaded")
        pool_step = ph.sem("pool_step")
        step = ph.sem("step")
        product = ph.sem("product")
        logged = ph.sem("logged")
        block = nc.Block()
        block.__enter__()

        @block.sync
        def _(sp):
            for n, name in enumerate(("L2_gnn_src", "L2_gnn_dst")):
                sp.dma_start(ends[:, n * EDGES:(n + 1) * EDGES], ins[name].rearrange("(a e) -> a e", a=1))\
                    .then_inc(loaded, 16)
            for n, name in enumerate(("L2_gnn_W_lin", "L2_gnn_W_val", "L2_gnn_W_out")):
                sp.dma_start(tile_of(raw_w, n), ins[name]).then_inc(loaded, 16)
            sp.dma_start(a_col[:, :], ins["L2_gnn_a"].rearrange("h (d a) -> (h d) a", a=1)).then_inc(loaded, 16)

        @block.gpsimd
        def _(pool):
            pool.memset(ones[:, :], 1.0).then_inc(pool_step, 1)
            pool.memset(heads_at[:, :], 1.0).then_inc(pool_step, 1)
            pool.iota(count[:, :], [[1, EDGES]], base=0, channel_multiplier=0, allow_small_or_imprecise_dtypes=True)\
                .then_inc(pool_step, 1)
            pool.iota(own[:, :], [[1, 1]], base=0, channel_multiplier=1, allow_small_or_imprecise_dtypes=True)\
                .then_inc(pool_step, 1)
            pool.wait_ge(pool_step, 4)
            d = P // HEADS
            pool.affine_select(out=heads_at[:, :], in_=heads_at[:, :], compare_op=ALU.is_ge, fill=0.0, base=0,
                               pattern=[[-d, HEADS]], channel_multiplier=1).then_inc(pool_step, 1)
            pool.wait_ge(pool_step, 5)
            pool.affine_select(out=heads_at[:, :], in_=heads_at[:, :], compare_op=ALU.is_gt, fill=0.0, base=d,
                               pattern=[[d, HEADS]], channel_multiplier=-1).then_inc(pool_step, 1)

        @block.vector
        def _(dve):
            done = [0]

            def link(op):
                op.then_inc(step, 1)
                done[0] += 1
                dve.wait_ge(step, done[0])

            dve.wait_ge(loaded, 96)
            dve.wait_ge(pool_step, 6)
            link(dve.tensor_copy(endsf[:, :], ends[:, :]))
            link(dve.scalar_tensor_tensor(out=key[:, :], in0=endsf[:, 0:EDGES], scalar=float(EDGES),
                                          in1=count[0:1, :], op0=ALU.mult, op1=ALU.add))
            assert done[0] == 2
            link(dve.tensor_scalar(t.heads[:, :], heads_at[:, :], a_col[:, 0:1], None, ALU.mult))
            dve.wait_ge(product, 1)
            link(dve.tensor_copy(key_all[:, :], banks[0][:, 0:EDGES]))
            link(dve.tensor_copy(key_col[:, :], banks[1][:, 0:3 * ET]))
            link(dve.tensor_copy(t.weights[:, :], banks[2][:, 0:3 * P]))
            for e in range(ET):
                link(dve.tensor_scalar(below[:, e, :], key_all[:, :], key_col[:, e:e + 1], None, ALU.is_lt))
            link(dve.reduce_sum(rank[:, :], below[:, :, :], AX.X))
            for e in range(ET):
                link(dve.tensor_scalar(perm[:, e, :], count[:, :], rank[:, e:e + 1], None, ALU.is_equal))
            for n in range(2 * ET):
                link(dve.tensor_scalar(spread[:, n, :], ones[:, :], key_col[:, ET + n:ET + n + 1], None, ALU.mult))
            assert done[0] == 15
            dve.wait_ge(product, 2)
            link(dve.tensor_copy(sorted_ends[:, :, :], banks[3][:, :].rearrange("p (n e) -> p n e", n=2)))
            link(dve.tensor_scalar(t.at_src[:, :], sorted_ends[:, 0, :], own[:, 0:1], None, ALU.is_equal))
            link(dve.tensor_scalar(t.at_dst[:, :], sorted_ends[:, 1, :], own[:, 0:1], None, ALU.is_equal))
            link(dve.tensor_tensor(t.at_both[:, :], t.at_src[:, :], t.at_dst[:, :], ALU.add))
            link(dve.memset(is_last[:, :], 1.0))
            link(dve.tensor_tensor(is_last[:, 0:EDGES - 1], sorted_ends[:, 0, 0:EDGES - 1], sorted_ends[:, 0, 1:EDGES],
                                   ALU.not_equal))
            link(dve.memset(t.restart[:, :], 0.0))
            link(dve.tensor_scalar(t.restart[:, 1:EDGES], is_last[:, 0:EDGES - 1], FAR, None, ALU.mult))
            link(dve.tensor_tensor(last_of[:, :], t.at_src[:, :], is_last[:, :], ALU.mult))
            assert done[0] == 24
            dve.wait_ge(product, 3)
            link(dve.tensor_copy(t.src_t[:, :, :], banks[4][:, 0:ET * P].rearrange("p (t n) -> p t n", t=ET)))
            link(dve.tensor_copy(dst_t[:, :, :], banks[5][:, 0:ET * P].rearrange("p (t n) -> p t n", t=ET)))
            link(dve.tensor_copy(t.last_t[:, :, :], banks[6][:, 0:ET * P].rearrange("p (t n) -> p t n", t=ET)))
            link(dve.tensor_tensor(adj_at[:, :, :], banks[7][:, 0:ET * P].rearrange("p (t n) -> p t n", t=ET),
                                   dst_t[:, :, :], ALU.mult))
            link(dve.reduce_sum(adj_sum[:, :], adj_at[:, :, :], AX.X))
            link(dve.tensor_scalar(adj_sum[:, :], adj_sum[:, :], EDGE_EPS, None, ALU.add))
            assert done[0] == 30

        @block.scalar
        def _(scalar):
            scalar.wait_ge(step, 30)
            scalar.activation(t.log_adj[:, :], adj_sum[:, :], ACT.Ln).then_inc(logged, 1)

        @block.tensor
        def _(pe):
            pe.wait_ge(step, 2)
            pe.matmul(banks[0][:, 0:EDGES], ones[0:1, :], key[:, :], start=True, stop=True)
            for e in range(ET):
                for n, row in enumerate((key, endsf, endsf)):
                    at = e * P + (EDGES if n == 2 else 0)
                    pe.matmul(banks[1][:, n * ET + e:n * ET + e + 1], row[:, at:at + P], ones[0:1, 0:1],
                              start=True, stop=True)
            for n in range(3):
                mm = pe.transpose(tile_of(banks[2], n), tile_of(raw_w, n), chip.ident[:, :])
            mm.then_inc(product, 1)
            pe.wait_ge(step, 15)
            for n in range(2):
                for e in range(ET):
                    mm = pe.matmul(banks[3][:, n * EDGES:(n + 1) * EDGES], spread[:, n * ET + e, :], perm[:, e, :],
                                   start=(e == 0), stop=(e == ET - 1))
            mm.then_inc(product, 1)
            pe.wait_ge(step, 24)
            for e in range(ET):
                pe.transpose(tile_of(banks[4], e), tile_of(t.at_src, e), chip.ident[:, :])
                pe.transpose(tile_of(banks[5], e), tile_of(t.at_dst, e), chip.ident[:, :])
                pe.transpose(tile_of(banks[6], e), tile_of(last_of, e), chip.ident[:, :])
                mm = pe.matmul(tile_of(banks[7], e), tile_of(t.at_src, e), chip.adj[:, :], start=True, stop=True)
            mm.then_inc(product, 1)

        block.__exit__(None, None, None)


def edge_scores(nc, chip, t, load_next):
    with Phase(nc, "esco") as ph:
        norm = Norm(ph, chip)
        xn = norm.xn
        xt = ph.sb("xt", [P, COLS])
        query = ph.sb("query", [P, COLS])
        small_sum = [ph.sb(f"small_sum{i}", [P, COLS]) for i in range(2)]
        leaky = [ph.sb(f"leaky{i}", [P, COLS]) for i in range(2)]
        turn, queries, values, score = (ph.bank(n) for n in ("turn", "queries", "values", "score"))
        sums = [ph.bank(f"sums{i}") for i in range(2)]
        turn_ready = ph.sem("turn_ready")
        xt_ready = ph.sem("xt_ready")
        query_ready = ph.sem("query_ready")
        value_ready = ph.sem("value_ready")
        query_taken = ph.sem("query_taken")
        value_taken = ph.sem("value_taken")
        sum_ready = ph.sem("sum_ready")
        small_ready = ph.sem("small_ready")
        leaky_ready = ph.sem("leaky_ready")
        score_ready = ph.sem("score_ready")
        score_taken = ph.sem("score_taken")
        block = nc.Block()
        block.__enter__()

        @block.sync
        def _(sp):
            load_next(sp)

        @block.gpsimd
        def _(pool):
            def group(g, behind, ahead):
                if ahead is not None:
                    norm.deviation(pool, ahead)

            norm.deviation(pool, group_number(0))
            over_groups(pool, group)

        @block.tensor
        def _(pe):
            def turn_tokens(h):
                pe.wait_ge(norm.xn_ready, h + 1)
                if h.least:
                    pe.wait_ge(xt_ready, h.n)
                for b in range(GB):
                    mm = pe.transpose(tile_of(turn, b), tile_of(xn[h.odd], b), chip.ident[:, :])
                mm.then_inc(turn_ready, 1)

            def project(h):
                pe.wait_ge(xt_ready, h + 1)
                if h.least:
                    pe.wait_ge(query_taken, h.n)
                for b in range(GB):
                    mm = pe.matmul(tile_of(queries, b), tile_of(xt, b), t.weights[:, 0:P], start=True, stop=True)
                mm.then_inc(query_ready, 1)
                if h.least:
                    pe.wait_ge(value_taken, h.n)
                for b in range(GB):
                    mm = pe.matmul(tile_of(values, b), tile_of(xt, b), t.weights[:, P:2 * P], start=True, stop=True)
                mm.then_inc(value_ready, 1)

            def sum_ends(h):
                pe.wait_ge(query_taken, h + 1)
                for i in range(2):
                    if h.least:
                        pe.wait_ge(leaky_ready, h * 2 - 1 + i)
                    for b in range(2):
                        mm = pe.matmul(sums[i][:, b * EDGES:(b + 1) * EDGES], tile_of(query, 2 * i + b),
                                       t.at_both[:, :], start=True, stop=True)
                    mm.then_inc(sum_ready, 1)

            def scores(g):
                if g.least:
                    pe.wait_ge(score_taken, g.n)
                for b in range(GB):
                    if b % 2 == 0:
                        pe.wait_ge(leaky_ready, g * 2 + b // 2 + 1)
                    for e in range(ET):
                        at = (b % 2) * EDGES + e * P
                        mm = pe.matmul(score[:, (e * GB + b) * HEADS:(e * GB + b + 1) * HEADS],
                                       leaky[b // 2][:, at:at + P], t.heads[:, :], start=True, stop=True)
                mm.then_inc(score_ready, 1)

            def group(g, behind, ahead):
                if ahead is not None:
                    turn_tokens(ahead)
                scores(g)
                if ahead is not None:
                    project(ahead)
                    sum_ends(ahead)

            turn_tokens(group_number(0))
            project(group_number(0))
            sum_ends(group_number(0))
            over_groups(pe, group)

        @block.scalar
        def _(scalar):
            def front(h):
                scalar.wait_ge(turn_ready, h + 1)
                if h.least:
                    scalar.wait_ge(value_ready, h.n)
                scalar.activation(xt[:, :], turn[:, :], ACT.Copy).then_inc(xt_ready, 1)
                scalar.wait_ge(query_ready, h + 1)
                if h.least:
                    scalar.wait_ge(sum_ready, h * 2)
                scalar.activation(query[:, :], queries[:, :], ACT.Copy).then_inc(query_taken, 1)

            def small(h):
                for i in range(2):
                    scalar.wait_ge(sum_ready, h * 2 + i + 1)
                    if h.least:
                        scalar.wait_ge(leaky_ready, h * 2 - 1 + i)
                    scalar.activation(small_sum[i][:, :], sums[i][:, :], ACT.Copy, scale=LRELU).then_inc(small_ready, 1)

            def group(g, behind, ahead):
                small(g)
                if ahead is not None:
                    front(ahead)

            front(group_number(0))
            over_groups(scalar, group)

        @block.vector
        def _(dve):
            def front(h):
                norm.moments(dve, h)
                if h.least >= 2:
                    dve.wait_ge(turn_ready, h - 1)
                norm.normalise(dve, h)

            def take_values(h):
                dve.wait_ge(value_ready, h + 1)
                dve.tensor_copy(group_of(t.values, h), values[:, :]).then_inc(value_taken, 1)

            def leak(h):
                for i in range(2):
                    dve.wait_ge(small_ready, h * 2 + i + 1)
                    if h.least:
                        dve.wait_ge(score_ready, h.n)
                    dve.tensor_tensor(leaky[i][:, :], sums[i][:, :], small_sum[i][:, :], ALU.max)\
                        .then_inc(leaky_ready, 1)

            def take_scores(g):
                dve.wait_ge(score_ready, g + 1)
                n = GB * HEADS
                for e in range(ET):
                    op = dve.tensor_scalar(t.score[:, e, bass.ds(g * n, n)], score[:, e * n:(e + 1) * n],
                                           t.log_adj[:, e:e + 1], None, ALU.add)
                op.then_inc(score_taken, 1)

            def group(g, behind, ahead):
                leak(g)
                if ahead is not None:
                    take_values(ahead)
                    if ahead.least < NG - 1:
                        front(ahead.next())
                take_scores(g)

            front(group_number(0))
            take_values(group_number(0))
            front(group_number(1))
            over_groups_wide(dve, group)

        block.__exit__(None, None, None)


def edge_softmax(nc, chip, t):
    with Phase(nc, "esof") as ph:
        rows = ph.sb("rows", [P, 2, EDGES])
        running = ph.sb("running", [P, 2, EDGES])
        running_t = ph.sb("running_t", [P, ET, ROWS])
        node_max = ph.sb("node_max", [P, ROWS])
        shifted = ph.sb("shifted", [P, ET, ROWS])
        expd = ph.sb("expd", [P, ET, ROWS])
        node_sum = ph.sb("node_sum", [P, ROWS])
        edge_inv = ph.sb("edge_inv", [P, ET, ROWS])
        turned, back, of_node, of_edge, sum_node, sum_edge = (ph.bank(n) for n in (
            "turned", "back", "of_node", "of_edge", "sum_node", "sum_edge"))
        product = ph.sem("product")
        step = ph.sem("step")
        exp_ready = ph.sem("exp_ready")
        block = nc.Block()
        block.__enter__()

        @block.tensor
        def _(pe):
            for r in range(2):
                for e in range(ET):
                    mm = pe.transpose(turned[:, r * EDGES + e * P:r * EDGES + (e + 1) * P],
                                      t.score[:, e, r * P:(r + 1) * P], chip.ident[:, :])
            mm.then_inc(product, 1)
            pe.wait_ge(step, 3)
            for r in range(2):
                for e in range(ET):
                    mm = pe.transpose(back[:, e * ROWS + r * P:e * ROWS + (r + 1) * P],
                                      running[:, r, e * P:(e + 1) * P], chip.ident[:, :])
            mm.then_inc(product, 1)
            pe.wait_ge(step, 4)
            for e in range(ET):
                mm = pe.matmul(of_node[:, 0:ROWS], t.last_t[:, e, :], running_t[:, e, :], start=(e == 0),
                               stop=(e == ET - 1))
            mm.then_inc(product, 1)
            pe.wait_ge(step, 5)
            for e in range(ET):
                mm = pe.matmul(of_edge[:, e * ROWS:(e + 1) * ROWS], tile_of(t.at_src, e), node_max[:, :],
                               start=True, stop=True)
            mm.then_inc(product, 1)
            pe.wait_ge(exp_ready, 1)
            for e in range(ET):
                mm = pe.matmul(sum_node[:, 0:ROWS], t.src_t[:, e, :], expd[:, e, :], start=(e == 0), stop=(e == ET - 1))
            mm.then_inc(product, 1)
            pe.wait_ge(step, 7)
            for e in range(ET):
                mm = pe.matmul(sum_edge[:, e * ROWS:(e + 1) * ROWS], tile_of(t.at_src, e), node_sum[:, :],
                               start=True, stop=True)
            mm.then_inc(product, 1)

        @block.vector
        def _(dve):
            def tiles(bank):
                return bank[:, :].rearrange("p (t r) -> p t r", t=2)

            dve.wait_ge(product, 1)
            dve.tensor_copy(rows[:, :, :], tiles(turned)).then_inc(step, 1)
            dve.wait_ge(step, 1)
            for r in range(2):
                dve.tensor_tensor_scan(running[:, r, :], t.restart[:, :], rows[:, r, :], FAR, ALU.add, ALU.max)\
                    .then_inc(step, 1)
            dve.wait_ge(product, 2)
            dve.tensor_copy(running_t[:, :, :], tiles(back)).then_inc(step, 1)
            dve.wait_ge(product, 3)
            dve.tensor_copy(node_max[:, :], of_node[:, 0:ROWS]).then_inc(step, 1)
            dve.wait_ge(product, 4)
            dve.tensor_tensor(shifted[:, :, :], t.score[:, :, :], tiles(of_edge), ALU.subtract).then_inc(step, 1)
            dve.wait_ge(product, 5)
            dve.tensor_copy(node_sum[:, :], sum_node[:, 0:ROWS]).then_inc(step, 1)
            dve.wait_ge(product, 6)
            dve.reciprocal(edge_inv[:, :, :], tiles(sum_edge)).then_inc(step, 1)
            dve.wait_ge(step, 8)
            dve.tensor_tensor(t.score[:, :, :], expd[:, :, :], edge_inv[:, :, :], ALU.mult).then_inc(step, 1)

        @block.scalar
        def _(scalar):
            scalar.wait_ge(step, 6)
            scalar.activation(expd[:, :, :], shifted[:, :, :], ACT.Exp).then_inc(exp_ready, 1)

        block.__exit__(None, None, None)


def edge_sums(nc, chip, t):
    with Phase(nc, "esum") as ph:
        weighed = [ph.sb(f"weighed{e}", [P, COLS]) for e in range(ET)]
        summed = ph.sb("summed", [P, COLS])
        at_edge = [ph.bank(f"at_edge{e}") for e in range(ET)]
        sums, out = ph.bank("sums"), ph.bank("out")
        at_edge_ready = ph.sem("at_edge_ready")
        weighed_ready = ph.sem("weighed_ready")
        sums_ready = ph.sem("sums_ready")
        summed_ready = ph.sem("summed_ready")
        out_ready = ph.sem("out_ready")
        added = ph.sem("added")
        block = nc.Block()
        block.__enter__()

        @block.tensor
        def _(pe):
            def gathers(h):
                for e in range(ET):
                    if h.least:
                        pe.wait_ge(weighed_ready, h * ET - ET + e + 1)
                    pe.matmul(at_edge[e][:, :], tile_of(t.at_dst, e), group_of(t.values, h), start=True, stop=True)\
                        .then_inc(at_edge_ready, 1)

            def segment_sums(g):
                pe.wait_ge(weighed_ready, g * ET + ET)
                if g.least:
                    pe.wait_ge(summed_ready, g.n)
                for b in range(GB):
                    for e in range(ET):
                        mm = pe.matmul(tile_of(sums, b), tile_of(weighed[e], b), t.src_t[:, e, :], start=(e == 0),
                                       stop=(e == ET - 1))
                mm.then_inc(sums_ready, 1)

            def outs(g):
                pe.wait_ge(summed_ready, g + 1)
                if g.least:
                    pe.wait_ge(added, g.n)
                for b in range(GB):
                    mm = pe.matmul(tile_of(out, b), tile_of(summed, b), t.weights[:, 2 * P:3 * P], start=True, stop=True)
                mm.then_inc(out_ready, 1)

            def group(g, behind, ahead):
                segment_sums(g)
                if ahead is not None:
                    gathers(ahead)
                outs(g)

            gathers(group_number(0))
            over_groups(pe, group)

        @block.scalar
        def _(scalar):
            def group(g, behind, ahead):
                scalar.wait_ge(sums_ready, g + 1)
                if g.least:
                    scalar.wait_ge(out_ready, g.n)
                scalar.activation(summed[:, :], sums[:, :], ACT.Copy).then_inc(summed_ready, 1)

            over_groups(scalar, group)

        @block.vector
        def _(dve):
            n = GB * HEADS

            def weigh(h):
                for e in range(ET):
                    dve.wait_ge(at_edge_ready, h * ET + e + 1)
                    if h.least:
                        dve.wait_ge(sums_ready, h.n)
                    dve.tensor_tensor(weighed[e][:, :].rearrange("e (r d) -> e r d", r=n),
                                      at_edge[e][:, :].rearrange("e (r d) -> e r d", r=n),
                                      t.score[:, e, bass.ds(h * n, n)].unsqueeze(2).to_broadcast([P, n, P // HEADS]),
                                      ALU.mult).then_inc(weighed_ready, 1)

            def add(g):
                dve.wait_ge(out_ready, g + 1)
                dve.tensor_tensor(group_of(chip.x, g), group_of(chip.x, g), out[:, :], ALU.add).then_inc(added, 1)

            def group(g, behind, ahead):
                if ahead is not None:
                    weigh(ahead)
                add(g)

            weigh(group_number(0))
            over_groups(dve, group)

        block.__exit__(None, None, None)

def mixture(nc, tag, chip, raw, raw_loaded, raw_count, tables, E, HT, act, weighting, residual, turned):
    K = E * HT
    THIRDS = 3 * E if 3 * E <= 32 else 96
    LAG = 3
    NH = LAG + 1
    W1_AT, W2_AT = 0, K * P
    late = 0 if K == 8 else 8
    S_STATS, S_NORM, S_TURN, S_LOW, S_GATE, S_ROUTE = (late + s for s in (0, 1, 2, 3, 3, 4))
    S_SPREAD = S_ROUTE + 5
    S_OUT, S_ADD, S_FINISH = LAG + 1, LAG + 2, LAG + 4
    full = weighting != "pair"
    EXP_AT = 11 + full
    ROUTE_STEPS = EXP_AT + 4 + 4 * (weighting == "renormed") + 7
    b1, b2s, gates, gate_bias, selector = (tables[n] for n in ("b1", "b2s", "gates", "gate_bias", "selector"))

    x = chip.x
    with Phase(nc, tag) as ph:
        sb, bank, sem = ph.sb, ph.bank, ph.sem

        high = sb("high", [P, 2 * K * P], F32R)
        low = sb("low", [P, 2 * K * P], F32R)
        scratch = sb("scratch", [P, 1])
        stats = sb("stats", [P, GB, 6])
        moments = sb("moments", [P, GB, 2])
        var_eps = sb("var_eps", [P, GB])
        rstd = sb("rstd", [P, GB])
        xn = [sb(f"xn{i}", [P, COLS]) for i in range(2)]
        xt = [sb(f"xt{i}", [P, COLS]) for i in range(2)]
        xt_high = [sb(f"xt_high{i}", [P, COLS], F32R) for i in range(2)]
        xt_low = [sb(f"xt_low{i}", [P, COLS], F32R) for i in range(2)]
        hid = [sb(f"hid{i}", [P, COLS]) for i in range(2)]
        scaled = [sb(f"scaled{i}", [P, COLS]) for i in range(NH)]
        hid_high = [sb(f"hid_high{i}", [P, COLS], F32R) for i in range(NH)]
        hid_low = [sb(f"hid_low{i}", [P, COLS], F32R) for i in range(NH)]
        weights_t = [sb(f"weights_t{i}", [3 * E, COLS], BF16) for i in range(2)]
        out_t = sb("out_t", [P, COLS])
        logits = sb("logits", [P, GB, E])
        top = sb("top", [P, GB, 8])
        top_at = sb("top_at", [P, GB, 8], U32)
        top_atf = sb("top_atf", [P, GB, 2])
        shifted = sb("shifted", [P, GB, 2])
        pair = sb("pair", [P, GB, 2])
        all_shifted = sb("all_shifted", [P, GB, E])
        all_exp = sb("all_exp", [P, GB, E])
        total = sb("total", [P, GB])
        inverse = sb("inverse", [P, GB])
        hot = sb("hot", [P, GB, 2, E])
        combine = sb("combine", [P, GB, E])
        left = sb("left", [P, GB, E])
        thirds = sb("thirds", [P, GB, THIRDS], BF16)
        if residual == "layernorm":
            mixed = sb("mixed", [P, COLS])
            normed = sb("normed", [P, COLS])
            mix_stats = sb("mix_stats", [P, GB, 6])
            mix_moments = sb("mix_moments", [P, GB, 2])
            mix_var = sb("mix_var", [P, GB])
            mix_rstd = sb("mix_rstd", [P, GB])

        up = [bank(f"up{i}") for i in range(2)]
        spread = [bank(f"spread{i}") for i in range(2)]
        down = bank("down")
        turn = bank("turn")
        small = bank("small")
        back = bank("back")

        w_turned = sem("w_turned")
        w_high = sem("w_high")
        w_low = sem("w_low")
        up_ready = sem("up_ready")
        hid_ready = sem("hid_ready")
        scaled_ready = sem("scaled_ready")
        high_ready = sem("high_ready")
        low_ready = sem("low_ready")
        down_ready = sem("down_ready")
        spread_ready = sem("spread_ready")
        stats_step = sem("stats_step")
        rstd_step = sem("rstd_step")
        xn_ready = sem("xn_ready")
        turn_ready = sem("turn_ready")
        xt_ready = sem("xt_ready")
        xt_low_ready = sem("xt_low_ready")
        gate_ready = sem("gate_ready")
        route_step = sem("route_step")
        exp_ready = sem("exp_ready")
        thirds_clear = sem("thirds_clear")
        thirds_turned = sem("thirds_turned")
        weights_ready = sem("weights_ready")
        out_ready = sem("out_ready")
        back_ready = sem("back_ready")
        added = sem("added")
        if residual == "normed":
            x_plus = sem("x_plus")
        if residual == "layernorm":
            mix_step = sem("mix_step")
            mix_rstd_step = sem("mix_rstd_step")
            mix_out = sem("mix_out")

        block = nc.Block()
        block.__enter__()

        CHUNKS = 2 * K // GB
        N_STATS = 2

        @block.tensor
        def _(pe):
            pe.wait_ge(raw_loaded, raw_count)
            if turned:
                for c in range(CHUNKS):
                    if c >= 2:
                        pe.wait_ge(w_high, c - 1)
                        pe.wait_ge(w_low, c - 1)
                    for b in range(GB):
                        mm = pe.transpose(tile_of(up[c % 2], b), tile_of(raw[:, c * COLS:(c + 1) * COLS], b),
                                          chip.ident[:, :])
                    mm.then_inc(w_turned, 1)

            def first_product(g, k):
                if k >= 2 or g.least:
                    pe.wait_ge(hid_ready, g * K + k - 1)
                if k == 0:
                    pe.wait_ge(xt_low_ready, g + 1)
                p = g.odd
                w = slice(W1_AT + k * P, W1_AT + (k + 1) * P)
                pe.matmul(up[k % 2][:, :], high[:, w], xt_high[p][:, :], start=True, stop=False)
                pe.matmul(up[k % 2][:, :], high[:, w], xt_low[p][:, :], start=False, stop=False)
                pe.matmul(up[k % 2][:, :], low[:, w], xt_high[p][:, :], start=False, stop=True)\
                    .then_inc(up_ready, 1)

            def spread_weight(g, e):
                if e >= 2 or g.least:
                    pe.wait_ge(scaled_ready, (g * E + e - 1) * HT)
                if e == 0:
                    pe.wait_ge(weights_ready, g + 1)
                pe.matmul(spread[e % 2][:, :], selector[:, e * P:(e + 1) * P], weights_t[g.odd][:, :],
                          start=True, stop=True).then_inc(spread_ready, 1)

            def second_product(g, k):
                if k == 0:
                    if g.least:
                        pe.wait_ge(out_ready, g.n)
                    for n in range(3):
                        pe.matmul(down[:, :], b2s[n][:, :], weights_t[g.odd][:, :],
                                  start=(n == 0), stop=False)
                pe.wait_ge(low_ready, g * K + k + 1)
                w = slice(W2_AT + k * P, W2_AT + (k + 1) * P)
                n = k % NH
                pe.matmul(down[:, :], high[:, w], hid_high[n][:, :], start=False, stop=False)
                pe.matmul(down[:, :], high[:, w], hid_low[n][:, :], start=False, stop=False)
                pe.matmul(down[:, :], low[:, w], hid_high[n][:, :], start=False, stop=(k == K - 1))\
                    .then_inc(down_ready, 1)

            def turn_tokens(h):
                pe.wait_ge(xn_ready, h + 1)
                if h.least:
                    pe.wait_ge(xt_ready, h.n)
                for b in range(GB):
                    mm = pe.transpose(tile_of(turn, b), tile_of(xn[h.odd], b), chip.ident[:, :])
                mm.then_inc(turn_ready, 1)

            def gate_products(h):
                pe.wait_ge(xt_ready, h + 1)
                if h.least:
                    pe.wait_ge(weights_ready, h.n)
                for b in range(GB):
                    mm = pe.matmul(small[:, b * E:(b + 1) * E], tile_of(xt[h.odd], b), gates[:, :],
                                   start=True, stop=True)
                mm.then_inc(gate_ready, 1)

            def turn_weights(h):
                pe.wait_ge(route_step, (h + 1) * ROUTE_STEPS)
                for b in range(GB):
                    mm = pe.transpose(tile_of(small[0:THIRDS, :].bitcast(BF16), b), thirds[:, b, :],
                                      chip.ident_bf[:, :])
                mm.then_inc(thirds_turned, 1)

            def turn_back(g):
                pe.wait_ge(out_ready, g + 1)
                if g.least:
                    pe.wait_ge(added, g.n)
                for b in range(GB):
                    mm = pe.transpose(tile_of(back, b), tile_of(out_t, b), chip.ident[:, :])
                mm.then_inc(back_ready, 1)

            def group(g, behind, ahead):
                for k in range(K):
                    first_product(g, k)
                    if k == 0 and S_SPREAD >= K:
                        turn_weights(g)
                    if k % HT == 0:
                        spread_weight(g, k // HT)
                    if k >= LAG:
                        second_product(g, k - LAG)
                    elif behind is not None:
                        second_product(behind, K - LAG + k)
                    if k == S_OUT and behind is not None:
                        turn_back(behind)
                    if ahead is not None:
                        if k == S_TURN:
                            turn_tokens(ahead)
                        if k == S_GATE:
                            gate_products(ahead)
                        if k == S_SPREAD:
                            turn_weights(ahead)

            pe.wait_ge(w_high, CHUNKS)
            pe.wait_ge(w_low, CHUNKS)
            turn_tokens(group_number(0))
            gate_products(group_number(0))
            if S_SPREAD < K:
                turn_weights(group_number(0))
            over_groups(pe, group)
            for k in range(K - LAG, K):
                second_product(group_number(NG - 1), k)
            turn_back(group_number(NG - 1))

        @block.scalar
        def _(scalar):
            scalar.wait_ge(raw_loaded, raw_count)
            for c in range(CHUNKS):
                if turned:
                    scalar.wait_ge(w_turned, c + 1)
                src = up[c % 2][:, :] if turned else raw[:, c * COLS:(c + 1) * COLS]
                scalar.activation(high[:, c * COLS:(c + 1) * COLS], src, ACT.Copy).then_inc(w_high, 1)

            def activate(g, k):
                scalar.wait_ge(up_ready, g * K + k + 1)
                if k >= 2 or g.least:
                    scalar.wait_ge(scaled_ready, g * K + k - 1)
                scalar.activation(hid[k % 2][:, :], up[k % 2][:, :], act, bias=b1[:, k:k + 1]).then_inc(hid_ready, 1)

            def high_half(g, k):
                scalar.wait_ge(scaled_ready, g * K + k + 1)
                if k >= NH or g.least:
                    scalar.wait_ge(down_ready, g * K + k - NH + 1)
                scalar.activation(hid_high[k % NH][:, :], scaled[k % NH][:, :], ACT.Copy).then_inc(high_ready, 1)

            def take_turned(h):
                scalar.wait_ge(turn_ready, h + 1)
                if h.least >= 2:
                    scalar.wait_ge(up_ready, (h - 1) * K)
                    scalar.wait_ge(gate_ready, h - 1)
                    scalar.wait_ge(xt_low_ready, h - 1)
                scalar.activation(xt[h.odd][:, :], turn[:, :], ACT.Copy)
                scalar.activation(xt_high[h.odd][:, :], turn[:, :], ACT.Copy).then_inc(xt_ready, 1)

            def exponentials(h):
                scalar.wait_ge(route_step, h * ROUTE_STEPS + EXP_AT)
                if full:
                    scalar.activation(all_exp[:, :, :], all_shifted[:, :, :], ACT.Exp)
                scalar.activation(pair[:, :, :], shifted[:, :, :], ACT.Exp).then_inc(exp_ready, 1)

            def take_weights(h):
                scalar.wait_ge(thirds_turned, h + 1)
                if h.least >= 2:
                    scalar.wait_ge(spread_ready, (h - 1) * E)
                    scalar.wait_ge(down_ready, (h - 2) * K + 1)
                scalar.activation(weights_t[h.odd][:, :], small[0:3 * E, :].bitcast(BF16)[:, 0:COLS],
                                ACT.Copy).then_inc(weights_ready, 1)

            def take_out(g):
                scalar.wait_ge(down_ready, (g + 1) * K)
                if g.least:
                    scalar.wait_ge(back_ready, g.n)
                scalar.activation(out_t[:, :], down[:, :], ACT.Copy).then_inc(out_ready, 1)

            def group(g, behind, ahead):
                for k in range(K):
                    activate(g, k)
                    if k == 0 and S_SPREAD >= K:
                        take_weights(g)
                    if k >= 1:
                        high_half(g, k - 1)
                    elif behind is not None:
                        high_half(behind, K - 1)
                    if k == LAG and behind is not None:
                        take_out(behind)
                    if ahead is not None:
                        if k == S_TURN:
                            take_turned(ahead)
                        if k == S_ROUTE + 2:
                            exponentials(ahead)
                        if k == S_SPREAD:
                            take_weights(ahead)

            take_turned(group_number(0))
            exponentials(group_number(0))
            if S_SPREAD < K:
                take_weights(group_number(0))
            over_groups(scalar, group)
            high_half(group_number(NG - 1), K - 1)
            take_out(group_number(NG - 1))

        @block.vector
        def _(dve):
            dve.wait_ge(raw_loaded, raw_count)
            for c in range(CHUNKS):
                dve.wait_ge(w_high, c + 1)
                cols = slice(c * COLS, (c + 1) * COLS)
                src = up[c % 2][:, :] if turned else raw[:, cols]
                dve.tensor_tensor(low[:, cols], src, high[:, cols].bitcast(F32), ALU.subtract).then_inc(w_low, 1)

            def scale(g, k):
                dve.wait_ge(hid_ready, g * K + k + 1)
                if k % HT == 0:
                    dve.wait_ge(spread_ready, g * E + k // HT + 1)
                if k >= NH or g.least:
                    dve.wait_ge(low_ready, g * K + k - NH + 1)
                dve.tensor_tensor(scaled[k % NH][:, :], hid[k % 2][:, :], spread[k // HT % 2][:, :],
                                  ALU.mult).then_inc(scaled_ready, 1)

            def low_half(g, k):
                dve.wait_ge(high_ready, g * K + k + 1)
                if k >= NH or g.least:
                    dve.wait_ge(down_ready, g * K + k - NH + 1)
                dve.tensor_tensor(hid_low[k % NH][:, :], scaled[k % NH][:, :], hid_high[k % NH][:, :].bitcast(F32),
                                  ALU.subtract).then_inc(low_ready, 1)

            def moments_of(h):
                if h.least:
                    dve.wait_ge(rstd_step, h * 2)
                for b in range(GB):
                    op = dve.bn_stats(stats[:, b, :], graph_of(x, h, b))
                op.then_inc(stats_step, 1)
                wait_apart(dve, stats_step, h * N_STATS + 1, scratch)
                for b in range(GB):
                    op = dve.bn_aggr(moments[:, b, :], stats[:, b, :])
                op.then_inc(stats_step, 1)

            def normalise(h):
                dve.wait_ge(rstd_step, h * 2 + 2)
                if h.least >= 2:
                    dve.wait_ge(turn_ready, h - 1)
                    if residual == "normed":
                        dve.wait_ge(x_plus, h - 1)
                for b in range(GB):
                    op = dve.tensor_scalar(tile_of(xn[h.odd], b), graph_of(x, h, b),
                                           moments[:, b, 0:1], rstd[:, b:b + 1], ALU.subtract, ALU.mult)
                op.then_inc(xn_ready, 1)

            def low_tokens(h):
                dve.wait_ge(xt_ready, h + 1)
                if h.least >= 2:
                    dve.wait_ge(up_ready, (h - 1) * K)
                dve.tensor_tensor(xt_low[h.odd][:, :], xt[h.odd][:, :], xt_high[h.odd][:, :].bitcast(F32),
                                  ALU.subtract).then_inc(xt_low_ready, 1)

            def over_experts(ap):
                return ap.unsqueeze(2).to_broadcast([P, GB, E])

            def route(h, part):
                at = [{0: 0, 1: 5, 2: EXP_AT, 3: ROUTE_STEPS - 7}[part]]

                def step(op):
                    op.then_inc(route_step, 1)
                    at[0] += 1
                    return h * ROUTE_STEPS + at[0]

                if part == 0:
                    dve.wait_ge(gate_ready, h + 1)
                    n = step(dve.tensor_tensor(logits[:, :, :], small[:, 0:GB * E].rearrange("p (b e) -> p b e", b=GB),
                                               gate_bias.unsqueeze(1).to_broadcast([P, GB, E]), ALU.add))
                    wait_apart(dve, route_step, n, scratch)
                    for b in range(GB):
                        step(dve.max(top[:, b, :], logits[:, b, :]))
                if part == 1:
                    wait_apart(dve, route_step, h * ROUTE_STEPS + 5, scratch)
                    for b in range(GB):
                        n = step(dve.max_index(top_at[:, b, :], top[:, b, :], logits[:, b, :]))
                    dve.wait_ge(route_step, n)
                    step(dve.tensor_copy(top_atf[:, :, :], top_at[:, :, 0:2]))
                    if h.least:
                        dve.wait_ge(exp_ready, h.n)
                    if full:
                        step(dve.tensor_tensor(all_shifted[:, :, :], logits[:, :, :],
                                               top[:, :, 0:1].to_broadcast([P, GB, E]), ALU.subtract))
                    step(dve.tensor_tensor(shifted[:, :, :], top[:, :, 0:2],
                                           top[:, :, 0:1].to_broadcast([P, GB, 2]), ALU.subtract))
                if part == 2:
                    dve.wait_ge(exp_ready, h + 1)
                    n = step(dve.reduce_sum(total[:, :], (all_exp if full else pair)[:, :, :], AX.X))
                    dve.wait_ge(route_step, n)
                    n = step(dve.reciprocal(inverse[:, :], total[:, :]))
                    dve.wait_ge(route_step, n)
                    n = step(dve.tensor_tensor(pair[:, :, :], pair[:, :, :],
                                               inverse[:, :].unsqueeze(2).to_broadcast([P, GB, 2]), ALU.mult))
                    if weighting == "renormed":
                        dve.wait_ge(route_step, n)
                        n = step(dve.reduce_sum(total[:, :], pair[:, :, :], AX.X))
                        dve.wait_ge(route_step, n)
                        n = step(dve.tensor_scalar(total[:, :], total[:, :], 1e-12, None, ALU.max))
                        dve.wait_ge(route_step, n)
                        n = step(dve.reciprocal(inverse[:, :], total[:, :]))
                        dve.wait_ge(route_step, n)
                        n = step(dve.tensor_tensor(pair[:, :, :], pair[:, :, :],
                                                   inverse[:, :].unsqueeze(2).to_broadcast([P, GB, 2]), ALU.mult))
                    step(dve.tensor_tensor(hot[:, :, :, :],
                                           chip.numbers[:, 0:E].unsqueeze(1).unsqueeze(1).to_broadcast([P, GB, 2, E]),
                                           top_atf[:, :, :].unsqueeze(3).to_broadcast([P, GB, 2, E]), ALU.is_equal))
                if part == 3:
                    dve.wait_ge(route_step, h * ROUTE_STEPS + ROUTE_STEPS - 7)
                    n = step(dve.tensor_tensor(hot[:, :, :, :], hot[:, :, :, :],
                                               pair[:, :, :].unsqueeze(3).to_broadcast([P, GB, 2, E]), ALU.mult))
                    dve.wait_ge(route_step, n)
                    n = step(dve.tensor_tensor(combine[:, :, :], hot[:, :, 0, :], hot[:, :, 1, :], ALU.add))
                    dve.wait_ge(route_step, n)
                    if h.least:
                        dve.wait_ge(thirds_turned, h.n)
                    n = step(dve.tensor_copy(thirds[:, :, 0:E], combine[:, :, :]))
                    dve.wait_ge(route_step, n)
                    n = step(dve.tensor_tensor(left[:, :, :], combine[:, :, :], thirds[:, :, 0:E], ALU.subtract))
                    dve.wait_ge(route_step, n)
                    n = step(dve.tensor_copy(thirds[:, :, E:2 * E], left[:, :, :]))
                    dve.wait_ge(route_step, n)
                    n = step(dve.tensor_tensor(left[:, :, :], left[:, :, :], thirds[:, :, E:2 * E], ALU.subtract))
                    dve.wait_ge(route_step, n)
                    step(dve.tensor_copy(thirds[:, :, 2 * E:3 * E], left[:, :, :]))
                if part in (1, 2):
                    assert at[0] == (EXP_AT if part == 1 else ROUTE_STEPS - 7), (part, at[0])

            def add_out(g):
                dve.wait_ge(back_ready, g + 1)
                if residual == "normed":
                    dve.wait_ge(x_plus, g + 1)
                if residual != "layernorm":
                    dve.tensor_tensor(group_of(x, g), group_of(x, g), back[:, :], ALU.add).then_inc(added, 1)
                    return
                if g.least:
                    dve.wait_ge(mix_out, g * 3)
                    dve.wait_ge(mix_rstd_step, g * 2)
                dve.tensor_tensor(mixed[:, :], xn[g.odd][:, :], back[:, :], ALU.add).then_inc(added, 1)
                dve.wait_ge(added, g + 1)
                for b in range(GB):
                    op = dve.bn_stats(mix_stats[:, b, :], tile_of(mixed, b))
                op.then_inc(mix_step, 1)
                wait_apart(dve, mix_step, g * 3 + 1, scratch)
                for b in range(GB):
                    op = dve.bn_aggr(mix_moments[:, b, :], mix_stats[:, b, :])
                op.then_inc(mix_step, 1)

            def finish_out(g):
                dve.wait_ge(mix_rstd_step, g * 2 + 2)
                for b in range(GB):
                    op = dve.tensor_scalar(tile_of(normed, b), tile_of(mixed, b),
                                           mix_moments[:, b, 0:1], mix_rstd[:, b:b + 1], ALU.subtract, ALU.mult)
                op.then_inc(mix_step, 1)

            def group(g, behind, ahead):
                for k in range(K):
                    scale(g, k)
                    if k >= 1:
                        low_half(g, k - 1)
                    elif behind is not None:
                        low_half(behind, K - 1)
                    if behind is not None:
                        if k == S_ADD:
                            add_out(behind)
                        if k == S_FINISH and residual == "layernorm":
                            finish_out(behind)
                    if ahead is not None:
                        if k == S_STATS:
                            moments_of(ahead)
                        if k == S_NORM:
                            normalise(ahead)
                        if k == S_LOW:
                            low_tokens(ahead)
                        if S_ROUTE <= k < S_ROUTE + 4:
                            route(ahead, k - S_ROUTE)

            dve.wait_ge(thirds_clear, 1)
            moments_of(group_number(0))
            normalise(group_number(0))
            low_tokens(group_number(0))
            for part in range(4):
                route(group_number(0), part)
            over_groups(dve, group)
            low_half(group_number(NG - 1), K - 1)
            add_out(group_number(NG - 1))
            if residual == "layernorm":
                finish_out(group_number(NG - 1))

        @block.gpsimd
        def _(pool):
            pool.memset(thirds[:, :, :], 0.0).then_inc(thirds_clear, 1)

            def inverse_deviation(step_sem, mom, var, out, h):
                pool.tensor_tensor(var[:, :], mom[:, :, 1], chip.eps[:, :], ALU.add).then_inc(step_sem, 1)
                pool.wait_ge(step_sem, h * 2 + 1)
                pool.tensor_tensor(out[:, :], var[:, :], chip.minus_half[:, :], ALU.pow).then_inc(step_sem, 1)

            def front(h):
                if h.least:
                    pool.wait_ge(xn_ready, h.n)
                pool.wait_ge(stats_step, h * N_STATS + 2)
                inverse_deviation(rstd_step, moments, var_eps, rstd, h)
                if residual == "normed":
                    pool.wait_ge(xn_ready, h + 1)
                    xg = group_of(x, h)
                    pool.tensor_tensor(xg, xg, xn[h.odd][:, :],
                                       ALU.add).then_inc(x_plus, 1)

            def outer_norm(g):
                pool.wait_ge(mix_step, g * 3 + 2)
                inverse_deviation(mix_rstd_step, mix_moments, mix_var, mix_rstd, g)
                pool.wait_ge(mix_step, g * 3 + 3)
                wide = normed[:, :].rearrange("p (b d) -> p b d", b=GB)
                pool.tensor_tensor(wide, wide, tables["gamma"].unsqueeze(1).to_broadcast([P, GB, P]),
                                   ALU.mult).then_inc(mix_out, 1)
                pool.wait_ge(mix_out, g * 3 + 1)
                pool.tensor_tensor(wide, wide, tables["beta"].unsqueeze(1).to_broadcast([P, GB, P]),
                                   ALU.add).then_inc(mix_out, 1)
                pool.wait_ge(mix_out, g * 3 + 2)
                xg = group_of(x, g)
                pool.tensor_tensor(xg, xg, normed[:, :], ALU.add).then_inc(mix_out, 1)

            def group(g, behind, ahead):
                if residual == "layernorm" and behind is not None:
                    outer_norm(behind)
                if ahead is not None:
                    front(ahead)

            front(group_number(0))
            over_groups(pool, group)
            if residual == "layernorm":
                outer_norm(group_number(NG - 1))

        block.__exit__(None, None, None)
class Chip:
    pass


def setup(nc, chip, ins, keep, x_from):
    rows_of = [("L0_b1", ins["L0_ffn_b1"].rearrange("e (t h) -> (e t) h", h=P), 32),
               ("L1_b1", ins["L1_ffn_b1"], 8),
               ("L2_b1", ins["L2_ffn_b1"].rearrange("e (t h) -> (e t) h", h=P), 32),
               ("L3_b1", ins["L3_ffn_b1"].rearrange("e (t h) -> (e t) h", h=P), 16),
               ("bih", ins["L1_gnn_bih"].rearrange("p (t h) -> (p t) h", h=P), 16),
               ("b_lin", ins["L0_gnn_b_lin"].rearrange("(a d) -> a d", a=1), 1),
               ("bg0", ins["L1_gnn_bg0"].rearrange("(a d) -> a d", a=1), 1),
               ("bhh", ins["L1_gnn_bhh"].rearrange("p (t h) -> (p t) h", h=P), 16)]
    at = {}
    n_rows = 0
    for name, _, n in rows_of:
        at[name] = n_rows
        n_rows += n
    wide_of = [("L0_b", ins["L0_gnn_b"], P), ("bg1", ins["L1_gnn_bg1"], P), ("gamma", ins["L2_ffn_gamma"], P),
               ("beta", ins["L2_ffn_beta"], P), ("L3_b", ins["L3_gnn_bias"], P), ("L0_bg", ins["L0_ffn_bg"], 8),
               ("L2_bg", ins["L2_ffn_gate_b"], 16), ("L3_bg", ins["L3_ffn_gate_b"], 8)]
    wide_at = {}
    n_wide = 0
    for name, _, n in wide_of:
        wide_at[name] = n_wide
        n_wide += n
    b2_of = [("L0", ins["L0_ffn_b2"], 8), ("L1", ins["L1_ffn_b2"], 8), ("L2", ins["L2_ffn_b2"], 16),
             ("L3", ins["L3_ffn_b2"], 8)]

    def kept(name, shape, dt=F32):
        return keep.enter_context(nc.sbuf_tensor(name, shape, dt))

    chip.ident = kept("ident", [P, P])
    chip.ident_bf = kept("ident_bf", [P, P], BF16)
    chip.numbers = kept("numbers", [P, P])
    chip.minus_half = kept("minus_half", [P, GB])
    chip.eps = kept("eps", [P, GB])
    chip.adj = kept("adj_rows", [P, P])
    chip.adj_t = kept("adj_t", [P, P])
    chip.columns = kept("columns", [P, n_rows])
    chip.gate_cols = kept("gate_cols", [P, 16 + 16 + 8])
    chip.lstm_bias = kept("lstm_bias", [P, 16])
    chip.wide = kept("wide", [P, n_wide])
    chip.zero_bias = kept("zero_bias", [P, 8])
    chip.selector = {E: kept(f"selector{E}", [3 * E, E * P], BF16) for E in (8, 16)}
    chip.b2s = {name: [kept(f"{name}_b2_{n}", [3 * E, P], BF16) for n in range(3)] for name, _, E in b2_of}

    with Phase(nc, "setup") as ph:
        rows = ph.sb("rows", [n_rows, P])
        gate_rows = ph.sb("gate_rows", [16, P])
        wide_row = ph.sb("wide_row", [1, n_wide])
        ones = ph.sb("ones", [1, P])
        b2_rows = [ph.sb(f"b2_rows{n}", [3 * E, P]) for n, (_, _, E) in enumerate(b2_of)]
        turned, gates_turned, adj_turned = ph.bank("turned"), ph.bank("gates_turned"), ph.bank("adj_turned")
        spread = [ph.bank("spread0"), ph.bank("spread1")]
        loaded = ph.sem("loaded")
        selector_zero = ph.sem("selector_zero")
        selector_step = ph.sem("selector_step")
        ident_step = ph.sem("ident_step")
        ones_set = ph.sem("ones_set")
        turn_done = ph.sem("turn_done")
        columns_ready = ph.sem("columns_ready")
        b2_step = ph.sem("b2_step")
        N_LOADS = len(rows_of) + 2 + 2 + len(wide_of) + 3 * len(b2_of) + 1

        block = nc.Block()
        block.__enter__()

        @block.sync
        def _(sp):
            for name, src, n in rows_of:
                sp.dma_start(rows[at[name]:at[name] + n, :], src).then_inc(loaded, 16)
            sp.dma_start(gate_rows[0:8, :], ins["L0_ffn_Wg"]).then_inc(loaded, 16)
            sp.dma_start(gate_rows[8:16, :], ins["L1_ffn_router_w"]).then_inc(loaded, 16)
            sp.dma_start(chip.gate_cols[:, 16:32], ins["L2_ffn_gate_w"]).then_inc(loaded, 16)
            sp.dma_start(chip.gate_cols[:, 32:40], ins["L3_ffn_gate_w"]).then_inc(loaded, 16)
            sp.dma_start(chip.adj[:, :], ins["adj"]).then_inc(loaded, 16)
            for name, src, n in wide_of:
                sp.dma_start(wide_row[:, wide_at[name]:wide_at[name] + n],
                             src.rearrange("(a d) -> a d", a=1)).then_inc(loaded, 16)
            sp.wait_ge(loaded, 16 * N_LOADS)

        @block.scalar
        def _(scalar):
            for n, (_, src, E) in enumerate(b2_of):
                for third in range(3):
                    scalar.dma_start(b2_rows[n][third * E:(third + 1) * E, :], src).then_inc(loaded, 16)
            for c in range(4):
                graphs = slice(c * NB // 4, (c + 1) * NB // 4)
                scalar.dma_start(chip.x[:, c * NB * P // 4:(c + 1) * NB * P // 4].rearrange("n (b d) -> n b d", d=P),
                                 x_from[graphs].rearrange("b n d -> n b d")).then_inc(chip.x_loaded, 16)
            scalar.wait_ge(chip.x_loaded, 64)

        @block.gpsimd
        def _(pool):
            pool.memset(chip.ident[:, :], 0.0).then_inc(selector_zero, 1)
            pool.memset(chip.ident_bf[:, :], 0.0).then_inc(selector_zero, 1)
            for E in (8, 16):
                pool.memset(chip.selector[E][:, :], 0.0).then_inc(selector_zero, 1)
            pool.wait_ge(selector_zero, 4)
            for m in (chip.ident, chip.ident_bf):
                pool.affine_select(out=m[:, :], in_=m[:, :], compare_op=ALU.not_equal, fill=1.0, base=0,
                                   pattern=[[-1, P]], channel_multiplier=1).then_inc(ident_step, 1)
            pool.iota(chip.numbers[:, :], [[1, P]], base=0, channel_multiplier=0,
                      allow_small_or_imprecise_dtypes=True).then_inc(ident_step, 1)
            pool.memset(chip.minus_half[:, :], -0.5).then_inc(ident_step, 1)
            pool.memset(chip.zero_bias[:, :], 0.0).then_inc(ident_step, 1)
            pool.memset(chip.eps[:, :], EPS).then_inc(ident_step, 1)
            pool.memset(ones[:, :], 1.0).then_inc(ones_set, 1)
            done = 0
            for E in (8, 16):
                s = chip.selector[E][:, :].rearrange("r (e p) -> r e p", p=P)
                for third in range(3):
                    pool.affine_select(out=s, in_=s, compare_op=ALU.not_equal, fill=1.0, base=-third * E,
                                       pattern=[[-1, E], [0, P]], channel_multiplier=1).then_inc(selector_step, 1)
                    done += 1
                    pool.wait_ge(selector_step, done)

        @block.tensor
        def _(pe):
            pe.wait_ge(loaded, 16 * N_LOADS)
            pe.wait_ge(ident_step, 6)
            pe.wait_ge(ones_set, 1)
            pe.transpose(turned[:, 0:n_rows], rows[:, :], chip.ident[0:n_rows, 0:n_rows]).then_inc(turn_done, 1)
            pe.transpose(gates_turned[:, 0:16], gate_rows[:, :], chip.ident[0:16, 0:16]).then_inc(turn_done, 1)
            pe.transpose(adj_turned[:, 0:P], chip.adj[:, :], chip.ident[:, :]).then_inc(turn_done, 1)
            pe.matmul(spread[0][:, :], ones[:, :], wide_row[:, 0:COLS], start=True, stop=True).then_inc(turn_done, 1)
            pe.matmul(spread[1][:, 0:n_wide - COLS], ones[:, :], wide_row[:, COLS:n_wide], start=True, stop=True)\
                .then_inc(turn_done, 1)

        @block.vector
        def _(dve):
            dve.wait_ge(turn_done, 5)
            dve.tensor_copy(chip.columns[:, :], turned[:, 0:n_rows]).then_inc(columns_ready, 1)
            dve.tensor_copy(chip.gate_cols[:, 0:16], gates_turned[:, 0:16])
            dve.tensor_copy(chip.adj_t[:, :], adj_turned[:, 0:P])
            dve.tensor_copy(chip.wide[:, 0:COLS], spread[0][:, :])
            dve.tensor_copy(chip.wide[:, COLS:n_wide], spread[1][:, 0:n_wide - COLS])
            dve.wait_ge(columns_ready, 1)
            dve.tensor_tensor(chip.lstm_bias[:, :], chip.columns[:, at["bih"]:at["bih"] + 16],
                              chip.columns[:, at["bhh"]:at["bhh"] + 16], ALU.add)
            dve.wait_ge(loaded, 16 * N_LOADS)
            step = 0
            for n, (name, _, E) in enumerate(b2_of):
                for third in range(3):
                    dve.tensor_copy(chip.b2s[name][third][:, :], b2_rows[n][:, :]).then_inc(b2_step, 1)
                    step += 1
                    dve.wait_ge(b2_step, step)
                    if third < 2:
                        dve.tensor_tensor(b2_rows[n][:, :], b2_rows[n][:, :], chip.b2s[name][third][:, :],
                                          ALU.subtract).then_inc(b2_step, 1)
                        step += 1
                        dve.wait_ge(b2_step, step)

        block.__exit__(None, None, None)

    def table(b1, n_b1, b2, E, gates, bias):
        return {"b1": chip.columns[:, at[b1]:at[b1] + n_b1], "b2s": chip.b2s[b2], "gates": chip.gate_cols[:, gates:gates + E],
                "gate_bias": chip.zero_bias[:, 0:E] if bias is None else chip.wide[:, wide_at[bias]:wide_at[bias] + E],
                "selector": chip.selector[E]}

    chip.tables = {"L0": table("L0_b1", 32, "L0", 8, 0, "L0_bg"), "L1": table("L1_b1", 8, "L1", 8, 8, None),
                   "L2": table("L2_b1", 32, "L2", 16, 16, "L2_bg"), "L3": table("L3_b1", 16, "L3", 8, 32, "L3_bg")}
    for name in ("gamma", "beta", "L0_b", "bg1", "L3_b"):
        chip.tables["L2"][name] = chip.wide[:, wide_at[name]:wide_at[name] + P]
    chip.b_lin = chip.columns[:, at["b_lin"]:at["b_lin"] + 1]
    chip.bg0 = chip.columns[:, at["bg0"]:at["bg0"] + 1]


def load_experts(engine, chip, w1, w2, turned):
    tiles = w1.shape[0] * w1.shape[2] // P if not turned else w1.shape[0] * w1.shape[1] // P
    first = chip.raw[:, 0:tiles * P].rearrange("p (e f) -> p e f", e=w1.shape[0])
    second = chip.raw[:, tiles * P:2 * tiles * P]
    if turned:
        first = chip.raw[:, 0:tiles * P].rearrange("p (r f) -> p r f", f=P)
        engine.dma_start(first, w1.rearrange("e (t h) d -> h (e t) d", h=P)).then_inc(chip.raw_loaded, 16)
        second = second.rearrange("p (e f) -> p e f", e=w2.shape[0])
        engine.dma_start(second, w2.rearrange("e d h -> d e h")).then_inc(chip.raw_loaded, 16)
    else:
        engine.dma_start(first, w1.rearrange("e d h -> d e h")).then_inc(chip.raw_loaded, 16)
        second = second.rearrange("p (r f) -> p r f", f=P)
        engine.dma_start(second, w2.rearrange("e (t h) d -> h (e t) d", h=P)).then_inc(chip.raw_loaded, 16)


EXPERTS = {"L0": ("L0_ffn_W1", "L0_ffn_W2", 8, 4, ACT.Relu, "pair", "plain", True),
           "L1": ("L1_ffn_w1", "L1_ffn_w2", 8, 1, ACT.Gelu, "renormed", "normed", False),
           "L2": ("L2_ffn_w1", "L2_ffn_w2", 16, 2, ACT.Relu, "pair", "layernorm", False),
           "L3": ("L3_ffn_W1", "L3_ffn_W2", 8, 2, ACT.Gelu, "probs", "plain", False)}


def program(nc, ins, out, layers=("G0", "L0", "G1", "L1", "G2", "L2", "G3", "L3")):
    with ExitStack() as keep:
        chip = Chip()
        chip.x = keep.enter_context(nc.sbuf_tensor("x_all", [P, NB * P], F32))
        chip.raw = keep.enter_context(nc.sbuf_tensor("raw_experts", [P, 64 * P], F32))
        chip.x_loaded = keep.enter_context(nc.semaphore("x_loaded"))
        chip.raw_loaded = keep.enter_context(nc.semaphore("raw_loaded"))
        chip.stored = keep.enter_context(nc.semaphore("stored"))
        setup(nc, chip, ins, keep, ins["x"])
        graph_layers = {"G0": attention, "G1": recurrent, "G2": edges, "G3": three_hops}
        count = 0
        for name in ("0", "1", "2", "3"):
            w1, w2, E, HT, act, weighting, residual, turned = EXPERTS["L" + name]

            def load(engine, w1=w1, w2=w2, turned=turned):
                load_experts(engine, chip, ins[w1], ins[w2], turned)

            if "G" + name in layers:
                graph_layers["G" + name](nc, chip, ins, load)
            elif "L" + name in layers:
                with nc.Block() as block:
                    @block.sync
                    def _(sp):
                        load(sp)
            if "G" + name in layers or "L" + name in layers:
                count += 32
            if "L" + name in layers:
                mixture(nc, "mix" + name, chip, chip.raw, chip.raw_loaded, count, chip.tables["L" + name],
                        E, HT, act, weighting, residual, turned)
        with nc.Block() as block:
            @block.sync
            def _(sp):
                sp.wait_ge(chip.raw_loaded, count)
                for c in range(4):
                    graphs = slice(c * NB // 4, (c + 1) * NB // 4)
                    sp.dma_start(out[graphs].rearrange("b n d -> n b d"),
                                 chip.x[:, c * NB * P // 4:(c + 1) * NB * P // 4].rearrange("n (b d) -> n b d", d=P))\
                        .then_inc(chip.stored, 16)
                sp.wait_ge(chip.stored, 64)


_INS = ['x', 'adj', 'L0_gnn_W', 'L0_gnn_b_lin', 'L0_gnn_b', 'L0_ffn_Wg', 'L0_ffn_bg', 'L0_ffn_W1', 'L0_ffn_b1',
        'L0_ffn_W2', 'L0_ffn_b2', 'L1_gnn_Wg0', 'L1_gnn_bg0', 'L1_gnn_Wg1', 'L1_gnn_bg1', 'L1_gnn_Wih',
        'L1_gnn_Whh', 'L1_gnn_bih', 'L1_gnn_bhh', 'L1_ffn_router_w', 'L1_ffn_w1', 'L1_ffn_b1', 'L1_ffn_w2',
        'L1_ffn_b2', 'L2_gnn_W_lin', 'L2_gnn_W_val', 'L2_gnn_a', 'L2_gnn_W_out', 'L2_gnn_src', 'L2_gnn_dst',
        'L2_ffn_gate_w', 'L2_ffn_gate_b', 'L2_ffn_w1', 'L2_ffn_b1', 'L2_ffn_w2', 'L2_ffn_b2', 'L2_ffn_gamma',
        'L2_ffn_beta', 'L3_gnn_W', 'L3_gnn_bias', 'L3_ffn_gate_w', 'L3_ffn_gate_b', 'L3_ffn_W1', 'L3_ffn_b1',
        'L3_ffn_W2', 'L3_ffn_b2']


def kernel(**inputs):
    import numpy as _np
    import concourse.bacc as _bacc
    from concourse import mybir as _mybir
    from concourse.bass_utils import run_bass_kernel_spmd as _run

    nc = _bacc.Bacc("TRN2", target_bir_lowering=False, num_devices=1)
    arrays, ins = {}, {}
    for name in _INS:
        a = _np.ascontiguousarray(inputs[name])
        arrays[f"in_{name}_dram"] = a
        ins[name] = nc.dram_tensor(f"in_{name}_dram", a.shape, _mybir.dt.from_np(a.dtype), kind="ExternalInput").ap()
    out = nc.dram_tensor("out_0_dram", (NB, P, P), _mybir.dt.float32, kind="ExternalOutput").ap()
    program(nc, ins, out)
    r = _run(nc, [arrays], core_ids=[0])
    return r.results[0]["out_0_dram"]
```

```python
from contextlib import ExitStack

import concourse.bass as bass
from concourse import mybir

P = 128
NB = 64
GB = 4
NG = NB // GB
COLS = GB * P
EPS = 1e-5
HALF = P // 2

ALU = mybir.AluOpType
ACT = mybir.ActivationFunctionType
AX = mybir.AxisListType
F32 = mybir.dt.float32
F32R = mybir.dt.float32r
BF16 = mybir.dt.bfloat16
U32 = mybir.dt.uint32
I32 = mybir.dt.int32


class Group:

    def __init__(self, n, odd, least):
        self.n, self.odd, self.least = n, odd, least

    def __mul__(self, k):
        return self.n * k

    def __add__(self, k):
        return self.n + k

    def __sub__(self, k):
        return self.n - k

    def next(self):
        return Group(self.n + 1, 1 - self.odd, self.least + 1)

    def last(self):
        return Group(self.n - 1, 1 - self.odd, self.least - 1)


def group_number(n):
    return Group(n, n % 2, n)


def over_groups(engine, group, count=NG):
    first, end = group_number(0), group_number(count - 1)
    group(first, None, first.next())
    with engine.Fori(0, (count - 2) // 2) as i:
        g = Group(i * 2 + 1, 1, 1)
        group(g, g.last(), g.next())
        g = g.next()
        group(g, g.last(), g.next())
    group(end, end.last(), None)


def over_groups_wide(engine, group, count=NG, head=2):
    for n in range(head):
        group(group_number(n), group_number(n - 1) if n else None, group_number(n + 1))
    with engine.Fori(0, (count - head - 2) // 2) as i:
        g = Group(i * 2 + head, 0, head)
        group(g, g.last(), g.next())
        g = g.next()
        group(g, g.last(), g.next())
    for n in (count - 2, count - 1):
        group(group_number(n), group_number(n - 1), group_number(n + 1) if n < count - 1 else None)


def wait_apart(dve, sem, value, scratch):
    dve.wait_ge(sem, value)
    dve.memset(scratch[:, 0:1], 0.0)


def tile_of(buf, b):
    return buf[:, b * P:(b + 1) * P]


def graph_of(x, g, b):
    return x[:, bass.ds((g * GB + b) * P, P)]


def group_of(x, g):
    return x[:, bass.ds(g * COLS, COLS)]


def by_graph(ap):
    return ap.rearrange("p (b d) -> p b d", b=GB)


class Phase:

    def __init__(self, nc, tag):
        self.nc, self.tag, self.sems = nc, tag, []

    def __enter__(self):
        self.ctx = ExitStack()
        return self

    def sem(self, name):
        s = self.ctx.enter_context(self.nc.semaphore(f"{self.tag}_{name}"))
        self.sems.append(s)
        return s

    def sb(self, name, shape, dt=F32):
        return self.ctx.enter_context(self.nc.sbuf_tensor(f"{self.tag}_{name}", shape, dt))

    def bank(self, name):
        return self.ctx.enter_context(self.nc.psum_tensor(f"{self.tag}_{name}", [P, COLS], F32))

    def __exit__(self, *failed):
        if failed[0] is None:
            for s in self.sems:
                self.nc.gpsimd.sem_clear(s)
            self.nc.all_engine_barrier()
        self.ctx.close()

NT = NB
UPS = 4
NH = 4


def split_experts(nc, tag, chip, keep, raw_count, K, turned):
    high, low = (keep.enter_context(nc.sbuf_tensor(f"{tag}_{name}", [P, 2 * K * P], F32R)) for name in ("high", "low"))
    CHUNKS = 2 * K // GB
    raw = chip.raw
    with Phase(nc, tag) as ph:
        turn = [ph.bank(f"turn{i}") for i in range(4)]
        w_turned = ph.sem("w_turned")
        w_high = ph.sem("w_high")
        w_low = ph.sem("w_low")
        block = nc.Block()
        block.__enter__()

        def source(c):
            return turn[c % 4][:, :] if turned else raw[:, c * COLS:(c + 1) * COLS]

        @block.tensor
        def _(pe):
            if turned:
                pe.wait_ge(chip.raw_loaded, raw_count)
                for c in range(CHUNKS):
                    if c >= 4:
                        pe.wait_ge(w_high, c - 3)
                        pe.wait_ge(w_low, c - 3)
                    for b in range(GB):
                        mm = pe.transpose(tile_of(turn[c % 4], b), tile_of(raw[:, c * COLS:(c + 1) * COLS], b),
                                          chip.ident)
                    mm.then_inc(w_turned, 1)

        @block.scalar
        def _(scalar):
            scalar.wait_ge(chip.raw_loaded, raw_count)
            for c in range(CHUNKS):
                if turned:
                    scalar.wait_ge(w_turned, c + 1)
                scalar.activation(high[:, c * COLS:(c + 1) * COLS], source(c), ACT.Copy).then_inc(w_high, 1)

        @block.vector
        def _(dve):
            for c in range(CHUNKS):
                dve.wait_ge(w_high, c + 1)
                cols = slice(c * COLS, (c + 1) * COLS)
                dve.tensor_tensor(low[:, cols], source(c), high[:, cols].bitcast(F32), ALU.subtract)\
                    .then_inc(w_low, 1)

        block.__exit__(None, None, None)
    return high, low


def mixture(nc, tag, chip, split, tables, E, HT, act, weighting, residual):
    with ExitStack() as keep:
        def kept(name, shape, dt, side=None):
            return keep.enter_context(nc.sbuf_tensor(f"{tag}_{name}", shape, dt, side=side))

        s = Chip()
        s.high, s.low = split
        s.xt_high = kept("xt_high", [P, NB * P], F32R)
        s.xt_low = kept("xt_low", [P, NB * P], F32R, "right")
        s.weights_t = kept("weights_t", [P, NB * P // 2], BF16)
        s.selector = kept("selector", [3 * E, E * P], BF16)
        s.b2s = [kept(f"b2_{n}", [3 * E, P], BF16) for n in range(3)]
        routing(nc, tag + "r", chip, s, tables, E, weighting)
        expert_products(nc, tag + "p", chip, s, tables, E, HT, act, residual)


def routing(nc, tag, chip, s, tables, E, weighting):
    full = weighting != "pair"
    with Phase(nc, tag) as ph:
        sb, bank, sem = ph.sb, ph.bank, ph.sem
        norm = Norm(ph, chip)
        xn = norm.xn
        xt = [sb(f"xt{i}", [P, COLS]) for i in range(2)]
        scratch = sb("routing", [P, NT * P // 4])
        thirds = scratch[:, :].bitcast(BF16).rearrange("p (q b h c) -> p q b h c", b=GB, h=2, c=HALF)
        scratches = [sb(f"scratch{i}", [P, 1]) for i in range(2)]
        own_logits = [sb(f"own_logits{i}", [P, GB, E]) for i in range(2)]
        own_top = [sb(f"own_top{i}", [P, GB, 8]) for i in range(2)]
        own_top_at = [sb(f"own_top_at{i}", [P, GB, 8], U32) for i in range(2)]
        logits, top, top_at, all_exp = (
            scratch[:, n * NT:(n + width) * NT].rearrange("p (t n) -> p t n", t=NT)
            for n, width in ((0, E), (E, 8), (E + 8, 8), (E + 16, E if full else 0)))
        top_at = top_at.bitcast(U32)
        hot = s.weights_t[:, 0:NT * 4 * E].bitcast(F32).rearrange("p (t k e) -> p t k e", k=2, e=E)
        top_atf = sb("top_atf", [P, NT, 2])
        pair = sb("pair", [P, NT, 2])
        b2_left = sb("b2_left", [3 * E, P])
        total = sb("total", [P, NT])
        inverse = sb("inverse", [P, NT])
        turn = [bank(f"turn{i}") for i in range(2)]
        small = [bank(f"small{i}") for i in range(2)]
        turn_ready = sem("turn_ready")
        xt_ready = sem("xt_ready")
        xt_low_ready = sem("xt_low_ready")
        gate_ready = sem("gate_ready")
        logits_ready = sem("logits_ready")
        top_ready = sem("top_ready")
        top_at_ready = sem("top_at_ready")
        routes_kept = sem("routes_kept")
        step = sem("step")
        selector_step = sem("selector_step")
        b2_step = sem("b2_step")
        exp_ready = sem("exp_ready")
        thirds_turned = sem("thirds_turned")
        weights_ready = sem("weights_ready")
        block = nc.Block()
        block.__enter__()
        N_SHIFT = 2 + full
        N_ALL = N_SHIFT + (17 if weighting != "renormed" else 21)

        @block.tensor
        def _(pe):
            def turn_tokens(g):
                pe.wait_ge(norm.xn_ready, g + 1)
                if g.least >= 2:
                    pe.wait_ge(xt_ready, g - 1)
                for b in range(GB):
                    mm = pe.transpose(tile_of(turn[g.odd], b), tile_of(xn[g.odd], b), chip.ident)
                mm.then_inc(turn_ready, 1)

            def gate_products(g):
                pe.wait_ge(xt_ready, g + 1)
                if g.least >= 2:
                    pe.wait_ge(logits_ready, g - 1)
                for b in range(GB):
                    mm = pe.matmul(small[g.odd][:, b * E:(b + 1) * E], tile_of(xt[g.odd], b), tables["gates"],
                                   start=True, stop=True)
                mm.then_inc(gate_ready, 1)

            def group(g, behind, ahead):
                turn_tokens(g)
                if behind is not None:
                    gate_products(behind)

            over_groups_wide(pe, group, head=4)
            gate_products(group_number(NG - 1))
            pe.wait_ge(step, N_ALL)

            def turn_weights(q, behind, ahead):
                if q.least >= 2:
                    pe.wait_ge(weights_ready, q - 1)
                for b in range(GB):
                    mm = pe.transpose(tile_of(small[q.odd][:, :].bitcast(BF16), b),
                                      scratch[:, :].bitcast(BF16)[:, bass.ds((q * GB + b) * P, P)], chip.ident_bf[:, :])
                mm.then_inc(thirds_turned, 1)

            over_groups_wide(pe, turn_weights, NG // 2)

        @block.scalar
        def _(scalar):
            def group(g, behind, ahead):
                scalar.wait_ge(turn_ready, g + 1)
                if g.least >= 2:
                    scalar.wait_ge(gate_ready, g - 1)
                    scalar.wait_ge(xt_low_ready, g - 1)
                scalar.activation(xt[g.odd][:, :], turn[g.odd][:, :], ACT.Copy)
                scalar.activation(group_of(s.xt_high, g), turn[g.odd][:, :], ACT.Copy).then_inc(xt_ready, 1)

            over_groups_wide(scalar, group, head=4)
            scalar.wait_ge(step, N_SHIFT)
            if full:
                scalar.activation(all_exp[:, :, :], logits[:, :, :], ACT.Exp)
            scalar.activation(pair[:, :, :], pair[:, :, :], ACT.Exp).then_inc(exp_ready, 1)

            def take_weights(q, behind, ahead):
                scalar.wait_ge(thirds_turned, q + 1)
                scalar.activation(group_of(s.weights_t, q), small[q.odd][:, :].bitcast(BF16)[:, 0:COLS],
                                  ACT.Copy).then_inc(weights_ready, 1)

            over_groups_wide(scalar, take_weights, NG // 2)

        @block.vector
        def _(dve):
            norm.moments(dve, group_number(0))
            b2, rest = tables["b2"], b2_left[:, :]
            dve.tensor_copy(rest, b2).then_inc(b2_step, 1)
            dve.wait_ge(b2_step, 1)
            for n in range(3):
                dve.tensor_copy(s.b2s[n][:, :], rest).then_inc(b2_step, 1)
                dve.wait_ge(b2_step, 2 * n + 2)
                if n < 2:
                    dve.tensor_tensor(rest, rest, s.b2s[n][:, :], ALU.subtract).then_inc(b2_step, 1)
                    dve.wait_ge(b2_step, 2 * n + 3)

            def take_logits(g):
                dve.wait_ge(gate_ready, g + 1)
                if g.least >= 2:
                    dve.wait_ge(routes_kept, (g - 1) * 3)
                dve.tensor_tensor(own_logits[g.odd][:, :, :], small[g.odd][:, 0:GB * E].rearrange("p (b e) -> p b e", b=GB),
                                  tables["gate_bias"].unsqueeze(1).to_broadcast([P, GB, E]), ALU.add)\
                    .then_inc(logits_ready, 1)

            def largest(g):
                wait_apart(dve, logits_ready, g + 1, scratches[0])
                for b in range(GB):
                    op = dve.max(own_top[g.odd][:, b, :], own_logits[g.odd][:, b, :])
                op.then_inc(top_ready, 1)

            def experts_of(g):
                wait_apart(dve, top_ready, g + 1, scratches[1])
                for b in range(GB):
                    op = dve.max_index(own_top_at[g.odd][:, b, :], own_top[g.odd][:, b, :], own_logits[g.odd][:, b, :])
                op.then_inc(top_at_ready, 1)

            def group(g, behind, ahead):
                if g.least >= 2:
                    dve.wait_ge(turn_ready, g - 1)
                norm.normalise(dve, g)
                if ahead is not None:
                    norm.moments(dve, ahead)
                if behind is not None:
                    if behind.least:
                        experts_of(behind.last())
                    take_logits(behind)
                    largest(behind)

            over_groups_wide(dve, group, head=4)
            end = group_number(NG - 1)
            experts_of(end.last())
            take_logits(end)
            largest(end)
            experts_of(end)

            def over_pair(ap):
                return ap.unsqueeze(2).to_broadcast([P, NT, 2])

            done = [0]

            def link(op):
                op.then_inc(step, 1)
                done[0] += 1
                dve.wait_ge(step, done[0])

            dve.wait_ge(routes_kept, 3 * NG)
            link(dve.tensor_copy(top_atf[:, :, :], top_at[:, :, 0:2]))
            if full:
                link(dve.tensor_tensor(logits[:, :, :], logits[:, :, :], top[:, :, 0:1].to_broadcast([P, NT, E]),
                                       ALU.subtract))
            link(dve.tensor_tensor(pair[:, :, :], top[:, :, 0:2], top[:, :, 0:1].to_broadcast([P, NT, 2]),
                                   ALU.subtract))
            assert done[0] == N_SHIFT
            link(dve.tensor_tensor(hot[:, :, :, :],
                                   chip.numbers[:, 0:E].unsqueeze(1).unsqueeze(1).to_broadcast([P, NT, 2, E]),
                                   top_atf[:, :, :].unsqueeze(3).to_broadcast([P, NT, 2, E]), ALU.is_equal))
            dve.wait_ge(exp_ready, 1)
            link(dve.reduce_sum(total[:, :], (all_exp if full else pair)[:, :, :], AX.X))
            link(dve.reciprocal(inverse[:, :], total[:, :]))
            link(dve.tensor_tensor(pair[:, :, :], pair[:, :, :], over_pair(inverse[:, :]), ALU.mult))
            if weighting == "renormed":
                link(dve.reduce_sum(total[:, :], pair[:, :, :], AX.X))
                link(dve.tensor_scalar(total[:, :], total[:, :], 1e-12, None, ALU.max))
                link(dve.reciprocal(inverse[:, :], total[:, :]))
                link(dve.tensor_tensor(pair[:, :, :], pair[:, :, :], over_pair(inverse[:, :]), ALU.mult))
            link(dve.tensor_tensor(hot[:, :, :, :], hot[:, :, :, :],
                                   pair[:, :, :].unsqueeze(3).to_broadcast([P, NT, 2, E]), ALU.mult))
            left = hot[:, :, 0, :]
            link(dve.tensor_tensor(left, left, hot[:, :, 1, :], ALU.add))
            link(dve.memset(scratch[:, :], 0.0))
            for half in range(2):
                rest = left.rearrange("p (q h b) e -> p q h b e", h=2, b=GB)[:, :, half, :, :]
                for n in range(3):
                    part = thirds[:, :, :, half, n * E:(n + 1) * E]
                    link(dve.tensor_copy(part, rest))
                    if n < 2:
                        link(dve.tensor_tensor(rest, rest, part, ALU.subtract))
            assert done[0] == N_ALL, (done[0], N_ALL)

        @block.gpsimd
        def _(pool):
            norm.deviation(pool, group_number(0))
            pool.memset(s.selector[:, :], 0.0).then_inc(selector_step, 1)
            rows = s.selector[:, :].rearrange("r (e p) -> r e p", p=P)
            for third in range(3):
                pool.wait_ge(selector_step, third + 1)
                pool.affine_select(out=rows, in_=rows, compare_op=ALU.not_equal, fill=1.0, base=-third * E,
                                   pattern=[[-1, E], [0, P]], channel_multiplier=1).then_inc(selector_step, 1)

            def low_tokens(g):
                pool.wait_ge(xt_ready, g + 1)
                pool.tensor_tensor(group_of(s.xt_low, g), xt[g.odd][:, :], group_of(s.xt_high, g).bitcast(F32),
                                   ALU.subtract).then_inc(xt_low_ready, 1)

            def keep_routes(g):
                pool.wait_ge(top_at_ready, g + 1)
                tiles = bass.ds(g * GB, GB)
                pool.tensor_copy(logits[:, tiles, :], own_logits[g.odd][:, :, :]).then_inc(routes_kept, 1)
                pool.tensor_copy(top[:, tiles, :], own_top[g.odd][:, :, :]).then_inc(routes_kept, 1)
                pool.tensor_copy(top_at[:, tiles, :], own_top_at[g.odd][:, :, :]).then_inc(routes_kept, 1)

            def group(g, behind, ahead):
                if ahead is not None:
                    norm.deviation(pool, ahead)
                if behind is not None:
                    if behind.least:
                        keep_routes(behind.last())
                    low_tokens(behind)

            over_groups_wide(pool, group, head=4)
            low_tokens(group_number(NG - 1))
            keep_routes(group_number(NG - 2))
            keep_routes(group_number(NG - 1))

        block.__exit__(None, None, None)


def expert_products(nc, tag, chip, s, tables, E, HT, act, residual):
    K = E * HT
    SCALE, HALVES, DOWN = 1, 2, 4
    S_OUT, S_BACK, S_ADD, S_FINISH = DOWN, DOWN + 1, DOWN + 2, DOWN + 4
    POOLED = (3,)
    NS = 2
    b1, b2s, selector = tables["b1"], s.b2s, s.selector
    layernorm = residual == "layernorm"
    x = chip.x

    def lows(k, pooled):
        mine = [i for i in range(NH) if (i in POOLED) == pooled]
        return k // NH * len(mine) + sum(i < k % NH for i in mine)

    with Phase(nc, tag) as ph:
        sb, bank, sem = ph.sb, ph.bank, ph.sem
        hid = [sb(f"hid{i}", [P, COLS]) for i in range(NS)]
        scaled = [sb(f"scaled{i}", [P, COLS]) for i in range(NS)]
        hid_high = [sb(f"hid_high{i}", [P, COLS], F32R) for i in range(NH)]
        hid_low = [sb(f"hid_low{i}", [P, COLS], F32R) for i in range(NH)]
        out_t = sb("out_t", [P, COLS])
        own_weights = [sb(f"own_weights{i}", [3 * E, COLS], BF16) for i in range(2)]
        if layernorm:
            normed = out_t
            scratch = sb("scratch", [P, 1])
            mix_stats = sb("mix_stats", [P, GB, 6])
            mix_moments = sb("mix_moments", [P, GB, 2])
            mix_var = sb("mix_var", [P, GB])
            mix_rstd = sb("mix_rstd", [P, GB])
        up = [bank(f"up{i}") for i in range(UPS)]
        spread = [bank(f"spread{i}") for i in range(2)]
        down = [bank(f"down{i}") for i in range(2)]

        weights_ready = sem("weights_ready")
        up_ready = sem("up_ready")
        hid_ready = sem("hid_ready")
        scaled_ready = sem("scaled_ready")
        high_ready = sem("high_ready")
        low_ready = {False: sem("low_ready"), True: sem("low_ready_pool")}
        down_ready = sem("down_ready")
        spread_ready = sem("spread_ready")
        out_ready = sem("out_ready")
        back_ready = sem("back_ready")
        added = sem("added")
        if layernorm:
            mix_step = sem("mix_step")
            mix_rstd_step = sem("mix_rstd_step")
            mix_out = sem("mix_out")

        def is_pooled(k):
            return k % NH in POOLED

        def wait_low(engine, g, k):
            p = is_pooled(k)
            engine.wait_ge(low_ready[p], g * lows(K, p) + (lows(k, p) + 1))

        def tiles(engine, stages, extra):
            def group(g, behind, ahead):
                for k in range(K):
                    for stage, lag in stages:
                        if k >= lag:
                            stage(g, k - lag)
                        elif behind is not None:
                            stage(behind, K + k - lag)
                    if behind is not None:
                        extra(behind, k)

            over_groups_wide(engine, group)
            end = group_number(NG - 1)
            for k in range(K):
                for stage, lag in stages:
                    if k < lag:
                        stage(end, K + k - lag)
                extra(end, k)

        block = nc.Block()
        block.__enter__()

        @block.tensor
        def _(pe):
            def first_product(g, k):
                if k >= UPS or g.least:
                    pe.wait_ge(hid_ready, g * K + (k - UPS + 1))
                w = slice(k * P, (k + 1) * P)
                bank = up[k % UPS][:, :]
                pe.matmul(bank, s.high[:, w], group_of(s.xt_high, g), start=True, stop=False)
                pe.matmul(bank, s.high[:, w], group_of(s.xt_low, g), start=False, stop=False)
                pe.matmul(bank, s.low[:, w], group_of(s.xt_high, g), start=False, stop=True).then_inc(up_ready, 1)
                if k == 0:
                    pe.wait_ge(weights_ready, g + 1)
                if k % HT == 0:
                    e = k // HT
                    if e >= 2 or g.least:
                        pe.wait_ge(scaled_ready, (g * E + (e - 1)) * HT)
                    pe.matmul(spread[e % 2][:, :], selector[:, e * P:(e + 1) * P], own_weights[g.odd][:, :],
                              start=True, stop=True).then_inc(spread_ready, 1)

            def second_product(g, k):
                bank = down[g.odd][:, :]
                if k == 0:
                    if g.least >= 2:
                        pe.wait_ge(added, g - 1)
                    for n in range(3):
                        pe.matmul(bank, b2s[n][:, :], own_weights[g.odd][:, :], start=(n == 0), stop=False)
                    if residual != "plain":
                        pe.matmul(bank, chip.ident_r, group_of(s.xt_high, g), start=False, stop=False)
                        pe.matmul(bank, chip.ident_r, group_of(s.xt_low, g), start=False, stop=False)
                wait_low(pe, g, k)
                w = slice((K + k) * P, (K + k + 1) * P)
                n = k % NH
                pe.matmul(bank, s.high[:, w], hid_high[n][:, :], start=False, stop=False)
                pe.matmul(bank, s.high[:, w], hid_low[n][:, :], start=False, stop=False)
                pe.matmul(bank, s.low[:, w], hid_high[n][:, :], start=False, stop=(k == K - 1))\
                    .then_inc(down_ready, 1)

            def turn_back(g, k):
                if k == S_BACK:
                    pe.wait_ge(out_ready, g + 1)
                    for b in range(GB):
                        mm = pe.transpose(tile_of(down[g.odd], b), tile_of(out_t, b), chip.ident)
                    mm.then_inc(back_ready, 1)

            tiles(pe, ((first_product, 0), (second_product, DOWN)), turn_back)

        @block.scalar
        def _(scalar):
            def high_half(g, k):
                scalar.wait_ge(scaled_ready, g * K + (k + 1))
                if k >= NH or g.least:
                    scalar.wait_ge(down_ready, g * K + (k - NH + 1))
                scalar.activation(hid_high[k % NH][:, :], scaled[k % NS][:, :], ACT.Copy)\
                    .then_inc(high_ready, 1)

            def activate(g, k):
                scalar.wait_ge(up_ready, g * K + (k + 1))
                if k >= NS or g.least:
                    scalar.wait_ge(scaled_ready, g * K + (k - NS + 1))
                scalar.activation(hid[k % NS][:, :], up[k % UPS][:, :], act, bias=b1[:, k:k + 1])\
                    .then_inc(hid_ready, 1)

            def weights_for(g):
                if g.least >= 2:
                    scalar.wait_ge(spread_ready, (g - 1) * E)
                    scalar.wait_ge(down_ready, (g - 2) * K + 1)
                first = HALF * g.odd
                scalar.activation(own_weights[g.odd][:, :],
                                 s.weights_t[first:first + 3 * E, bass.ds((g - g.odd) * (COLS // 2), COLS)], ACT.Copy)\
                    .then_inc(weights_ready, 1)

            def take_out(g, k):
                if k == S_BACK and g.least < NG - 2:
                    weights_for(g.next().next())
                if k == S_OUT:
                    scalar.wait_ge(down_ready, g * K + K)
                    if g.least:
                        scalar.wait_ge(back_ready, g.n)
                        if layernorm:
                            scalar.wait_ge(mix_out, g * 3)
                    scalar.activation(out_t[:, :], down[g.odd][:, :], ACT.Copy).then_inc(out_ready, 1)

            weights_for(group_number(0))
            weights_for(group_number(1))
            tiles(scalar, ((high_half, HALVES), (activate, 0)), take_out)

        @block.vector
        def _(dve):
            def scale(g, k):
                dve.wait_ge(hid_ready, g * K + (k + 1))
                if k % HT == 0:
                    dve.wait_ge(spread_ready, g * E + (k // HT + 1))
                if k >= NS or g.least:
                    wait_low(dve, g, k - NS)
                weight = spread[k // HT % 2][:, :]
                dve.tensor_tensor(scaled[k % NS][:, :], hid[k % NS][:, :], weight, ALU.mult).then_inc(scaled_ready, 1)

            def low_half(g, k):
                if is_pooled(k):
                    return
                dve.wait_ge(high_ready, g * K + (k + 1))
                if k >= NH or g.least:
                    dve.wait_ge(down_ready, g * K + (k - NH + 1))
                high = hid_high[k % NH][:, :].bitcast(F32)
                dve.tensor_tensor(hid_low[k % NH][:, :], scaled[k % NS][:, :], high, ALU.subtract)\
                    .then_inc(low_ready[False], 1)

            def add_out(g, k):
                if k == S_ADD and not layernorm:
                    dve.wait_ge(back_ready, g + 1)
                    dve.tensor_tensor(group_of(x, g), group_of(x, g), down[g.odd][:, :], ALU.add).then_inc(added, 1)
                if k == S_ADD and layernorm:
                    if g.least:
                        dve.wait_ge(mix_rstd_step, g * 2)
                    wait_apart(dve, back_ready, g + 1, scratch)
                    for b in range(GB):
                        op = dve.bn_stats(mix_stats[:, b, :], tile_of(down[g.odd], b))
                    op.then_inc(mix_step, 1)
                    wait_apart(dve, mix_step, g * 2 + 1, scratch)
                    for b in range(GB):
                        op = dve.bn_aggr(mix_moments[:, b, :], mix_stats[:, b, :])
                    op.then_inc(mix_step, 1)
                if k == S_FINISH and layernorm:
                    dve.wait_ge(mix_rstd_step, g * 2 + 2)
                    for b in range(GB):
                        op = dve.tensor_scalar(tile_of(normed, b), tile_of(down[g.odd], b),
                                               mix_moments[:, b, 0:1], mix_rstd[:, b:b + 1], ALU.subtract, ALU.mult)
                    op.then_inc(added, 1)

            tiles(dve, ((scale, SCALE), (low_half, HALVES)), add_out)

        @block.gpsimd
        def _(pool):
            def low_half(g, k):
                if not is_pooled(k):
                    return
                pool.wait_ge(high_ready, g * K + (k + 1))
                if k >= NH or g.least:
                    pool.wait_ge(down_ready, g * K + (k - NH + 1))
                pool.tensor_tensor(hid_low[k % NH][:, :], scaled[k % NS][:, :], hid_high[k % NH][:, :].bitcast(F32),
                                   ALU.subtract).then_inc(low_ready[True], 1)

            def outer_norm(g, k):
                if not layernorm:
                    return
                wide = by_graph(normed[:, :])
                if k == S_ADD:
                    if g.least:
                        pool.wait_ge(added, g.n)
                    pool.wait_ge(mix_step, g * 2 + 2)
                    pool.tensor_tensor(mix_var[:, :], mix_moments[:, :, 1], chip.eps[:, :], ALU.add)\
                        .then_inc(mix_rstd_step, 1)
                    pool.wait_ge(mix_rstd_step, g * 2 + 1)
                    pool.tensor_tensor(mix_rstd[:, :], mix_var[:, :], chip.minus_half[:, :], ALU.pow)\
                        .then_inc(mix_rstd_step, 1)
                if k == S_FINISH:
                    pool.wait_ge(added, g + 1)
                    pool.tensor_tensor(wide, wide, tables["gamma"].unsqueeze(1).to_broadcast([P, GB, P]),
                                       ALU.mult).then_inc(mix_out, 1)
                if k == S_FINISH + 4:
                    pool.wait_ge(mix_out, g * 3 + 1)
                    pool.tensor_tensor(wide, wide, tables["beta"].unsqueeze(1).to_broadcast([P, GB, P]),
                                       ALU.add).then_inc(mix_out, 1)
                if k == S_FINISH + 8:
                    pool.wait_ge(mix_out, g * 3 + 2)
                    xg = group_of(x, g)
                    pool.tensor_tensor(xg, xg, normed[:, :], ALU.add).then_inc(mix_out, 1)

            tiles(pool, ((low_half, HALVES),), outer_norm)

        block.__exit__(None, None, None)
class Norm:

    def __init__(self, ph, chip):
        self.x, self.minus_half, self.eps = chip.x, chip.minus_half, chip.eps
        self.scratch = ph.sb("scratch", [P, 1])
        self.stats, self.means, self.var_eps, self.rstd, self.xn = (
            [ph.sb(f"{name}{i}", shape) for i in range(2)] for name, shape in (
                ("stats", [P, GB, 6]), ("means", [P, GB, 2]), ("var_eps", [P, GB]), ("rstd", [P, GB]),
                ("xn", [P, COLS])))
        self.stats_step = ph.sem("stats_step")
        self.rstd_step = ph.sem("rstd_step")
        self.xn_ready = ph.sem("xn_ready")

    def moments(self, dve, h):
        stats, means = self.stats[h.odd], self.means[h.odd]
        if h.least >= 2:
            dve.wait_ge(self.xn_ready, h - 1)
        for b in range(GB):
            op = dve.bn_stats(stats[:, b, :], graph_of(self.x, h, b))
        op.then_inc(self.stats_step, 1)
        wait_apart(dve, self.stats_step, h * 2 + 1, self.scratch)
        for b in range(GB):
            op = dve.bn_aggr(means[:, b, :], stats[:, b, :])
        op.then_inc(self.stats_step, 1)

    def deviation(self, pool, h):
        if h.least >= 2:
            pool.wait_ge(self.xn_ready, h - 1)
        pool.wait_ge(self.stats_step, h * 2 + 2)
        var_eps, rstd = self.var_eps[h.odd], self.rstd[h.odd]
        pool.tensor_tensor(var_eps[:, :], self.means[h.odd][:, :, 1], self.eps[:, :], ALU.add)\
            .then_inc(self.rstd_step, 1)
        pool.wait_ge(self.rstd_step, h * 2 + 1)
        pool.tensor_tensor(rstd[:, :], var_eps[:, :], self.minus_half[:, :], ALU.pow)\
            .then_inc(self.rstd_step, 1)

    def normalise(self, dve, h):
        dve.wait_ge(self.rstd_step, h * 2 + 2)
        for b in range(GB):
            op = dve.tensor_scalar(tile_of(self.xn[h.odd], b), graph_of(self.x, h, b), self.means[h.odd][:, b, 0:1],
                                   self.rstd[h.odd][:, b:b + 1], ALU.subtract, ALU.mult)
        op.then_inc(self.xn_ready, 1)


NEVER = -1e16


def attention(nc, chip, ins, load_next):
    with Phase(nc, "att") as ph:
        norm = Norm(ph, chip)
        x, xn = chip.x, norm.xn
        weight = ph.sb("weight", [P, P])
        xt = ph.sb("xt", [P, COLS])
        ht = [ph.sb(f"ht{i}", [P, COLS]) for i in range(2)]
        hn = [ph.sb(f"hn{i}", [P, COLS]) for i in range(2)]
        product = ph.sb("product", [P, COLS])
        barred = ph.sb("barred", [P, COLS])
        score = [ph.sb(f"score{i}", [P, COLS]) for i in range(2)]
        minus_max = [ph.sb(f"minus_max{i}", [P, GB]) for i in range(2)]
        prob = ph.sb("prob", [P, COLS])
        total = ph.sb("total", [P, GB])
        inverse = ph.sb("inverse", [P, GB])
        prob_t = ph.sb("prob_t", [P, COLS])
        turn, project, turn_h, scores, turn_p, mix = (ph.bank(n) for n in
                                                      ("turn", "project", "turn_h", "scores", "turn_p", "mix"))
        loaded = ph.sem("loaded")
        turn_ready = ph.sem("turn_ready")
        xt_ready = ph.sem("xt_ready")
        project_ready = ph.sem("project_ready")
        ht_ready = ph.sem("ht_ready")
        turn_h_ready = ph.sem("turn_h_ready")
        hn_ready = ph.sem("hn_ready")
        scores_ready = ph.sem("scores_ready")
        mask_step = ph.sem("mask_step")
        prob_ready = ph.sem("prob_ready")
        turn_p_ready = ph.sem("turn_p_ready")
        prob_t_ready = ph.sem("prob_t_ready")
        mix_ready = ph.sem("mix_ready")
        inverse_ready = ph.sem("inverse_ready")
        added = ph.sem("added")
        bias_added = ph.sem("bias_added")
        block = nc.Block()
        block.__enter__()

        @block.sync
        def _(sp):
            sp.dma_start(weight[:, :], ins["L0_gnn_W"]).then_inc(loaded, 16)
            load_next(sp)

        @block.tensor
        def _(pe):
            def turn_tokens(h):
                pe.wait_ge(norm.xn_ready, h + 1)
                if h.least:
                    pe.wait_ge(xt_ready, h.n)
                for b in range(GB):
                    mm = pe.transpose(tile_of(turn, b), tile_of(xn[h.odd], b), chip.ident)
                mm.then_inc(turn_ready, 1)

            def projection(h):
                pe.wait_ge(xt_ready, h + 1)
                if h.least:
                    pe.wait_ge(ht_ready, h.n)
                pe.matmul(project[:, :], weight[:, :], xt[:, :], start=True, stop=True).then_inc(project_ready, 1)

            def h_and_scores(h):
                pe.wait_ge(ht_ready, h + 1)
                if h.least:
                    pe.wait_ge(hn_ready, h.n)
                for b in range(GB):
                    mm = pe.transpose(tile_of(turn_h, b), tile_of(ht[h.odd], b), chip.ident)
                mm.then_inc(turn_h_ready, 1)
                if h.least:
                    pe.wait_ge(mask_step, h * 4 - 3)
                for b in range(GB):
                    hb = tile_of(ht[h.odd], b)
                    mm = pe.matmul(tile_of(scores, b), hb, hb, start=True, stop=True)
                mm.then_inc(scores_ready, 1)

            def turn_probs(g):
                pe.wait_ge(prob_ready, g + 1)
                if g.least:
                    pe.wait_ge(prob_t_ready, g.n)
                for b in range(GB):
                    mm = pe.transpose(tile_of(turn_p, b), tile_of(prob, b), chip.ident)
                mm.then_inc(turn_p_ready, 1)

            def mixture_of_h(g):
                pe.wait_ge(prob_t_ready, g + 1)
                pe.wait_ge(hn_ready, g + 1)
                if g.least:
                    pe.wait_ge(added, g.n)
                for b in range(GB):
                    mm = pe.matmul(tile_of(mix, b), tile_of(prob_t, b), tile_of(hn[g.odd], b), start=True, stop=True)
                mm.then_inc(mix_ready, 1)

            def group(g, behind, ahead):
                if ahead is not None:
                    turn_tokens(ahead)
                    projection(ahead)
                turn_probs(g)
                if ahead is not None:
                    h_and_scores(ahead)
                mixture_of_h(g)

            pe.wait_ge(loaded, 16)
            turn_tokens(group_number(0))
            projection(group_number(0))
            h_and_scores(group_number(0))
            over_groups(pe, group)

        @block.scalar
        def _(scalar):
            def take_turned(h):
                scalar.wait_ge(turn_ready, h + 1)
                if h.least:
                    scalar.wait_ge(project_ready, h.n)
                scalar.activation(xt[:, :], turn[:, :], ACT.Copy).then_inc(xt_ready, 1)

            def take_h(h):
                scalar.wait_ge(project_ready, h + 1)
                if h.least >= 2:
                    scalar.wait_ge(scores_ready, h - 1)
                scalar.activation(ht[h.odd][:, :], project[:, :], ACT.Identity, bias=chip.b_lin).then_inc(ht_ready, 1)

            def take_turned_h(h):
                scalar.wait_ge(turn_h_ready, h + 1)
                if h.least >= 2:
                    scalar.wait_ge(mix_ready, h - 1)
                scalar.activation(hn[h.odd][:, :], turn_h[:, :], ACT.Copy).then_inc(hn_ready, 1)

            def exponentials(g):
                scalar.wait_ge(mask_step, g * 4 + 4)
                if g.least:
                    scalar.wait_ge(turn_p_ready, g.n)
                    scalar.wait_ge(inverse_ready, g.n)
                for b in range(GB):
                    op = scalar.activation(tile_of(prob, b), tile_of(score[g.odd], b), ACT.Exp,
                                           bias=minus_max[g.odd][:, b:b + 1], accum_out=total[:, b:b + 1])
                op.then_inc(prob_ready, 1)

            def take_probs(g):
                scalar.wait_ge(turn_p_ready, g + 1)
                if g.least:
                    scalar.wait_ge(mix_ready, g.n)
                scalar.activation(prob_t[:, :], turn_p[:, :], ACT.Copy).then_inc(prob_t_ready, 1)

            def group(g, behind, ahead):
                exponentials(g)
                if ahead is not None:
                    take_turned(ahead)
                    take_h(ahead)
                take_probs(g)
                if ahead is not None:
                    take_turned_h(ahead)

            take_turned(group_number(0))
            take_h(group_number(0))
            take_turned_h(group_number(0))
            over_groups(scalar, group)

        @block.vector
        def _(dve):
            every_graph = chip.adj[:, :].unsqueeze(1).to_broadcast([P, GB, P])

            def mask(h):
                dve.wait_ge(scores_ready, h + 1)
                if h.least:
                    dve.wait_ge(mask_step, h * 4)
                dve.tensor_tensor(by_graph(product[:, :]), by_graph(scores[:, :]), every_graph, ALU.mult)\
                    .then_inc(mask_step, 1)
                dve.wait_ge(mask_step, h * 4 + 1)
                dve.tensor_scalar(barred[:, :], product[:, :], 0.0, NEVER, ALU.is_equal, ALU.mult)\
                    .then_inc(mask_step, 1)
                dve.wait_ge(mask_step, h * 4 + 2)
                if h.least >= 2:
                    dve.wait_ge(prob_ready, h - 1)
                dve.tensor_tensor(score[h.odd][:, :], product[:, :], barred[:, :], ALU.add).then_inc(mask_step, 1)
                dve.wait_ge(mask_step, h * 4 + 3)
                dve.tensor_reduce(minus_max[h.odd][:, :], by_graph(score[h.odd][:, :]), AX.X, ALU.max, negate=True)\
                    .then_inc(mask_step, 1)

            def add(g):
                dve.wait_ge(prob_ready, g + 1)
                if g.least:
                    dve.wait_ge(added, g.n)
                dve.reciprocal(inverse[:, :], total[:, :]).then_inc(inverse_ready, 1)
                dve.wait_ge(inverse_ready, g + 1)
                dve.wait_ge(mix_ready, g + 1)
                dve.wait_ge(bias_added, g + 1)
                for b in range(GB):
                    xb = graph_of(x, g, b)
                    op = dve.scalar_tensor_tensor(out=xb, in0=tile_of(mix, b), scalar=inverse[:, b:b + 1], in1=xb,
                                                  op0=ALU.mult, op1=ALU.add)
                op.then_inc(added, 1)

            def front(h):
                norm.moments(dve, h)
                if h.least >= 2:
                    dve.wait_ge(turn_ready, h - 1)
                norm.normalise(dve, h)

            def group(g, behind, ahead):
                if ahead is not None:
                    front(ahead)
                add(g)
                if ahead is not None:
                    mask(ahead)

            front(group_number(0))
            mask(group_number(0))
            over_groups(dve, group)

        @block.gpsimd
        def _(pool):
            def bias(g):
                pool.wait_ge(norm.xn_ready, g + 1)
                pool.tensor_tensor(by_graph(group_of(x, g)), by_graph(group_of(x, g)),
                                   chip.tables["L2"]["L0_b"].unsqueeze(1).to_broadcast([P, GB, P]), ALU.add)\
                    .then_inc(bias_added, 1)

            def group(g, behind, ahead):
                if ahead is not None:
                    norm.deviation(pool, ahead)
                bias(g)

            norm.deviation(pool, group_number(0))
            over_groups(pool, group)

        block.__exit__(None, None, None)


def three_hops(nc, chip, ins, load_next):
    with Phase(nc, "hops") as ph:
        norm = Norm(ph, chip)
        x, xn = chip.x, norm.xn
        weight = ph.sb("weight", [P, 3 * P])
        parts = ph.sb("parts", [P, 3 * P])
        near = [ph.sb(f"near{b}", [P, 3 * P]) for b in range(GB)]
        gather = [ph.bank(f"gather{b}") for b in range(GB)]
        out = [ph.bank(f"out{i}") for i in range(2)]
        loaded = ph.sem("loaded")
        parts_step = ph.sem("parts_step")
        gather_ready = ph.sem("gather_ready")
        near_ready = ph.sem("near_ready")
        near_ready_v = ph.sem("near_ready_v")
        out_ready = ph.sem("out_ready")
        added = ph.sem("added")
        bias_added = ph.sem("bias_added")
        block = nc.Block()
        block.__enter__()

        @block.sync
        def _(sp):
            sp.dma_start(weight[:, :].rearrange("f (k o) -> f k o", k=3), ins["L3_gnn_W"].rearrange("k f o -> f k o"))\
                .then_inc(loaded, 16)
            load_next(sp)

        @block.tensor
        def _(pe):
            def gathers(h):
                pe.wait_ge(norm.xn_ready, h + 1)
                for b in range(GB):
                    if h.least:
                        pe.wait_ge(near_ready_v if b % 2 else near_ready, h * 2 + b // 2 - 1)
                    pe.matmul(gather[b][:, 0:3 * P], tile_of(xn[h.odd], b), parts[:, :], start=True, stop=True)\
                        .then_inc(gather_ready, 1)

            def outs(g):
                if g.least >= 2:
                    pe.wait_ge(added, g - 1)
                for b in range(GB):
                    pe.wait_ge(near_ready_v if b % 2 else near_ready, g * 2 + b // 2 + 1)
                    for k in range(3):
                        mm = pe.matmul(tile_of(out[g.odd], b), near[b][:, k * P:(k + 1) * P],
                                       weight[:, k * P:(k + 1) * P], start=(k == 0), stop=(k == 2))
                    mm.then_inc(out_ready, 1)

            def group(g, behind, ahead):
                if ahead is not None:
                    gathers(ahead)
                outs(g)

            pe.wait_ge(loaded, 16)
            pe.wait_ge(parts_step, 3)
            gathers(group_number(0))
            over_groups(pe, group)

        def take(engine, copy, done, g, b):
            engine.wait_ge(gather_ready, g * GB + b + 1)
            if g.least:
                engine.wait_ge(out_ready, g * GB - GB + b + 1)
            copy(near[b][:, :], gather[b][:, 0:3 * P]).then_inc(done, 1)

        @block.scalar
        def _(scalar):
            def group(g, behind, ahead):
                for b in (0, 2):
                    take(scalar, lambda o, i: scalar.activation(o, i, ACT.Copy), near_ready, g, b)

            over_groups(scalar, group)

        @block.vector
        def _(dve):
            def front(h):
                norm.moments(dve, h)
                if h.least >= 2:
                    dve.wait_ge(gather_ready, h * GB - GB)
                norm.normalise(dve, h)

            def add(g):
                dve.wait_ge(out_ready, g * GB + GB)
                dve.wait_ge(bias_added, g + 1)
                dve.tensor_tensor(group_of(x, g), group_of(x, g), out[g.odd][:, :], ALU.add).then_inc(added, 1)

            def group(g, behind, ahead):
                for b in (1, 3):
                    take(dve, dve.tensor_copy, near_ready_v, g, b)
                if ahead is not None:
                    front(ahead)
                add(g)

            front(group_number(0))
            over_groups(dve, group)

        @block.gpsimd
        def _(pool):
            done = 0
            for k, compare, sign in ((0, ALU.is_equal, 1), (1, ALU.is_gt, 1), (2, ALU.is_gt, -1)):
                pool.affine_select(out=parts[:, k * P:(k + 1) * P], in_=chip.adj_t[:, :], compare_op=compare, fill=0.0,
                                   base=0, pattern=[[-sign, P]], channel_multiplier=sign).then_inc(parts_step, 1)

            def bias(g):
                pool.wait_ge(norm.xn_ready, g + 1)
                pool.tensor_tensor(by_graph(group_of(x, g)), by_graph(group_of(x, g)),
                                   chip.tables["L2"]["L3_b"].unsqueeze(1).to_broadcast([P, GB, P]), ALU.add)\
                    .then_inc(bias_added, 1)

            def group(g, behind, ahead):
                if ahead is not None:
                    norm.deviation(pool, ahead)
                bias(g)

            norm.deviation(pool, group_number(0))
            over_groups(pool, group)

        block.__exit__(None, None, None)



def recurrent(nc, chip, ins, load_next):
    with ExitStack() as keep:
        hidden = keep.enter_context(nc.sbuf_tensor("hidden", [P, NB * P], F32))
        lstm_w = keep.enter_context(nc.sbuf_tensor("lstm_w", [P, 2 * 16 * P], F32))
        lstm_loaded = keep.enter_context(nc.semaphore("lstm_loaded"))
        convolutions(nc, chip, ins, hidden, lstm_w, lstm_loaded)
        lstms(nc, chip, hidden, lstm_w, lstm_loaded, load_next)
        add_hidden(nc, chip, hidden)


def convolutions(nc, chip, ins, hidden, lstm_w, lstm_loaded):
    with Phase(nc, "conv") as ph:
        norm = Norm(ph, chip)
        x, xn = chip.x, norm.xn
        w0, w1 = ph.sb("w0", [P, P]), ph.sb("w1", [P, P])
        ones = ph.sb("ones", [P, P])
        bias0 = ph.sb("bias0", [P, P])
        near = ph.sb("near", [P, COLS])
        first_sum = ph.sb("first_sum", [P, COLS])
        first = ph.sb("first", [P, COLS])
        second = ph.sb("second", [P, COLS])
        gather, project0, project1, gather1, sums = (ph.bank(n) for n in
                                                     ("gather", "project0", "project1", "gather1", "sums"))
        loaded = ph.sem("loaded")
        ones_set = ph.sem("ones_set")
        sums_ready = ph.sem("sums_ready")
        bias0_ready = ph.sem("bias0_ready")
        gather_ready = ph.sem("gather_ready")
        near_ready = ph.sem("near_ready")
        project0_ready = ph.sem("project0_ready")
        sum0_ready = ph.sem("sum0_ready")
        first_ready = ph.sem("first_ready")
        project1_ready = ph.sem("project1_ready")
        second_ready = ph.sem("second_ready")
        gather1_ready = ph.sem("gather1_ready")
        hidden_ready = ph.sem("hidden_ready")
        block = nc.Block()
        block.__enter__()

        @block.sync
        def _(sp):
            sp.dma_start(w0[:, :], ins["L1_gnn_Wg0"]).then_inc(loaded, 16)
            sp.dma_start(w1[:, :], ins["L1_gnn_Wg1"]).then_inc(loaded, 16)
            for n, name in enumerate(("L1_gnn_Wih", "L1_gnn_Whh")):
                sp.dma_start(lstm_w[:, n * 16 * P:(n + 1) * 16 * P].rearrange("h (r d) -> h r d", d=P),
                             ins[name].rearrange("p (t h) d -> h (p t) d", h=P)).then_inc(lstm_loaded, 16)

        @block.gpsimd
        def _(pool):
            pool.memset(ones[:, :], 1.0).then_inc(ones_set, 1)
            norm.deviation(pool, group_number(0))

            def group(g, behind, ahead):
                if ahead is not None:
                    norm.deviation(pool, ahead)

            over_groups(pool, group)

        @block.tensor
        def _(pe):
            def gathers(h):
                pe.wait_ge(norm.xn_ready, h + 1)
                if h.least:
                    pe.wait_ge(near_ready, h.n)
                for b in range(GB):
                    mm = pe.matmul(tile_of(gather, b), tile_of(xn[h.odd], b), chip.adj_t[:, :], start=True, stop=True)
                mm.then_inc(gather_ready, 1)

            def first_projection(h):
                pe.wait_ge(near_ready, h + 1)
                if h.least:
                    pe.wait_ge(sum0_ready, h.n)
                pe.matmul(project0[:, :], w0[:, :], near[:, :], start=True, stop=True).then_inc(project0_ready, 1)

            def second_projection(g):
                pe.wait_ge(first_ready, g + 1)
                if g.least:
                    pe.wait_ge(second_ready, g.n)
                for b in range(GB):
                    mm = pe.matmul(tile_of(project1, b), tile_of(first, b), w1[:, :], start=True, stop=True)
                mm.then_inc(project1_ready, 1)

            def second_gathers(g):
                pe.wait_ge(second_ready, g + 1)
                if g.least:
                    pe.wait_ge(hidden_ready, g.n)
                for b in range(GB):
                    mm = pe.matmul(tile_of(gather1, b), tile_of(second, b), chip.adj_t[:, :], start=True, stop=True)
                mm.then_inc(gather1_ready, 1)

            def group(g, behind, ahead):
                if ahead is not None:
                    gathers(ahead)
                second_projection(g)
                if ahead is not None:
                    first_projection(ahead)
                second_gathers(g)

            pe.wait_ge(loaded, 32)
            pe.wait_ge(ones_set, 1)
            pe.matmul(sums[:, 0:P], ones[:, :], chip.adj_t[:, :], start=True, stop=True).then_inc(sums_ready, 1)
            gathers(group_number(0))
            first_projection(group_number(0))
            over_groups(pe, group)

        @block.scalar
        def _(scalar):
            def take_near(h):
                scalar.wait_ge(gather_ready, h + 1)
                if h.least:
                    scalar.wait_ge(project0_ready, h.n)
                scalar.activation(near[:, :], gather[:, :], ACT.Copy).then_inc(near_ready, 1)

            def take_first(h):
                scalar.wait_ge(sum0_ready, h + 1)
                if h.least:
                    scalar.wait_ge(project1_ready, h.n)
                scalar.activation(first[:, :], first_sum[:, :], ACT.Relu).then_inc(first_ready, 1)

            def take_hidden(g):
                scalar.wait_ge(gather1_ready, g + 1)
                scalar.activation(group_of(hidden, g), gather1[:, :], ACT.Relu).then_inc(hidden_ready, 1)

            def group(g, behind, ahead):
                if ahead is not None:
                    take_near(ahead)
                    take_first(ahead)
                take_hidden(g)

            take_near(group_number(0))
            take_first(group_number(0))
            over_groups(scalar, group)

        @block.vector
        def _(dve):
            def front(h):
                norm.moments(dve, h)
                if h.least >= 2:
                    dve.wait_ge(gather_ready, h - 1)
                norm.normalise(dve, h)

            def add_bias0(h):
                dve.wait_ge(project0_ready, h + 1)
                if h.least:
                    dve.wait_ge(first_ready, h.n)
                dve.tensor_tensor(by_graph(first_sum[:, :]), by_graph(project0[:, :]),
                                  bias0[:, :].unsqueeze(1).to_broadcast([P, GB, P]), ALU.add).then_inc(sum0_ready, 1)

            def add_bias1(g):
                dve.wait_ge(project1_ready, g + 1)
                if g.least:
                    dve.wait_ge(gather1_ready, g.n)
                dve.tensor_tensor(by_graph(second[:, :]), by_graph(project1[:, :]),
                                  chip.tables["L2"]["bg1"].unsqueeze(1).to_broadcast([P, GB, P]), ALU.add)\
                    .then_inc(second_ready, 1)

            def group(g, behind, ahead):
                add_bias1(g)
                if ahead is not None:
                    add_bias0(ahead)
                    if ahead.least < NG - 1:
                        front(ahead.next())

            dve.wait_ge(sums_ready, 1)
            dve.tensor_scalar(bias0[:, :], sums[:, 0:P], chip.bg0, None, ALU.mult).then_inc(bias0_ready, 1)
            front(group_number(0))
            front(group_number(1))
            dve.wait_ge(bias0_ready, 1)
            add_bias0(group_number(0))
            over_groups_wide(dve, group)

        block.__exit__(None, None, None)


LSTMS = ((1, 4), (2, 8), (3, 8), (4, 16))


def lstms(nc, chip, hidden, lstm_w, lstm_loaded, load_next):
    with Phase(nc, "lstm") as ph:
        weight = ph.sb("weight", [P, 2 * 16 * P])
        gates = [[ph.bank(f"gate{c}_{j}") for j in range(4)] for c in range(2)]
        value = [[ph.sb(f"value{c}_{j}", [P, COLS]) for j in range(4)] for c in range(2)]
        cell = [ph.sb(f"cell{c}", [P, COLS]) for c in range(2)]
        kept = [ph.sb(f"kept{c}", [P, COLS]) for c in range(2)]
        cell_tanh = [ph.sb(f"cell_tanh{c}", [P, COLS]) for c in range(2)]
        state = [ph.sb(f"state{c}", [P, COLS]) for c in range(2)]
        turned = ph.sem("turned")
        weights_ready = ph.sem("weights_ready")
        gate_ready = ph.sem("gate_ready")
        gate_done = ph.sem("gate_done")
        kept_step = ph.sem("kept_step")
        cell_ready = ph.sem("cell_ready")
        tanh_ready = ph.sem("tanh_ready")
        state_ready = ph.sem("state_ready")
        block = nc.Block()
        block.__enter__()
        ORDER = (0, 2, 1, 3)

        def gates_of(s):
            return [j for j in ORDER if s or j != 1]

        def over_units(engine, unit):
            units = later = gates_before = 0
            for p, graphs in LSTMS:
                pairs = NB // graphs // 2
                per_pair = 2 * sum(len(gates_of(s)) for s in range(p))

                def two(pair, opening):
                    u, at = pair * (2 * p) + units, pair * per_pair + gates_before
                    more = pair * (2 * p - 2) + later
                    n = 0
                    for s in range(p):
                        for c in range(2):
                            unit(p, graphs, pair, s, c, u + (2 * s + c), more + (2 * s - 2 + c), at + n,
                                 opening and s == 0)
                            n += len(gates_of(s))

                two(0, True)
                with engine.Fori(1, pairs) as pair:
                    two(pair, False)
                units += pairs * 2 * p
                later += pairs * 2 * (p - 1)
                gates_before += pairs * per_pair

        def windows(p, graphs, pair, c, s):
            n = P // p
            chunk = hidden[:, bass.ds((pair * 2 + c) * (graphs * P), graphs * P)].rearrange("h (b t) -> h b t", t=P)
            return chunk[:, :, s:s + p * (n - 1) + 1:p]

        def columns(buf, p, graphs):
            return buf[:, 0:graphs * (P // p)]

        def as_windows(buf, p, graphs):
            return columns(buf, p, graphs).rearrange("h (b w) -> h b w", b=graphs)

        @block.sync
        def _(sp):
            load_next(sp)

        @block.tensor
        def _(pe):
            pe.wait_ge(lstm_loaded, 32)
            for c in range(8):
                if c >= 8:
                    pe.wait_ge(weights_ready, c - 7)
                for b in range(GB):
                    mm = pe.transpose(tile_of(gates[c // 4][c % 4], b), tile_of(lstm_w[:, c * COLS:(c + 1) * COLS], b),
                                      chip.ident)
                mm.then_inc(turned, 1)
            pe.wait_ge(weights_ready, 8)

            def unit(p, graphs, pair, s, c, units, later, gates_before, opening):
                if not (p == 1 and opening):
                    behind = gates_before_last(p, s, c, opening)
                    pe.wait_ge(gate_done, gates_before - behind)
                if opening and p > 1 and c == 0:
                    pe.wait_ge(state_ready, units)
                for j in gates_of(s):
                    mm = pe.matmul(as_windows(gates[c][j], p, graphs), weight[:, ((p - 1) * 4 + j) * P:((p - 1) * 4 + j + 1) * P],
                                   windows(p, graphs, pair, c, s), start=True, stop=(s == 0))
                    if s == 0:
                        mm.then_inc(gate_ready, 1)
                if s:
                    pe.wait_ge(state_ready, units - 1)
                    for j in gates_of(s):
                        at = (16 + (p - 1) * 4 + j) * P
                        pe.matmul(columns(gates[c][j], p, graphs), weight[:, at:at + P], columns(state[c], p, graphs),
                                  start=False, stop=True).then_inc(gate_ready, 1)

            def gates_before_last(p, s, c, opening):
                if c == 1:
                    return len(gates_of(s))
                if s:
                    return len(gates_of(s - 1))
                return len(gates_of((p - 1) if not opening else (p - 2)))

            over_units(pe, unit)

        @block.scalar
        def _(scalar):
            for c in range(8):
                scalar.wait_ge(turned, c + 1)
                scalar.activation(weight[:, c * COLS:(c + 1) * COLS], gates[c // 4][c % 4][:, :], ACT.Copy)\
                    .then_inc(weights_ready, 1)

            def unit(p, graphs, pair, s, c, units, later, gates_before, opening):
                if not (p == 1 and opening):
                    scalar.wait_ge(state_ready, units - 1)
                for n, j in enumerate(gates_of(s)):
                    scalar.wait_ge(gate_ready, gates_before + (n + 1))
                    scalar.activation(columns(value[c][j], p, graphs), columns(gates[c][j], p, graphs),
                                      ACT.Tanh if j == 2 else ACT.Sigmoid,
                                      bias=chip.lstm_bias[:, (p - 1) * 4 + j:(p - 1) * 4 + j + 1]).then_inc(gate_done, 1)
                scalar.wait_ge(cell_ready, units + 1)
                scalar.activation(columns(cell_tanh[c], p, graphs), columns(cell[c], p, graphs), ACT.Tanh)\
                    .then_inc(tanh_ready, 1)

            over_units(scalar, unit)

        @block.vector
        def _(dve):
            def unit(p, graphs, pair, s, c, units, later, gates_before, opening):
                def cols(buf):
                    return columns(buf, p, graphs)

                i, f, g, o = (cols(value[c][j]) for j in range(4))
                if not (p == 1 and opening):
                    dve.wait_ge(cell_ready, units - 1)
                    dve.wait_ge(tanh_ready, units - 1)
                if s == 0:
                    dve.wait_ge(gate_done, gates_before + 2)
                    dve.tensor_tensor(cols(cell[c]), i, g, ALU.mult).then_inc(cell_ready, 1)
                else:
                    dve.wait_ge(gate_done, gates_before + 2)
                    dve.tensor_tensor(cols(kept[c]), i, g, ALU.mult).then_inc(kept_step, 1)
                    dve.wait_ge(gate_done, gates_before + 3)
                    dve.tensor_tensor(cols(cell[c]), cols(cell[c]), f, ALU.mult).then_inc(kept_step, 1)
                    dve.wait_ge(kept_step, later * 2 + 2)
                    dve.tensor_tensor(cols(cell[c]), cols(cell[c]), cols(kept[c]), ALU.add).then_inc(cell_ready, 1)
                dve.wait_ge(tanh_ready, units + 1)
                if s < p - 1:
                    dve.tensor_tensor(cols(state[c]), o, cols(cell_tanh[c]), ALU.mult).then_inc(state_ready, 1)
                else:
                    dve.tensor_tensor(windows(p, graphs, pair, c, s), as_windows(value[c][3], p, graphs),
                                      as_windows(cell_tanh[c], p, graphs), ALU.mult).then_inc(state_ready, 1)

            over_units(dve, unit)

        block.__exit__(None, None, None)


def add_hidden(nc, chip, hidden):
    with Phase(nc, "fold") as ph:
        copy = [ph.sb(f"copy{i}", [P, COLS]) for i in range(2)]
        turn = [ph.bank(f"turn{i}") for i in range(2)]
        copy_ready = ph.sem("copy_ready")
        turn_ready = ph.sem("turn_ready")
        added = ph.sem("added")
        block = nc.Block()
        block.__enter__()

        @block.scalar
        def _(scalar):
            def group(g, behind, ahead):
                if g.least >= 2:
                    scalar.wait_ge(turn_ready, g - 1)
                scalar.activation(copy[g.odd][:, :], group_of(hidden, g), ACT.Copy).then_inc(copy_ready, 1)

            over_groups_wide(scalar, group)

        @block.tensor
        def _(pe):
            def group(g, behind, ahead):
                pe.wait_ge(copy_ready, g + 1)
                if g.least >= 2:
                    pe.wait_ge(added, g - 1)
                for b in range(GB):
                    mm = pe.transpose(tile_of(turn[g.odd], b), tile_of(copy[g.odd], b), chip.ident)
                mm.then_inc(turn_ready, 1)

            over_groups_wide(pe, group)

        @block.vector
        def _(dve):
            def group(g, behind, ahead):
                dve.wait_ge(turn_ready, g + 1)
                dve.tensor_tensor(group_of(chip.x, g), group_of(chip.x, g), turn[g.odd][:, :], ALU.add)\
                    .then_inc(added, 1)

            over_groups_wide(dve, group)

        block.__exit__(None, None, None)



HEADS = 4
EDGES = 256
ET = EDGES // P
ROWS = NB * HEADS
LRELU = 0.2
EDGE_EPS = 1e-8
FAR = -1e30


def edges(nc, chip, ins, load_next):
    with ExitStack() as keep:
        def kept(name, shape):
            return keep.enter_context(nc.sbuf_tensor(f"edge_{name}", shape, F32))

        t = Chip()
        t.loaded = keep.enter_context(nc.semaphore("edge_loaded"))
        t.at_src = kept("at_src", [P, EDGES])
        t.at_dst = kept("at_dst", [P, EDGES])
        t.at_both = kept("at_both", [P, EDGES])
        t.src_t = kept("src_t", [P, ET, P])
        t.last_t = kept("last_t", [P, ET, P])
        t.restart = kept("restart", [P, EDGES])
        t.log_adj = kept("log_adj", [P, ET])
        t.heads = kept("heads", [P, HEADS])
        t.weights = kept("weights", [P, 3 * P])
        t.values = kept("values", [P, NB * P])
        t.score = kept("score", [P, ET, ROWS])
        edge_tables(nc, chip, ins, t)
        edge_scores(nc, chip, t, load_next)
        edge_softmax(nc, chip, t)
        edge_sums(nc, chip, t)


def edge_tables(nc, chip, ins, t):
    with Phase(nc, "etab") as ph:
        ends = ph.sb("ends", [1, 2 * EDGES], I32)
        endsf = ph.sb("endsf", [1, 2 * EDGES])
        key = ph.sb("key", [1, EDGES])
        ones = ph.sb("ones", [P, P])
        count = ph.sb("count", [P, EDGES])
        own = ph.sb("own", [P, 1])
        heads_at = ph.sb("heads_at", [P, HEADS])
        a_col = ph.sb("a_col", [P, 1])
        raw_w = ph.sb("raw_w", [P, 3 * P])
        key_all = ph.sb("key_all", [P, EDGES])
        key_col = ph.sb("key_col", [P, 3 * ET])
        below = ph.sb("below", [P, ET, EDGES])
        rank = ph.sb("rank", [P, ET])
        perm = ph.sb("perm", [P, ET, EDGES])
        spread = ph.sb("spread", [P, 2 * ET, P])
        sorted_ends = ph.sb("sorted_ends", [P, 2, EDGES])
        is_last = ph.sb("is_last", [P, EDGES])
        dst_t = ph.sb("dst_t", [P, ET, P])
        last_of = ph.sb("last_of", [P, EDGES])
        adj_at = ph.sb("adj_at", [P, ET, P])
        adj_sum = ph.sb("adj_sum", [P, ET])
        banks = [ph.bank(f"bank{i}") for i in range(8)]
        loaded = ph.sem("loaded")
        pool_step = ph.sem("pool_step")
        step = ph.sem("step")
        product = ph.sem("product")
        logged = ph.sem("logged")
        block = nc.Block()
        block.__enter__()

        @block.sync
        def _(sp):
            for n, name in enumerate(("L2_gnn_src", "L2_gnn_dst")):
                sp.dma_start(ends[:, n * EDGES:(n + 1) * EDGES], ins[name].rearrange("(a e) -> a e", a=1))\
                    .then_inc(loaded, 16)
            for n, name in enumerate(("L2_gnn_W_lin", "L2_gnn_W_val", "L2_gnn_W_out")):
                sp.dma_start(tile_of(raw_w, n), ins[name]).then_inc(loaded, 16)
            sp.dma_start(a_col[:, :], ins["L2_gnn_a"].rearrange("h (d a) -> (h d) a", a=1)).then_inc(loaded, 16)

        @block.gpsimd
        def _(pool):
            pool.memset(ones[:, :], 1.0).then_inc(pool_step, 1)
            pool.memset(heads_at[:, :], 1.0).then_inc(pool_step, 1)
            pool.iota(count[:, :], [[1, EDGES]], base=0, channel_multiplier=0, allow_small_or_imprecise_dtypes=True)\
                .then_inc(pool_step, 1)
            pool.iota(own[:, :], [[1, 1]], base=0, channel_multiplier=1, allow_small_or_imprecise_dtypes=True)\
                .then_inc(pool_step, 1)
            pool.wait_ge(pool_step, 4)
            d = P // HEADS
            pool.affine_select(out=heads_at[:, :], in_=heads_at[:, :], compare_op=ALU.is_ge, fill=0.0, base=0,
                               pattern=[[-d, HEADS]], channel_multiplier=1).then_inc(pool_step, 1)
            pool.wait_ge(pool_step, 5)
            pool.affine_select(out=heads_at[:, :], in_=heads_at[:, :], compare_op=ALU.is_gt, fill=0.0, base=d,
                               pattern=[[d, HEADS]], channel_multiplier=-1).then_inc(pool_step, 1)

        @block.vector
        def _(dve):
            done = [0]

            def link(op):
                op.then_inc(step, 1)
                done[0] += 1
                dve.wait_ge(step, done[0])

            dve.wait_ge(loaded, 96)
            dve.wait_ge(pool_step, 6)
            link(dve.tensor_copy(endsf[:, :], ends[:, :]))
            link(dve.scalar_tensor_tensor(out=key[:, :], in0=endsf[:, 0:EDGES], scalar=float(EDGES),
                                          in1=count[0:1, :], op0=ALU.mult, op1=ALU.add))
            assert done[0] == 2
            link(dve.tensor_scalar(t.heads[:, :], heads_at[:, :], a_col[:, 0:1], None, ALU.mult))
            dve.wait_ge(product, 1)
            link(dve.tensor_copy(key_all[:, :], banks[0][:, 0:EDGES]))
            link(dve.tensor_copy(key_col[:, :], banks[1][:, 0:3 * ET]))
            link(dve.tensor_copy(t.weights[:, :], banks[2][:, 0:3 * P]))
            for e in range(ET):
                link(dve.tensor_scalar(below[:, e, :], key_all[:, :], key_col[:, e:e + 1], None, ALU.is_lt))
            link(dve.reduce_sum(rank[:, :], below[:, :, :], AX.X))
            for e in range(ET):
                link(dve.tensor_scalar(perm[:, e, :], count[:, :], rank[:, e:e + 1], None, ALU.is_equal))
            for n in range(2 * ET):
                link(dve.tensor_scalar(spread[:, n, :], ones[:, :], key_col[:, ET + n:ET + n + 1], None, ALU.mult))
            assert done[0] == 15
            dve.wait_ge(product, 2)
            link(dve.tensor_copy(sorted_ends[:, :, :], banks[3][:, :].rearrange("p (n e) -> p n e", n=2)))
            link(dve.tensor_scalar(t.at_src[:, :], sorted_ends[:, 0, :], own[:, 0:1], None, ALU.is_equal))
            link(dve.tensor_scalar(t.at_dst[:, :], sorted_ends[:, 1, :], own[:, 0:1], None, ALU.is_equal))
            link(dve.tensor_tensor(t.at_both[:, :], t.at_src[:, :], t.at_dst[:, :], ALU.add))
            link(dve.memset(is_last[:, :], 1.0))
            link(dve.tensor_tensor(is_last[:, 0:EDGES - 1], sorted_ends[:, 0, 0:EDGES - 1], sorted_ends[:, 0, 1:EDGES],
                                   ALU.not_equal))
            link(dve.memset(t.restart[:, :], 0.0))
            link(dve.tensor_scalar(t.restart[:, 1:EDGES], is_last[:, 0:EDGES - 1], FAR, None, ALU.mult))
            link(dve.tensor_tensor(last_of[:, :], t.at_src[:, :], is_last[:, :], ALU.mult))
            assert done[0] == 24
            dve.wait_ge(product, 3)
            link(dve.tensor_copy(t.src_t[:, :, :], banks[4][:, 0:ET * P].rearrange("p (t n) -> p t n", t=ET)))
            link(dve.tensor_copy(dst_t[:, :, :], banks[5][:, 0:ET * P].rearrange("p (t n) -> p t n", t=ET)))
            link(dve.tensor_copy(t.last_t[:, :, :], banks[6][:, 0:ET * P].rearrange("p (t n) -> p t n", t=ET)))
            link(dve.tensor_tensor(adj_at[:, :, :], banks[7][:, 0:ET * P].rearrange("p (t n) -> p t n", t=ET),
                                   dst_t[:, :, :], ALU.mult))
            link(dve.reduce_sum(adj_sum[:, :], adj_at[:, :, :], AX.X))
            link(dve.tensor_scalar(adj_sum[:, :], adj_sum[:, :], EDGE_EPS, None, ALU.add))
            assert done[0] == 30

        @block.scalar
        def _(scalar):
            scalar.wait_ge(step, 30)
            scalar.activation(t.log_adj[:, :], adj_sum[:, :], ACT.Ln).then_inc(logged, 1)

        @block.tensor
        def _(pe):
            pe.wait_ge(step, 2)
            pe.matmul(banks[0][:, 0:EDGES], ones[0:1, :], key[:, :], start=True, stop=True)
            for e in range(ET):
                for n, row in enumerate((key, endsf, endsf)):
                    at = e * P + (EDGES if n == 2 else 0)
                    pe.matmul(banks[1][:, n * ET + e:n * ET + e + 1], row[:, at:at + P], ones[0:1, 0:1],
                              start=True, stop=True)
            for n in range(3):
                mm = pe.transpose(tile_of(banks[2], n), tile_of(raw_w, n), chip.ident)
            mm.then_inc(product, 1)
            pe.wait_ge(step, 15)
            for n in range(2):
                for e in range(ET):
                    mm = pe.matmul(banks[3][:, n * EDGES:(n + 1) * EDGES], spread[:, n * ET + e, :], perm[:, e, :],
                                   start=(e == 0), stop=(e == ET - 1))
            mm.then_inc(product, 1)
            pe.wait_ge(step, 24)
            for e in range(ET):
                pe.transpose(tile_of(banks[4], e), tile_of(t.at_src, e), chip.ident)
                pe.transpose(tile_of(banks[5], e), tile_of(t.at_dst, e), chip.ident)
                pe.transpose(tile_of(banks[6], e), tile_of(last_of, e), chip.ident)
                mm = pe.matmul(tile_of(banks[7], e), tile_of(t.at_src, e), chip.adj[:, :], start=True, stop=True)
            mm.then_inc(product, 1)

        block.__exit__(None, None, None)


def edge_scores(nc, chip, t, load_next):
    with Phase(nc, "esco") as ph:
        norm = Norm(ph, chip)
        xn = norm.xn
        xt = ph.sb("xt", [P, COLS])
        query = ph.sb("query", [P, COLS])
        small_sum = [ph.sb(f"small_sum{i}", [P, COLS]) for i in range(2)]
        leaky = [ph.sb(f"leaky{i}", [P, COLS]) for i in range(2)]
        turn, queries, values, score = (ph.bank(n) for n in ("turn", "queries", "values", "score"))
        sums = [ph.bank(f"sums{i}") for i in range(2)]
        turn_ready = ph.sem("turn_ready")
        xt_ready = ph.sem("xt_ready")
        query_ready = ph.sem("query_ready")
        value_ready = ph.sem("value_ready")
        query_taken = ph.sem("query_taken")
        value_taken = ph.sem("value_taken")
        sum_ready = ph.sem("sum_ready")
        small_ready = ph.sem("small_ready")
        leaky_ready = ph.sem("leaky_ready")
        score_ready = ph.sem("score_ready")
        score_taken = ph.sem("score_taken")
        block = nc.Block()
        block.__enter__()

        @block.sync
        def _(sp):
            load_next(sp)

        @block.gpsimd
        def _(pool):
            def group(g, behind, ahead):
                if ahead is not None:
                    norm.deviation(pool, ahead)

            norm.deviation(pool, group_number(0))
            over_groups(pool, group)

        @block.tensor
        def _(pe):
            def turn_tokens(h):
                pe.wait_ge(norm.xn_ready, h + 1)
                if h.least:
                    pe.wait_ge(xt_ready, h.n)
                for b in range(GB):
                    mm = pe.transpose(tile_of(turn, b), tile_of(xn[h.odd], b), chip.ident)
                mm.then_inc(turn_ready, 1)

            def project(h):
                pe.wait_ge(xt_ready, h + 1)
                if h.least:
                    pe.wait_ge(query_taken, h.n)
                for b in range(GB):
                    mm = pe.matmul(tile_of(queries, b), tile_of(xt, b), t.weights[:, 0:P], start=True, stop=True)
                mm.then_inc(query_ready, 1)
                if h.least:
                    pe.wait_ge(value_taken, h.n)
                for b in range(GB):
                    mm = pe.matmul(tile_of(values, b), tile_of(xt, b), t.weights[:, P:2 * P], start=True, stop=True)
                mm.then_inc(value_ready, 1)

            def sum_ends(h):
                pe.wait_ge(query_taken, h + 1)
                for i in range(2):
                    if h.least:
                        pe.wait_ge(leaky_ready, h * 2 - 1 + i)
                    for b in range(2):
                        mm = pe.matmul(sums[i][:, b * EDGES:(b + 1) * EDGES], tile_of(query, 2 * i + b),
                                       t.at_both[:, :], start=True, stop=True)
                    mm.then_inc(sum_ready, 1)

            def scores(g):
                if g.least:
                    pe.wait_ge(score_taken, g.n)
                for b in range(GB):
                    if b % 2 == 0:
                        pe.wait_ge(leaky_ready, g * 2 + b // 2 + 1)
                    for e in range(ET):
                        at = (b % 2) * EDGES + e * P
                        mm = pe.matmul(score[:, (e * GB + b) * HEADS:(e * GB + b + 1) * HEADS],
                                       leaky[b // 2][:, at:at + P], t.heads[:, :], start=True, stop=True)
                mm.then_inc(score_ready, 1)

            def group(g, behind, ahead):
                if ahead is not None:
                    turn_tokens(ahead)
                scores(g)
                if ahead is not None:
                    project(ahead)
                    sum_ends(ahead)

            turn_tokens(group_number(0))
            project(group_number(0))
            sum_ends(group_number(0))
            over_groups(pe, group)

        @block.scalar
        def _(scalar):
            def front(h):
                scalar.wait_ge(turn_ready, h + 1)
                if h.least:
                    scalar.wait_ge(value_ready, h.n)
                scalar.activation(xt[:, :], turn[:, :], ACT.Copy).then_inc(xt_ready, 1)
                scalar.wait_ge(query_ready, h + 1)
                if h.least:
                    scalar.wait_ge(sum_ready, h * 2)
                scalar.activation(query[:, :], queries[:, :], ACT.Copy).then_inc(query_taken, 1)

            def small(h):
                for i in range(2):
                    scalar.wait_ge(sum_ready, h * 2 + i + 1)
                    if h.least:
                        scalar.wait_ge(leaky_ready, h * 2 - 1 + i)
                    scalar.activation(small_sum[i][:, :], sums[i][:, :], ACT.Copy, scale=LRELU).then_inc(small_ready, 1)

            def group(g, behind, ahead):
                small(g)
                if ahead is not None:
                    front(ahead)

            front(group_number(0))
            over_groups(scalar, group)

        @block.vector
        def _(dve):
            def front(h):
                norm.moments(dve, h)
                if h.least >= 2:
                    dve.wait_ge(turn_ready, h - 1)
                norm.normalise(dve, h)

            def take_values(h):
                dve.wait_ge(value_ready, h + 1)
                dve.tensor_copy(group_of(t.values, h), values[:, :]).then_inc(value_taken, 1)

            def leak(h):
                for i in range(2):
                    dve.wait_ge(small_ready, h * 2 + i + 1)
                    if h.least:
                        dve.wait_ge(score_ready, h.n)
                    dve.tensor_tensor(leaky[i][:, :], sums[i][:, :], small_sum[i][:, :], ALU.max)\
                        .then_inc(leaky_ready, 1)

            def take_scores(g):
                dve.wait_ge(score_ready, g + 1)
                n = GB * HEADS
                for e in range(ET):
                    op = dve.tensor_scalar(t.score[:, e, bass.ds(g * n, n)], score[:, e * n:(e + 1) * n],
                                           t.log_adj[:, e:e + 1], None, ALU.add)
                op.then_inc(score_taken, 1)

            def group(g, behind, ahead):
                leak(g)
                if ahead is not None:
                    take_values(ahead)
                    if ahead.least < NG - 1:
                        front(ahead.next())
                take_scores(g)

            front(group_number(0))
            take_values(group_number(0))
            front(group_number(1))
            over_groups_wide(dve, group)

        block.__exit__(None, None, None)


def edge_softmax(nc, chip, t):
    with Phase(nc, "esof") as ph:
        rows = ph.sb("rows", [P, 2, EDGES])
        running = ph.sb("running", [P, 2, EDGES])
        running_t = ph.sb("running_t", [P, ET, ROWS])
        node_max = ph.sb("node_max", [P, ROWS])
        shifted = ph.sb("shifted", [P, ET, ROWS])
        expd = ph.sb("expd", [P, ET, ROWS])
        node_sum = ph.sb("node_sum", [P, ROWS])
        edge_inv = ph.sb("edge_inv", [P, ET, ROWS])
        turned, back, of_node, of_edge, sum_node, sum_edge = (ph.bank(n) for n in (
            "turned", "back", "of_node", "of_edge", "sum_node", "sum_edge"))
        product = ph.sem("product")
        step = ph.sem("step")
        exp_ready = ph.sem("exp_ready")
        block = nc.Block()
        block.__enter__()

        @block.tensor
        def _(pe):
            for r in range(2):
                for e in range(ET):
                    mm = pe.transpose(turned[:, r * EDGES + e * P:r * EDGES + (e + 1) * P],
                                      t.score[:, e, r * P:(r + 1) * P], chip.ident)
            mm.then_inc(product, 1)
            pe.wait_ge(step, 3)
            for r in range(2):
                for e in range(ET):
                    mm = pe.transpose(back[:, e * ROWS + r * P:e * ROWS + (r + 1) * P],
                                      running[:, r, e * P:(e + 1) * P], chip.ident)
            mm.then_inc(product, 1)
            pe.wait_ge(step, 4)
            for e in range(ET):
                mm = pe.matmul(of_node[:, 0:ROWS], t.last_t[:, e, :], running_t[:, e, :], start=(e == 0),
                               stop=(e == ET - 1))
            mm.then_inc(product, 1)
            pe.wait_ge(step, 5)
            for e in range(ET):
                mm = pe.matmul(of_edge[:, e * ROWS:(e + 1) * ROWS], tile_of(t.at_src, e), node_max[:, :],
                               start=True, stop=True)
            mm.then_inc(product, 1)
            pe.wait_ge(exp_ready, 1)
            for e in range(ET):
                mm = pe.matmul(sum_node[:, 0:ROWS], t.src_t[:, e, :], expd[:, e, :], start=(e == 0), stop=(e == ET - 1))
            mm.then_inc(product, 1)
            pe.wait_ge(step, 7)
            for e in range(ET):
                mm = pe.matmul(sum_edge[:, e * ROWS:(e + 1) * ROWS], tile_of(t.at_src, e), node_sum[:, :],
                               start=True, stop=True)
            mm.then_inc(product, 1)

        @block.vector
        def _(dve):
            def tiles(bank):
                return bank[:, :].rearrange("p (t r) -> p t r", t=2)

            dve.wait_ge(product, 1)
            dve.tensor_copy(rows[:, :, :], tiles(turned)).then_inc(step, 1)
            dve.wait_ge(step, 1)
            for r in range(2):
                dve.tensor_tensor_scan(running[:, r, :], t.restart[:, :], rows[:, r, :], FAR, ALU.add, ALU.max)\
                    .then_inc(step, 1)
            dve.wait_ge(product, 2)
            dve.tensor_copy(running_t[:, :, :], tiles(back)).then_inc(step, 1)
            dve.wait_ge(product, 3)
            dve.tensor_copy(node_max[:, :], of_node[:, 0:ROWS]).then_inc(step, 1)
            dve.wait_ge(product, 4)
            dve.tensor_tensor(shifted[:, :, :], t.score[:, :, :], tiles(of_edge), ALU.subtract).then_inc(step, 1)
            dve.wait_ge(product, 5)
            dve.tensor_copy(node_sum[:, :], sum_node[:, 0:ROWS]).then_inc(step, 1)
            dve.wait_ge(product, 6)
            dve.reciprocal(edge_inv[:, :, :], tiles(sum_edge)).then_inc(step, 1)
            dve.wait_ge(step, 8)
            dve.tensor_tensor(t.score[:, :, :], expd[:, :, :], edge_inv[:, :, :], ALU.mult).then_inc(step, 1)

        @block.scalar
        def _(scalar):
            scalar.wait_ge(step, 6)
            scalar.activation(expd[:, :, :], shifted[:, :, :], ACT.Exp).then_inc(exp_ready, 1)

        block.__exit__(None, None, None)


def edge_sums(nc, chip, t):
    with Phase(nc, "esum") as ph:
        weighed = [ph.sb(f"weighed{e}", [P, COLS]) for e in range(ET)]
        summed = ph.sb("summed", [P, COLS])
        at_edge = [ph.bank(f"at_edge{e}") for e in range(ET)]
        sums, out = ph.bank("sums"), ph.bank("out")
        at_edge_ready = ph.sem("at_edge_ready")
        weighed_ready = ph.sem("weighed_ready")
        sums_ready = ph.sem("sums_ready")
        summed_ready = ph.sem("summed_ready")
        out_ready = ph.sem("out_ready")
        added = ph.sem("added")
        block = nc.Block()
        block.__enter__()

        @block.tensor
        def _(pe):
            def gathers(h):
                for e in range(ET):
                    if h.least:
                        pe.wait_ge(weighed_ready, h * ET - ET + e + 1)
                    pe.matmul(at_edge[e][:, :], tile_of(t.at_dst, e), group_of(t.values, h), start=True, stop=True)\
                        .then_inc(at_edge_ready, 1)

            def segment_sums(g):
                pe.wait_ge(weighed_ready, g * ET + ET)
                if g.least:
                    pe.wait_ge(summed_ready, g.n)
                for b in range(GB):
                    for e in range(ET):
                        mm = pe.matmul(tile_of(sums, b), tile_of(weighed[e], b), t.src_t[:, e, :], start=(e == 0),
                                       stop=(e == ET - 1))
                mm.then_inc(sums_ready, 1)

            def outs(g):
                pe.wait_ge(summed_ready, g + 1)
                if g.least:
                    pe.wait_ge(added, g.n)
                for b in range(GB):
                    mm = pe.matmul(tile_of(out, b), tile_of(summed, b), t.weights[:, 2 * P:3 * P], start=True, stop=True)
                mm.then_inc(out_ready, 1)

            def group(g, behind, ahead):
                segment_sums(g)
                if ahead is not None:
                    gathers(ahead)
                outs(g)

            gathers(group_number(0))
            over_groups(pe, group)

        @block.scalar
        def _(scalar):
            def group(g, behind, ahead):
                scalar.wait_ge(sums_ready, g + 1)
                if g.least:
                    scalar.wait_ge(out_ready, g.n)
                scalar.activation(summed[:, :], sums[:, :], ACT.Copy).then_inc(summed_ready, 1)

            over_groups(scalar, group)

        @block.vector
        def _(dve):
            n = GB * HEADS

            def weigh(h):
                for e in range(ET):
                    dve.wait_ge(at_edge_ready, h * ET + e + 1)
                    if h.least:
                        dve.wait_ge(sums_ready, h.n)
                    dve.tensor_tensor(weighed[e][:, :].rearrange("e (r d) -> e r d", r=n),
                                      at_edge[e][:, :].rearrange("e (r d) -> e r d", r=n),
                                      t.score[:, e, bass.ds(h * n, n)].unsqueeze(2).to_broadcast([P, n, P // HEADS]),
                                      ALU.mult).then_inc(weighed_ready, 1)

            def add(g):
                dve.wait_ge(out_ready, g + 1)
                dve.tensor_tensor(group_of(chip.x, g), group_of(chip.x, g), out[:, :], ALU.add).then_inc(added, 1)

            def group(g, behind, ahead):
                if ahead is not None:
                    weigh(ahead)
                add(g)

            weigh(group_number(0))
            over_groups(dve, group)

        block.__exit__(None, None, None)

class Chip:
    pass


def setup(nc, chip, ins, keep, x_from):
    rows_of = [("L0_b1", ins["L0_ffn_b1"].rearrange("e (t h) -> (e t) h", h=P), 32),
               ("L1_b1", ins["L1_ffn_b1"], 8),
               ("L2_b1", ins["L2_ffn_b1"].rearrange("e (t h) -> (e t) h", h=P), 32),
               ("L3_b1", ins["L3_ffn_b1"].rearrange("e (t h) -> (e t) h", h=P), 16),
               ("bih", ins["L1_gnn_bih"].rearrange("p (t h) -> (p t) h", h=P), 16),
               ("b_lin", ins["L0_gnn_b_lin"].rearrange("(a d) -> a d", a=1), 1),
               ("bg0", ins["L1_gnn_bg0"].rearrange("(a d) -> a d", a=1), 1),
               ("bhh", ins["L1_gnn_bhh"].rearrange("p (t h) -> (p t) h", h=P), 16)]
    at = {}
    n_rows = 0
    for name, _, n in rows_of:
        at[name] = n_rows
        n_rows += n
    wide_of = [("L0_b", ins["L0_gnn_b"], P), ("bg1", ins["L1_gnn_bg1"], P), ("gamma", ins["L2_ffn_gamma"], P),
               ("beta", ins["L2_ffn_beta"], P), ("L3_b", ins["L3_gnn_bias"], P), ("L0_bg", ins["L0_ffn_bg"], 8),
               ("L2_bg", ins["L2_ffn_gate_b"], 16), ("L3_bg", ins["L3_ffn_gate_b"], 8)]
    wide_at = {}
    n_wide = 0
    for name, _, n in wide_of:
        wide_at[name] = n_wide
        n_wide += n
    b2_of = [("L0", ins["L0_ffn_b2"], 8), ("L1", ins["L1_ffn_b2"], 8), ("L2", ins["L2_ffn_b2"], 16),
             ("L3", ins["L3_ffn_b2"], 8)]

    def kept(name, shape, dt=F32):
        return keep.enter_context(nc.sbuf_tensor(name, shape, dt))

    chip.ident = kept("ident", [P, P])[:, :]
    chip.ident_r = kept("ident_r", [P, P], F32R)[:, :]
    chip.ident_bf = kept("ident_bf", [P, P], BF16)
    chip.numbers = kept("numbers", [P, 16])
    chip.minus_half = kept("minus_half", [P, GB])
    chip.eps = kept("eps", [P, GB])
    chip.adj = kept("adj_rows", [P, P])
    chip.adj_t = kept("adj_t", [P, P])
    chip.columns = kept("columns", [P, n_rows])
    chip.gate_cols = kept("gate_cols", [P, 16 + 16 + 8])
    chip.lstm_bias = kept("lstm_bias", [P, 16])
    chip.wide = kept("wide", [P, n_wide])
    chip.zero_bias = kept("zero_bias", [P, 8])
    b2_tiles = [kept(f"b2_rows{n}", [P, P]) for n in range(2)]
    b2_rows = {"L0": b2_tiles[0][0:24, :], "L1": b2_tiles[0][32:56, :], "L3": b2_tiles[0][64:88, :],
               "L2": b2_tiles[1][0:48, :]}

    with Phase(nc, "setup") as ph:
        rows = ph.sb("rows", [n_rows, P])
        gate_rows = ph.sb("gate_rows", [16, P])
        wide_row = ph.sb("wide_row", [1, n_wide])
        ones = ph.sb("ones", [1, P])
        turned, gates_turned, adj_turned = ph.bank("turned"), ph.bank("gates_turned"), ph.bank("adj_turned")
        spread = [ph.bank("spread0"), ph.bank("spread1")]
        loaded = ph.sem("loaded")
        ident_zero = ph.sem("ident_zero")
        ident_step = ph.sem("ident_step")
        ones_set = ph.sem("ones_set")
        turn_done = ph.sem("turn_done")
        columns_ready = ph.sem("columns_ready")
        N_LOADS = len(rows_of) + 2 + 2 + len(wide_of) + len(b2_of) + 1

        block = nc.Block()
        block.__enter__()

        @block.sync
        def _(sp):
            for name, src, n in rows_of:
                sp.dma_start(rows[at[name]:at[name] + n, :], src).then_inc(loaded, 16)
            sp.dma_start(gate_rows[0:8, :], ins["L0_ffn_Wg"]).then_inc(loaded, 16)
            sp.dma_start(gate_rows[8:16, :], ins["L1_ffn_router_w"]).then_inc(loaded, 16)
            sp.dma_start(chip.gate_cols[:, 16:32], ins["L2_ffn_gate_w"]).then_inc(loaded, 16)
            sp.dma_start(chip.gate_cols[:, 32:40], ins["L3_ffn_gate_w"]).then_inc(loaded, 16)
            sp.dma_start(chip.adj[:, :], ins["adj"]).then_inc(loaded, 16)
            for name, src, n in wide_of:
                sp.dma_start(wide_row[:, wide_at[name]:wide_at[name] + n],
                             src.rearrange("(a d) -> a d", a=1)).then_inc(loaded, 16)
            sp.wait_ge(loaded, 16 * N_LOADS)

        @block.scalar
        def _(scalar):
            for name, src, E in b2_of:
                scalar.dma_start(b2_rows[name], src.unsqueeze(0).to_broadcast([3, E, P])).then_inc(loaded, 16)
            for c in range(4):
                graphs = slice(c * NB // 4, (c + 1) * NB // 4)
                scalar.dma_start(chip.x[:, c * NB * P // 4:(c + 1) * NB * P // 4].rearrange("n (b d) -> n b d", d=P),
                                 x_from[graphs].rearrange("b n d -> n b d")).then_inc(chip.x_loaded, 16)
            scalar.wait_ge(chip.x_loaded, 64)

        @block.gpsimd
        def _(pool):
            pool.memset(chip.ident, 0.0).then_inc(ident_zero, 1)
            pool.memset(chip.ident_bf[:, :], 0.0).then_inc(ident_zero, 1)
            pool.wait_ge(ident_zero, 2)
            for m in (chip.ident, chip.ident_bf[:, :]):
                pool.affine_select(out=m, in_=m, compare_op=ALU.not_equal, fill=1.0, base=0,
                                   pattern=[[-1, P]], channel_multiplier=1).then_inc(ident_step, 1)
            pool.wait_ge(ident_step, 1)
            pool.tensor_copy(chip.ident_r, chip.ident).then_inc(ident_step, 1)
            pool.iota(chip.numbers[:, :], [[1, 16]], base=0, channel_multiplier=0,
                      allow_small_or_imprecise_dtypes=True).then_inc(ident_step, 1)
            pool.memset(chip.minus_half[:, :], -0.5).then_inc(ident_step, 1)
            pool.memset(chip.zero_bias[:, :], 0.0).then_inc(ident_step, 1)
            pool.memset(chip.eps[:, :], EPS).then_inc(ident_step, 1)
            pool.memset(ones[:, :], 1.0).then_inc(ones_set, 1)

        @block.tensor
        def _(pe):
            pe.wait_ge(loaded, 16 * N_LOADS)
            pe.wait_ge(ident_step, 7)
            pe.wait_ge(ones_set, 1)
            pe.transpose(turned[:, 0:n_rows], rows[:, :], chip.ident[0:n_rows, 0:n_rows]).then_inc(turn_done, 1)
            pe.transpose(gates_turned[:, 0:16], gate_rows[:, :], chip.ident[0:16, 0:16]).then_inc(turn_done, 1)
            pe.transpose(adj_turned[:, 0:P], chip.adj[:, :], chip.ident).then_inc(turn_done, 1)
            pe.matmul(spread[0][:, :], ones[:, :], wide_row[:, 0:COLS], start=True, stop=True).then_inc(turn_done, 1)
            pe.matmul(spread[1][:, 0:n_wide - COLS], ones[:, :], wide_row[:, COLS:n_wide], start=True, stop=True)\
                .then_inc(turn_done, 1)

        @block.vector
        def _(dve):
            dve.wait_ge(turn_done, 5)
            dve.tensor_copy(chip.columns[:, :], turned[:, 0:n_rows]).then_inc(columns_ready, 1)
            dve.tensor_copy(chip.gate_cols[:, 0:16], gates_turned[:, 0:16])
            dve.tensor_copy(chip.adj_t[:, :], adj_turned[:, 0:P])
            dve.tensor_copy(chip.wide[:, 0:COLS], spread[0][:, :])
            dve.tensor_copy(chip.wide[:, COLS:n_wide], spread[1][:, 0:n_wide - COLS])
            dve.wait_ge(columns_ready, 1)
            dve.tensor_tensor(chip.lstm_bias[:, :], chip.columns[:, at["bih"]:at["bih"] + 16],
                              chip.columns[:, at["bhh"]:at["bhh"] + 16], ALU.add)

        block.__exit__(None, None, None)

    def table(b1, n_b1, b2, E, gates, bias):
        return {"b1": chip.columns[:, at[b1]:at[b1] + n_b1], "b2": b2_rows[b2], "gates": chip.gate_cols[:, gates:gates + E],
                "gate_bias": chip.zero_bias[:, 0:E] if bias is None else chip.wide[:, wide_at[bias]:wide_at[bias] + E]}

    chip.tables = {"L0": table("L0_b1", 32, "L0", 8, 0, "L0_bg"), "L1": table("L1_b1", 8, "L1", 8, 8, None),
                   "L2": table("L2_b1", 32, "L2", 16, 16, "L2_bg"), "L3": table("L3_b1", 16, "L3", 8, 32, "L3_bg")}
    for name in ("gamma", "beta", "L0_b", "bg1", "L3_b"):
        chip.tables["L2"][name] = chip.wide[:, wide_at[name]:wide_at[name] + P]
    chip.b_lin = chip.columns[:, at["b_lin"]:at["b_lin"] + 1]
    chip.bg0 = chip.columns[:, at["bg0"]:at["bg0"] + 1]


def load_experts(engine, chip, w1, w2, turned):
    tiles = w1.shape[0] * w1.shape[2] // P if not turned else w1.shape[0] * w1.shape[1] // P
    first = chip.raw[:, 0:tiles * P].rearrange("p (e f) -> p e f", e=w1.shape[0])
    second = chip.raw[:, tiles * P:2 * tiles * P]
    if turned:
        first = chip.raw[:, 0:tiles * P].rearrange("p (r f) -> p r f", f=P)
        engine.dma_start(first, w1.rearrange("e (t h) d -> h (e t) d", h=P)).then_inc(chip.raw_loaded, 16)
        second = second.rearrange("p (e f) -> p e f", e=w2.shape[0])
        engine.dma_start(second, w2.rearrange("e d h -> d e h")).then_inc(chip.raw_loaded, 16)
    else:
        engine.dma_start(first, w1.rearrange("e d h -> d e h")).then_inc(chip.raw_loaded, 16)
        second = second.rearrange("p (r f) -> p r f", f=P)
        engine.dma_start(second, w2.rearrange("e (t h) d -> h (e t) d", h=P)).then_inc(chip.raw_loaded, 16)


EXPERTS = {"L0": ("L0_ffn_W1", "L0_ffn_W2", 8, 4, ACT.Relu, "pair", "plain", True),
           "L1": ("L1_ffn_w1", "L1_ffn_w2", 8, 1, ACT.Gelu, "renormed", "normed", False),
           "L2": ("L2_ffn_w1", "L2_ffn_w2", 16, 2, ACT.Relu, "pair", "layernorm", False),
           "L3": ("L3_ffn_W1", "L3_ffn_W2", 8, 2, ACT.Gelu, "probs", "plain", False)}


def program(nc, ins, out, layers=("G0", "L0", "G1", "L1", "G2", "L2", "G3", "L3")):
    with ExitStack() as keep:
        chip = Chip()
        chip.x = keep.enter_context(nc.sbuf_tensor("x_all", [P, NB * P], F32))
        chip.x_loaded = keep.enter_context(nc.semaphore("x_loaded"))
        chip.raw_loaded = keep.enter_context(nc.semaphore("raw_loaded"))
        chip.stored = keep.enter_context(nc.semaphore("stored"))
        setup(nc, chip, ins, keep, ins["x"])
        graph_layers = {"G0": attention, "G1": recurrent, "G2": edges, "G3": three_hops}
        count = 0
        for name in ("0", "1", "2", "3"):
            w1, w2, E, HT, act, weighting, residual, turned = EXPERTS["L" + name]
            raw = nc.sbuf_tensor(f"raw_experts{name}", [P, 2 * E * HT * P], F32, side="right")
            chip.raw = raw.__enter__()

            def load(engine, w1=w1, w2=w2, turned=turned):
                load_experts(engine, chip, ins[w1], ins[w2], turned)

            if "G" + name in layers:
                graph_layers["G" + name](nc, chip, ins, load)
            elif "L" + name in layers:
                with nc.Block() as block:
                    @block.sync
                    def _(sp):
                        load(sp)
            if "G" + name in layers or "L" + name in layers:
                count += 32
            if "L" + name in layers:
                with ExitStack() as halves:
                    split = split_experts(nc, "split" + name, chip, halves, count, E * HT, turned)
                    raw.__exit__(None, None, None)
                    mixture(nc, "mix" + name, chip, split, chip.tables["L" + name], E, HT, act, weighting, residual)
            else:
                raw.__exit__(None, None, None)
        with nc.Block() as block:
            @block.sync
            def _(sp):
                sp.wait_ge(chip.raw_loaded, count)
                for c in range(4):
                    graphs = slice(c * NB // 4, (c + 1) * NB // 4)
                    sp.dma_start(out[graphs].rearrange("b n d -> n b d"),
                                 chip.x[:, c * NB * P // 4:(c + 1) * NB * P // 4].rearrange("n (b d) -> n b d", d=P))\
                        .then_inc(chip.stored, 16)
                sp.wait_ge(chip.stored, 64)


_INS = ['x', 'adj', 'L0_gnn_W', 'L0_gnn_b_lin', 'L0_gnn_b', 'L0_ffn_Wg', 'L0_ffn_bg', 'L0_ffn_W1', 'L0_ffn_b1',
        'L0_ffn_W2', 'L0_ffn_b2', 'L1_gnn_Wg0', 'L1_gnn_bg0', 'L1_gnn_Wg1', 'L1_gnn_bg1', 'L1_gnn_Wih',
        'L1_gnn_Whh', 'L1_gnn_bih', 'L1_gnn_bhh', 'L1_ffn_router_w', 'L1_ffn_w1', 'L1_ffn_b1', 'L1_ffn_w2',
        'L1_ffn_b2', 'L2_gnn_W_lin', 'L2_gnn_W_val', 'L2_gnn_a', 'L2_gnn_W_out', 'L2_gnn_src', 'L2_gnn_dst',
        'L2_ffn_gate_w', 'L2_ffn_gate_b', 'L2_ffn_w1', 'L2_ffn_b1', 'L2_ffn_w2', 'L2_ffn_b2', 'L2_ffn_gamma',
        'L2_ffn_beta', 'L3_gnn_W', 'L3_gnn_bias', 'L3_ffn_gate_w', 'L3_ffn_gate_b', 'L3_ffn_W1', 'L3_ffn_b1',
        'L3_ffn_W2', 'L3_ffn_b2']


def kernel(**inputs):
    import numpy as _np
    import concourse.bacc as _bacc
    from concourse import mybir as _mybir
    from concourse.bass_utils import run_bass_kernel_spmd as _run

    nc = _bacc.Bacc("TRN2", target_bir_lowering=False, num_devices=1)
    arrays, ins = {}, {}
    for name in _INS:
        a = _np.ascontiguousarray(inputs[name])
        arrays[f"in_{name}_dram"] = a
        ins[name] = nc.dram_tensor(f"in_{name}_dram", a.shape, _mybir.dt.from_np(a.dtype), kind="ExternalInput").ap()
    out = nc.dram_tensor("out_0_dram", (NB, P, P), _mybir.dt.float32, kind="ExternalOutput").ap()
    program(nc, ins, out)
    r = _run(nc, [arrays], core_ids=[0])
    return r.results[0]["out_0_dram"]
```

```python
from contextlib import ExitStack

import concourse.bass as bass
from concourse import mybir

P = 128
NB = 64
GB = 4
NG = NB // GB
COLS = GB * P
EPS = 1e-5

ALU = mybir.AluOpType
ACT = mybir.ActivationFunctionType
AX = mybir.AxisListType
F32 = mybir.dt.float32
F32R = mybir.dt.float32r
BF16 = mybir.dt.bfloat16
U32 = mybir.dt.uint32
I32 = mybir.dt.int32


class Group:

    def __init__(self, n, odd, least):
        self.n, self.odd, self.least = n, odd, least

    def __mul__(self, k):
        return self.n * k

    def __add__(self, k):
        return self.n + k

    def __sub__(self, k):
        return self.n - k

    def next(self):
        return Group(self.n + 1, 1 - self.odd, self.least + 1)

    def last(self):
        return Group(self.n - 1, 1 - self.odd, self.least - 1)


def group_number(n):
    return Group(n, n % 2, n)


def over_groups_wide(engine, group, count=NG, head=2, tail=2):
    def peeled(n):
        group(group_number(n), group_number(n - 1) if n else None, group_number(n + 1) if n < count - 1 else None)

    for n in range(head):
        peeled(n)
    with engine.Fori(0, (count - head - tail) // 2) as i:
        g = Group(i * 2 + head, 0, head)
        group(g, g.last(), g.next())
        g = g.next()
        group(g, g.last(), g.next())
    for n in range(count - tail, count):
        peeled(n)


def over_groups_ahead(engine, group, reach, count=NG):
    tail = reach + reach % 2

    def ahead_of(g, left):
        def ahead(n):
            return Group(g.n + n, (g.odd + n) % 2, g.least + n) if n <= left else None
        return ahead

    for n in range(2):
        group(group_number(n), ahead_of(group_number(n), count - 1 - n))
    with engine.Fori(0, (count - 2 - tail) // 2) as i:
        g = Group(i * 2 + 2, 0, 2)
        group(g, ahead_of(g, reach))
        g = g.next()
        group(g, ahead_of(g, reach))
    for n in range(count - tail, count):
        group(group_number(n), ahead_of(group_number(n), count - 1 - n))


def wait_apart(dve, sem, value, scratch):
    dve.wait_ge(sem, value)
    dve.memset(scratch[:, 0:1], 0.0)


def tile_of(buf, b):
    return buf[:, b * P:(b + 1) * P]


def graph_of(x, g, b):
    return x[:, bass.ds((g * GB + b) * P, P)]


def group_of(x, g):
    return x[:, bass.ds(g * COLS, COLS)]


def by_graph(ap):
    return ap.rearrange("p (b d) -> p b d", b=GB)


class Phase:

    def __init__(self, nc, tag):
        self.nc, self.tag, self.sems = nc, tag, []

    def __enter__(self):
        self.ctx = ExitStack()
        return self

    def sem(self, name):
        s = self.ctx.enter_context(self.nc.semaphore(f"{self.tag}_{name}"))
        self.sems.append(s)
        return s

    def sb(self, name, shape, dt=F32):
        return self.ctx.enter_context(self.nc.sbuf_tensor(f"{self.tag}_{name}", shape, dt))

    def bank(self, name):
        return self.ctx.enter_context(self.nc.psum_tensor(f"{self.tag}_{name}", [P, COLS], F32))

    def __exit__(self, *failed):
        if failed[0] is None:
            for s in self.sems:
                self.nc.gpsimd.sem_clear(s)
            self.nc.all_engine_barrier()
        self.ctx.close()

UPS = 2


def split_experts(nc, tag, chip, keep, raw_count, K, turned):
    high, low = (keep.enter_context(nc.sbuf_tensor(f"{tag}_{name}", [P, 2 * K * P], F32R)) for name in ("high", "low"))
    CHUNKS = 2 * K // GB
    raw = chip.raw
    with Phase(nc, tag) as ph:
        turn = [ph.bank(f"turn{i}") for i in range(4)]
        w_turned = ph.sem("w_turned")
        w_high = ph.sem("w_high")
        w_low = ph.sem("w_low")
        block = nc.Block()
        block.__enter__()

        def source(c):
            return turn[c % 4][:, :] if turned else raw[:, c * COLS:(c + 1) * COLS]

        @block.tensor
        def _(pe):
            if turned:
                pe.wait_ge(chip.raw_loaded, raw_count)
                for c in range(CHUNKS):
                    if c >= 4:
                        pe.wait_ge(w_high, c - 3)
                        pe.wait_ge(w_low, c - 3)
                    for b in range(GB):
                        mm = pe.transpose(tile_of(turn[c % 4], b), tile_of(raw[:, c * COLS:(c + 1) * COLS], b),
                                          chip.ident)
                    mm.then_inc(w_turned, 1)

        @block.scalar
        def _(scalar):
            scalar.wait_ge(chip.raw_loaded, raw_count)
            for c in range(CHUNKS):
                if turned:
                    scalar.wait_ge(w_turned, c + 1)
                scalar.activation(high[:, c * COLS:(c + 1) * COLS], source(c), ACT.Copy).then_inc(w_high, 1)

        @block.vector
        def _(dve):
            for c in range(CHUNKS):
                dve.wait_ge(w_high, c + 1)
                cols = slice(c * COLS, (c + 1) * COLS)
                dve.tensor_tensor(low[:, cols], source(c), high[:, cols].bitcast(F32), ALU.subtract)\
                    .then_inc(w_low, 1)

        block.__exit__(None, None, None)
    return high, low


def mixture(nc, tag, chip, split, tables, E, HT, act, weighting, residual, out):
    K = E * HT
    NH = 8
    SCALE, HALVES, DOWN = 1, 2, 5
    S_OUT, S_BACK, S_ADD, S_FINISH = DOWN, DOWN + 1, DOWN + 2, DOWN + 4
    if K > 8:
        S_BACK, S_ADD, S_FINISH = DOWN + 2, DOWN + 4, DOWN + 8
    U = K // 8
    if K < 32:
        LEAD = 2
        S_STATS, S_AGGREGATE, S_NORMAL = 0, U, 3 * U + U // 2
        S_TURN, S_TAKE, S_LOW, S_GATE, S_LOGITS, S_TOP, S_EXPERTS = U, 2 * U, 3 * U, 4 * U, 5 * U, 6 * U, 7 * U
        S_ROUTE, S_EXP, S_WEIGHTS, S_TAKE_WEIGHTS = (0, 2 * U, 3 * U, 4 * U, 4 * U + U // 2), U, 7 * U - 1, 8 * U - 1
    else:
        LEAD = 1
        S_STATS, S_AGGREGATE, S_NORMAL = 3, 5, 20
        S_TURN, S_TAKE, S_LOW, S_GATE, S_LOGITS, S_TOP, S_EXPERTS = 0, 1, 2, 4, 6, 7, 8
        S_ROUTE, S_EXP, S_WEIGHTS, S_TAKE_WEIGHTS = (10, 14, 16, 17, 18), 12, 24, 27
    POOLED = (1, 3, 5, 7) if K == 32 else (1, 2, 3, 5, 6, 7)
    VECTORED = () if act == ACT.Relu else tuple((S_EXP + n - HALVES) % K for n in range(2))
    NS = 4
    THIRDS = 3 * E if 3 * E <= 32 else 96
    full = weighting != "pair"
    A_END = 2 + full
    B_END = A_END + 2
    C_END = B_END + 2
    D_END = C_END + 4 * (weighting == "renormed")
    STEPS = D_END + 7
    b1 = tables["b1"]
    layernorm = residual == "layernorm"
    x = chip.x

    def lows(k, pooled):
        mine = [i for i in range(NH) if (i in POOLED) == pooled]
        return k // NH * len(mine) + sum(i < k % NH for i in mine)

    def is_pooled(k):
        return k % NH in POOLED

    high, low = split
    held = NG if LEAD == 2 else 2
    xt_low_guard = nc.sbuf_tensor(f"{tag}_xt_low", [P, held * COLS], F32R, side="right")
    xt_low = xt_low_guard.__enter__()

    def turned(buf, g):
        return group_of(buf, g) if LEAD == 2 else buf[:, g.odd * COLS:(g.odd + 1) * COLS]

    with Phase(nc, tag) as ph:
        sb, bank, sem = ph.sb, ph.bank, ph.sem
        norm = Norm(ph, chip)
        xn = norm.xn
        xt_high = sb("xt_high", [P, held * COLS], F32R)
        xt = sb("xt", [P, COLS])
        selector = sb("selector", [3 * E, E * P], BF16)
        b2s = [sb(f"b2_{n}", [3 * E, P], BF16) for n in range(3)]
        logits = sb("logits", [P, GB, E])
        top = sb("top", [P, GB, 8])
        top_at = sb("top_at", [P, GB, 8], U32)
        top_atf = sb("top_atf", [P, GB, 2])
        shifted = sb("shifted", [P, GB, 2])
        pair = sb("pair", [P, GB, 2])
        if full:
            all_shifted = sb("all_shifted", [P, GB, E])
            all_exp = sb("all_exp", [P, GB, E])
        total = sb("total", [P, GB])
        inverse = sb("inverse", [P, GB])
        hot = sb("hot", [P, GB, 2, E])
        thirds = sb("thirds", [P, GB, THIRDS], BF16)
        scratches = [sb(f"scratch{i}", [P, 1]) for i in range(4)]
        own_weights = [sb(f"own_weights{i}", [3 * E, COLS], BF16) for i in range(2)]
        hid = [sb(f"hid{i}", [P, COLS]) for i in range(NS)]
        scaled = [sb(f"scaled{i}", [P, COLS]) for i in range(NS)]
        hid_high = [sb(f"hid_high{i}", [P, COLS], F32R) for i in range(NH)]
        hid_low = [sb(f"hid_low{i}", [P, COLS], F32R) for i in range(NH)]
        out_t = sb("out_t", [P, COLS])
        b2_left = out_t[0:3 * E, 0:P]
        if layernorm:
            normed = out_t
            mix_stats = sb("mix_stats", [P, GB, 6])
            mix_moments = sb("mix_moments", [P, GB, 2])
            mix_var = sb("mix_var", [P, GB])
            mix_rstd = sb("mix_rstd", [P, GB])
        up = [bank(f"up{i}") for i in range(UPS)]
        spread = [bank(f"spread{i}") for i in range(2)]
        down = [bank(f"down{i}") for i in range(2)]
        turn = bank("turn")
        small = bank("small")

        turn_ready = sem("turn_ready")
        xt_ready = sem("xt_ready")
        xt_high_ready = sem("xt_high_ready")
        xt_low_ready = sem("xt_low_ready")
        gate_ready = sem("gate_ready")
        logits_ready = sem("logits_ready")
        top_ready = sem("top_ready")
        top_at_ready = sem("top_at_ready")
        step = sem("step")
        exp_ready = sem("exp_ready")
        thirds_clear = sem("thirds_clear")
        thirds_turned = sem("thirds_turned")
        weights_ready = sem("weights_ready")
        selector_step = sem("selector_step")
        b2_step = sem("b2_step")
        up_ready = sem("up_ready")
        hid_ready = sem("hid_ready")
        scaled_ready = sem("scaled_ready")
        high_ready = {False: sem("high_ready"), True: sem("high_ready_vector")}
        low_ready = {False: sem("low_ready"), True: sem("low_ready_pool")}
        down_ready = sem("down_ready")
        spread_ready = sem("spread_ready")
        out_ready = sem("out_ready")
        back_ready = sem("back_ready")
        added = sem("added")
        if layernorm:
            mix_step = sem("mix_step")
            mix_rstd_step = sem("mix_rstd_step")
            mix_out = sem("mix_out")

        def wait_low(engine, g, k):
            p = is_pooled(k)
            engine.wait_ge(low_ready[p], g * lows(K, p) + (lows(k, p) + 1))

        def wait_high(engine, g, k):
            vectored, before = k in VECTORED, sum(i < k for i in VECTORED)
            if vectored:
                engine.wait_ge(high_ready[True], g * len(VECTORED) + (before + 1))
            else:
                engine.wait_ge(high_ready[False], g * (K - len(VECTORED)) + (k - before + 1))

        def tiles(engine, stages, extra, prepare):
            def group(g, ahead):
                for k in range(K):
                    for stage, lag in stages:
                        if k >= lag:
                            stage(g, k - lag)
                        elif g.least:
                            stage(g.last(), K + k - lag)
                    if g.least:
                        extra(g.last(), k)
                    prepare(ahead, k)

            over_groups_ahead(engine, group, 3)
            end = group_number(NG - 1)
            for k in range(K):
                for stage, lag in stages:
                    if k < lag:
                        stage(end, K + k - lag)
                extra(end, k)

        block = nc.Block()
        block.__enter__()

        @block.sync
        def _(sp):
            def store(g, ahead):
                sp.wait_ge(added, g + 1)
                sp.dma_start(out[bass.ds(g * GB, GB)].rearrange("b n d -> n b d"),
                             group_of(x, g).rearrange("n (b d) -> n b d", d=P)).then_inc(chip.stored, 16)

            if out is not None:
                over_groups_ahead(sp, store, 0)
                sp.wait_ge(chip.stored, 16 * NG)

        @block.tensor
        def _(pe):
            def turn_tokens(h):
                pe.wait_ge(norm.xn_ready, h + 1)
                if h.least:
                    pe.wait_ge(xt_ready, h.n)
                for b in range(GB):
                    mm = pe.transpose(tile_of(turn, b), tile_of(xn[h.odd], b), chip.ident)
                mm.then_inc(turn_ready, 1)

            def gate_products(h, weights_before):
                pe.wait_ge(xt_ready, h + 1)
                if weights_before is not None:
                    pe.wait_ge(weights_ready, weights_before)
                for b in range(GB):
                    mm = pe.matmul(small[:, b * E:(b + 1) * E], tile_of(xt, b), tables["gates"], start=True, stop=True)
                mm.then_inc(gate_ready, 1)

            def turn_weights(h, logits_before):
                pe.wait_ge(step, h * STEPS + STEPS)
                pe.wait_ge(logits_ready, logits_before)
                for b in range(GB):
                    mm = pe.transpose(tile_of(small[0:THIRDS, :].bitcast(BF16), b), thirds[:, b, :], chip.ident_bf[:, :])
                mm.then_inc(thirds_turned, 1)

            def prepare(ahead, k):
                one, lead = ahead(1), ahead(LEAD)
                if lead and k == S_TURN:
                    turn_tokens(lead)
                if lead and k == S_GATE:
                    gate_products(lead, lead - (LEAD - 1))
                if one and k == S_WEIGHTS:
                    turn_weights(one, one + LEAD if lead else NG)

            def first_product(g, k):
                if k >= UPS or g.least:
                    pe.wait_ge(hid_ready, g * K + (k - UPS + 1))
                if k == 0:
                    pe.wait_ge(xt_low_ready, g + 1)
                w = slice(k * P, (k + 1) * P)
                bank = up[k % UPS][:, :]
                pe.matmul(bank, high[:, w], turned(xt_high, g), start=True, stop=False)
                pe.matmul(bank, high[:, w], turned(xt_low, g), start=False, stop=False)
                pe.matmul(bank, low[:, w], turned(xt_high, g), start=False, stop=True).then_inc(up_ready, 1)
                if k == 0:
                    pe.wait_ge(weights_ready, g + 1)
                if k % HT == 0:
                    e = k // HT
                    if e >= 2 or g.least:
                        pe.wait_ge(scaled_ready, (g * E + (e - 1)) * HT)
                    pe.matmul(spread[e % 2][:, :], selector[:, e * P:(e + 1) * P], own_weights[g.odd][:, :],
                              start=True, stop=True).then_inc(spread_ready, 1)

            def second_product(g, k):
                bank = down[g.odd][:, :]
                if k == 0:
                    if g.least >= 2:
                        pe.wait_ge(added, g - 1)
                    for n in range(3):
                        pe.matmul(bank, b2s[n][:, :], own_weights[g.odd][:, :], start=(n == 0), stop=False)
                    if residual != "plain":
                        pe.matmul(bank, chip.ident_r, turned(xt_high, g), start=False, stop=False)
                        pe.matmul(bank, chip.ident_r, turned(xt_low, g), start=False, stop=False)
                wait_low(pe, g, k)
                w = slice((K + k) * P, (K + k + 1) * P)
                n = k % NH
                pe.matmul(bank, high[:, w], hid_high[n][:, :], start=False, stop=False)
                pe.matmul(bank, high[:, w], hid_low[n][:, :], start=False, stop=False)
                pe.matmul(bank, low[:, w], hid_high[n][:, :], start=False, stop=(k == K - 1))\
                    .then_inc(down_ready, 1)

            def turn_back(g, k):
                if k == S_BACK:
                    pe.wait_ge(out_ready, g + 1)
                    for b in range(GB):
                        mm = pe.transpose(tile_of(down[g.odd], b), tile_of(out_t, b), chip.ident)
                    mm.then_inc(back_ready, 1)

            first, second = group_number(0), group_number(1)
            turn_tokens(first)
            gate_products(first, None)
            if LEAD == 2:
                turn_tokens(second)
            turn_weights(first, 1)
            if LEAD == 2:
                gate_products(second, 1)
            pe.wait_ge(selector_step, 4)
            pe.wait_ge(b2_step, 6)
            tiles(pe, ((first_product, 0), (second_product, DOWN)), turn_back, prepare)

        @block.scalar
        def _(scalar):
            def high_tokens(h):
                scalar.wait_ge(xt_ready, h + 1)
                if h.least >= 2 and LEAD == 1:
                    scalar.wait_ge(up_ready, (h - 1) * K)
                    scalar.wait_ge(down_ready, (h - 2) * K + 1)
                    scalar.wait_ge(xt_low_ready, h - 1)
                scalar.activation(turned(xt_high, h), xt[:, :], ACT.Copy).then_inc(xt_high_ready, 1)

            def exponentials(h):
                scalar.wait_ge(step, h * STEPS + A_END)
                if full:
                    scalar.activation(all_exp[:, :, :], all_shifted[:, :, :], ACT.Exp)
                scalar.activation(pair[:, :, :], shifted[:, :, :], ACT.Exp).then_inc(exp_ready, 1)

            def take_weights(h):
                scalar.wait_ge(thirds_turned, h + 1)
                if h.least >= 2:
                    scalar.wait_ge(spread_ready, (h - 1) * E)
                    scalar.wait_ge(down_ready, (h - 2) * K + 1)
                scalar.activation(own_weights[h.odd][:, :], small[0:3 * E, :].bitcast(BF16)[:, 0:COLS], ACT.Copy)\
                    .then_inc(weights_ready, 1)

            def prepare(ahead, k):
                one, lead = ahead(1), ahead(LEAD)
                if one and k == S_EXP:
                    exponentials(one)
                if lead and k == S_TAKE:
                    high_tokens(lead)
                if one and k == S_TAKE_WEIGHTS:
                    take_weights(one)

            def high_half(g, k):
                if k in VECTORED:
                    return
                scalar.wait_ge(scaled_ready, g * K + (k + 1))
                if k >= NH or g.least:
                    scalar.wait_ge(down_ready, g * K + (k - NH + 1))
                scalar.activation(hid_high[k % NH][:, :], scaled[k % NS][:, :], ACT.Copy).then_inc(high_ready[False], 1)

            def activate(g, k):
                scalar.wait_ge(up_ready, g * K + (k + 1))
                if k >= NS or g.least:
                    scalar.wait_ge(scaled_ready, g * K + (k - NS + 1))
                scalar.activation(hid[k % NS][:, :], up[k % UPS][:, :], act, bias=b1[:, k:k + 1])\
                    .then_inc(hid_ready, 1)

            def take_out(g, k):
                if k == S_OUT:
                    scalar.wait_ge(down_ready, g * K + K)
                    if g.least:
                        scalar.wait_ge(back_ready, g.n)
                        if layernorm:
                            scalar.wait_ge(mix_out, g * 3)
                    scalar.activation(out_t[:, :], down[g.odd][:, :], ACT.Copy).then_inc(out_ready, 1)

            first, second = group_number(0), group_number(1)
            high_tokens(first)
            exponentials(first)
            take_weights(first)
            if LEAD == 2:
                high_tokens(second)
            scalar.wait_ge(b2_step, 6)
            tiles(scalar, ((high_half, HALVES), (activate, 0)), take_out, prepare)

        @block.vector
        def _(dve):
            def split_b2():
                dve.tensor_copy(b2_left, tables["b2"]).then_inc(b2_step, 1)
                dve.wait_ge(b2_step, 1)
                for n in range(3):
                    dve.tensor_copy(b2s[n][:, :], b2_left).then_inc(b2_step, 1)
                    dve.wait_ge(b2_step, 2 * n + 2)
                    if n < 2:
                        dve.tensor_tensor(b2_left, b2_left, b2s[n][:, :], ALU.subtract).then_inc(b2_step, 1)
                        dve.wait_ge(b2_step, 2 * n + 3)

            def normalise(h):
                if h.least >= 2:
                    dve.wait_ge(turn_ready, h - 1)
                norm.normalise(dve, h)

            def take_plain(h):
                dve.wait_ge(turn_ready, h + 1)
                if h.least:
                    dve.wait_ge(gate_ready, h.n)
                    dve.wait_ge(xt_low_ready, h.n)
                dve.tensor_copy(xt[:, :], turn[:, :]).then_inc(xt_ready, 1)

            def take_logits(h):
                dve.wait_ge(gate_ready, h + 1)
                if h.least:
                    dve.wait_ge(step, (h - 1) * STEPS + A_END)
                dve.tensor_tensor(logits[:, :, :], small[:, 0:GB * E].rearrange("p (b e) -> p b e", b=GB),
                                  tables["gate_bias"].unsqueeze(1).to_broadcast([P, GB, E]), ALU.add)\
                    .then_inc(logits_ready, 1)

            def largest(h):
                wait_apart(dve, logits_ready, h + 1, scratches[0])
                for b in range(GB):
                    op = dve.max(top[:, b, :], logits[:, b, :])
                op.then_inc(top_ready, 1)

            def experts_of(h):
                wait_apart(dve, top_ready, h + 1, scratches[1])
                for b in range(GB):
                    op = dve.max_index(top_at[:, b, :], top[:, b, :], logits[:, b, :])
                op.then_inc(top_at_ready, 1)

            def over_pair(ap):
                return ap.unsqueeze(2).to_broadcast([P, GB, 2])

            def route(h, part):
                at = [{0: 0, 1: A_END, 2: B_END, 3: C_END, 4: D_END}[part]]

                def then(op):
                    op.then_inc(step, 1)
                    at[0] += 1

                def wait_steps():
                    dve.wait_ge(step, h * STEPS + at[0])

                if part == 0:
                    dve.wait_ge(top_at_ready, h + 1)
                    if h.least:
                        dve.wait_ge(step, h * STEPS)
                    then(dve.tensor_copy(top_atf[:, :, :], top_at[:, :, 0:2]))
                    if h.least:
                        dve.wait_ge(exp_ready, h.n)
                    if full:
                        then(dve.tensor_tensor(all_shifted[:, :, :], logits[:, :, :],
                                               top[:, :, 0:1].to_broadcast([P, GB, E]), ALU.subtract))
                    then(dve.tensor_tensor(shifted[:, :, :], top[:, :, 0:2],
                                           top[:, :, 0:1].to_broadcast([P, GB, 2]), ALU.subtract))
                if part == 1:
                    dve.wait_ge(exp_ready, h + 1)
                    then(dve.reduce_sum(total[:, :], (all_exp if full else pair)[:, :, :], AX.X))
                    wait_steps()
                    then(dve.reciprocal(inverse[:, :], total[:, :]))
                if part == 2:
                    wait_steps()
                    then(dve.tensor_tensor(pair[:, :, :], pair[:, :, :], over_pair(inverse[:, :]), ALU.mult))
                    then(dve.tensor_tensor(hot[:, :, :, :],
                                           chip.numbers[:, 0:E].unsqueeze(1).unsqueeze(1).to_broadcast([P, GB, 2, E]),
                                           top_atf[:, :, :].unsqueeze(3).to_broadcast([P, GB, 2, E]), ALU.is_equal))
                if part == 3 and weighting == "renormed":
                    wait_steps()
                    then(dve.reduce_sum(total[:, :], pair[:, :, :], AX.X))
                    wait_steps()
                    then(dve.tensor_scalar(total[:, :], total[:, :], 1e-12, None, ALU.max))
                    wait_steps()
                    then(dve.reciprocal(inverse[:, :], total[:, :]))
                    wait_steps()
                    then(dve.tensor_tensor(pair[:, :, :], pair[:, :, :], over_pair(inverse[:, :]), ALU.mult))
                if part == 4:
                    wait_steps()
                    then(dve.tensor_tensor(hot[:, :, :, :], hot[:, :, :, :],
                                           pair[:, :, :].unsqueeze(3).to_broadcast([P, GB, 2, E]), ALU.mult))
                    wait_steps()
                    left = hot[:, :, 0, :]
                    then(dve.tensor_tensor(left, left, hot[:, :, 1, :], ALU.add))
                    if h.least:
                        dve.wait_ge(thirds_turned, h.n)
                    for n in range(3):
                        third = thirds[:, :, n * E:(n + 1) * E]
                        wait_steps()
                        then(dve.tensor_copy(third, left))
                        if n < 2:
                            wait_steps()
                            then(dve.tensor_tensor(left, left, third, ALU.subtract))

            def prepare(ahead, k):
                one, lead, three = ahead(1), ahead(LEAD), ahead(3)
                if three and k == S_STATS:
                    norm.statistics(dve, three)
                if three and k == S_AGGREGATE:
                    norm.aggregate(dve, three)
                if three and k == S_NORMAL:
                    normalise(three)
                for part in range(5):
                    if one and k == S_ROUTE[part]:
                        route(one, part)
                if lead and k == S_TAKE:
                    take_plain(lead)
                if lead and k == S_LOGITS:
                    take_logits(lead)
                if lead and k == S_TOP:
                    largest(lead)
                if lead and k == S_EXPERTS:
                    experts_of(lead)

            def scale(g, k):
                dve.wait_ge(hid_ready, g * K + (k + 1))
                if k % HT == 0:
                    dve.wait_ge(spread_ready, g * E + (k // HT + 1))
                if k >= NS or g.least:
                    wait_low(dve, g, k - NS)
                dve.tensor_tensor(scaled[k % NS][:, :], hid[k % NS][:, :], spread[k // HT % 2][:, :], ALU.mult)\
                    .then_inc(scaled_ready, 1)

            def high_half(g, k):
                if k not in VECTORED:
                    return
                dve.wait_ge(scaled_ready, g * K + (k + 1))
                if k >= NH or g.least:
                    dve.wait_ge(down_ready, g * K + (k - NH + 1))
                dve.tensor_copy(hid_high[k % NH][:, :], scaled[k % NS][:, :]).then_inc(high_ready[True], 1)

            def low_half(g, k):
                if is_pooled(k):
                    return
                wait_high(dve, g, k)
                if k >= NH or g.least:
                    dve.wait_ge(down_ready, g * K + (k - NH + 1))
                dve.tensor_tensor(hid_low[k % NH][:, :], scaled[k % NS][:, :], hid_high[k % NH][:, :].bitcast(F32),
                                  ALU.subtract).then_inc(low_ready[False], 1)

            def add_out(g, k):
                if k == S_ADD and not layernorm:
                    dve.wait_ge(back_ready, g + 1)
                    dve.tensor_tensor(group_of(x, g), group_of(x, g), down[g.odd][:, :], ALU.add).then_inc(added, 1)
                if k == S_ADD and layernorm:
                    if g.least:
                        dve.wait_ge(mix_rstd_step, g * 2)
                    wait_apart(dve, back_ready, g + 1, scratches[2])
                    for b in range(GB):
                        op = dve.bn_stats(mix_stats[:, b, :], tile_of(down[g.odd], b))
                    op.then_inc(mix_step, 1)
                    wait_apart(dve, mix_step, g * 2 + 1, scratches[3])
                    for b in range(GB):
                        op = dve.bn_aggr(mix_moments[:, b, :], mix_stats[:, b, :])
                    op.then_inc(mix_step, 1)
                if k == S_FINISH and layernorm:
                    dve.wait_ge(mix_rstd_step, g * 2 + 2)
                    for b in range(GB):
                        op = dve.tensor_scalar(tile_of(normed, b), tile_of(down[g.odd], b),
                                               mix_moments[:, b, 0:1], mix_rstd[:, b:b + 1], ALU.subtract, ALU.mult)
                    op.then_inc(added, 1)

            first, second, third = (group_number(n) for n in range(3))
            norm.moments(dve, first)
            norm.moments(dve, second)
            normalise(first)
            normalise(second)
            take_plain(first)
            split_b2()
            take_logits(first)
            largest(first)
            experts_of(first)
            dve.wait_ge(thirds_clear, 1)
            route(first, 0)
            norm.moments(dve, third)
            for part in range(1, 5):
                route(first, part)
            normalise(third)
            if LEAD == 2:
                take_plain(second)
                take_logits(second)
                largest(second)
                experts_of(second)
            tiles(dve, ((scale, SCALE), (high_half, HALVES), (low_half, HALVES)), add_out, prepare)

        @block.gpsimd
        def _(pool):
            def low_tokens(h):
                pool.wait_ge(xt_high_ready, h + 1)
                pool.tensor_tensor(turned(xt_low, h), xt[:, :], turned(xt_high, h).bitcast(F32),
                                   ALU.subtract).then_inc(xt_low_ready, 1)

            def prepare(ahead, k):
                if ahead(3) and k == S_AGGREGATE:
                    norm.deviation(pool, ahead(3))
                if ahead(LEAD) and k == S_LOW:
                    low_tokens(ahead(LEAD))

            def low_half(g, k):
                if not is_pooled(k):
                    return
                wait_high(pool, g, k)
                if k >= NH or g.least:
                    pool.wait_ge(down_ready, g * K + (k - NH + 1))
                pool.tensor_tensor(hid_low[k % NH][:, :], scaled[k % NS][:, :], hid_high[k % NH][:, :].bitcast(F32),
                                   ALU.subtract).then_inc(low_ready[True], 1)

            def outer_norm(g, k):
                if not layernorm:
                    return
                wide = by_graph(normed[:, :])
                if k == S_ADD + 1:
                    if g.least:
                        pool.wait_ge(added, g.n)
                    pool.wait_ge(mix_step, g * 2 + 2)
                    pool.tensor_tensor(mix_var[:, :], mix_moments[:, :, 1], chip.eps[:, :], ALU.add)\
                        .then_inc(mix_rstd_step, 1)
                    pool.wait_ge(mix_rstd_step, g * 2 + 1)
                    pool.tensor_tensor(mix_rstd[:, :], mix_var[:, :], chip.minus_half[:, :], ALU.pow)\
                        .then_inc(mix_rstd_step, 1)
                if k == S_FINISH + 1:
                    pool.wait_ge(added, g + 1)
                    pool.tensor_tensor(wide, wide, tables["gamma"].unsqueeze(1).to_broadcast([P, GB, P]),
                                       ALU.mult).then_inc(mix_out, 1)
                if k == S_FINISH + 5:
                    pool.wait_ge(mix_out, g * 3 + 1)
                    pool.tensor_tensor(wide, wide, tables["beta"].unsqueeze(1).to_broadcast([P, GB, P]),
                                       ALU.add).then_inc(mix_out, 1)
                if k == S_FINISH + 9:
                    pool.wait_ge(mix_out, g * 3 + 2)
                    xg = group_of(x, g)
                    pool.tensor_tensor(xg, xg, normed[:, :], ALU.add).then_inc(mix_out, 1)

            first, second, third = (group_number(n) for n in range(3))
            norm.deviation(pool, first)
            norm.deviation(pool, second)
            pool.memset(thirds[:, :, :], 0.0).then_inc(thirds_clear, 1)
            pool.memset(selector[:, :], 0.0).then_inc(selector_step, 1)
            rows = selector[:, :].rearrange("r (e p) -> r e p", p=P)
            for n in range(3):
                pool.wait_ge(selector_step, n + 1)
                pool.affine_select(out=rows, in_=rows, compare_op=ALU.not_equal, fill=1.0, base=-n * E,
                                   pattern=[[-1, E], [0, P]], channel_multiplier=1).then_inc(selector_step, 1)
            low_tokens(first)
            norm.deviation(pool, third)
            if LEAD == 2:
                low_tokens(second)
            tiles(pool, ((low_half, HALVES),), outer_norm, prepare)

        block.__exit__(None, None, None)
    xt_low_guard.__exit__(None, None, None)
class Norm:

    def __init__(self, ph, chip):
        self.x, self.minus_half, self.eps = chip.x, chip.minus_half, chip.eps
        self.scratch = ph.sb("scratch", [P, 1])
        self.stats, self.means, self.var_eps, self.rstd, self.xn = (
            [ph.sb(f"{name}{i}", shape) for i in range(2)] for name, shape in (
                ("stats", [P, GB, 6]), ("means", [P, GB, 2]), ("var_eps", [P, GB]), ("rstd", [P, GB]),
                ("xn", [P, COLS])))
        self.stats_step = ph.sem("stats_step")
        self.rstd_step = ph.sem("rstd_step")
        self.xn_ready = ph.sem("xn_ready")

    def moments(self, dve, h):
        self.statistics(dve, h)
        self.aggregate(dve, h)

    def statistics(self, dve, h):
        if h.least >= 2:
            dve.wait_ge(self.xn_ready, h - 1)
        for b in range(GB):
            op = dve.bn_stats(self.stats[h.odd][:, b, :], graph_of(self.x, h, b))
        op.then_inc(self.stats_step, 1)

    def aggregate(self, dve, h):
        stats, means = self.stats[h.odd], self.means[h.odd]
        wait_apart(dve, self.stats_step, h * 2 + 1, self.scratch)
        for b in range(GB):
            op = dve.bn_aggr(means[:, b, :], stats[:, b, :])
        op.then_inc(self.stats_step, 1)

    def deviation(self, pool, h):
        if h.least >= 2:
            pool.wait_ge(self.xn_ready, h - 1)
        pool.wait_ge(self.stats_step, h * 2 + 2)
        var_eps, rstd = self.var_eps[h.odd], self.rstd[h.odd]
        pool.tensor_tensor(var_eps[:, :], self.means[h.odd][:, :, 1], self.eps[:, :], ALU.add)\
            .then_inc(self.rstd_step, 1)
        pool.wait_ge(self.rstd_step, h * 2 + 1)
        pool.tensor_tensor(rstd[:, :], var_eps[:, :], self.minus_half[:, :], ALU.pow)\
            .then_inc(self.rstd_step, 1)

    def normalise(self, dve, h):
        dve.wait_ge(self.rstd_step, h * 2 + 2)
        for b in range(GB):
            op = dve.tensor_scalar(tile_of(self.xn[h.odd], b), graph_of(self.x, h, b), self.means[h.odd][:, b, 0:1],
                                   self.rstd[h.odd][:, b:b + 1], ALU.subtract, ALU.mult)
        op.then_inc(self.xn_ready, 1)


NEVER = -1e16


def attention(nc, chip, ins, load_next):
    with Phase(nc, "att") as ph:
        norm = Norm(ph, chip)
        x, xn = chip.x, norm.xn
        weight = ph.sb("weight", [P, P])
        xt = ph.sb("xt", [P, COLS])
        ht = [ph.sb(f"ht{i}", [P, COLS]) for i in range(2)]
        hn = [ph.sb(f"hn{i}", [P, COLS]) for i in range(2)]
        product = ph.sb("product", [P, COLS])
        barred = ph.sb("barred", [P, COLS])
        score = [ph.sb(f"score{i}", [P, COLS]) for i in range(2)]
        minus_max = [ph.sb(f"minus_max{i}", [P, GB]) for i in range(2)]
        prob = ph.sb("prob", [P, COLS])
        total = ph.sb("total", [P, GB])
        inverse = ph.sb("inverse", [P, GB])
        prob_t = ph.sb("prob_t", [P, COLS])
        turn, project, turn_h, scores, turn_p, mix = (ph.bank(n) for n in
                                                      ("turn", "project", "turn_h", "scores", "turn_p", "mix"))
        loaded = ph.sem("loaded")
        turn_ready = ph.sem("turn_ready")
        xt_ready = ph.sem("xt_ready")
        project_ready = ph.sem("project_ready")
        ht_ready = ph.sem("ht_ready")
        turn_h_ready = ph.sem("turn_h_ready")
        hn_ready = ph.sem("hn_ready")
        scores_ready = ph.sem("scores_ready")
        mask_step = ph.sem("mask_step")
        score_ready = ph.sem("score_ready")
        prob_ready = ph.sem("prob_ready")
        turn_p_ready = ph.sem("turn_p_ready")
        prob_t_ready = ph.sem("prob_t_ready")
        mix_ready = ph.sem("mix_ready")
        inverse_ready = ph.sem("inverse_ready")
        added = ph.sem("added")
        bias_added = ph.sem("bias_added")
        block = nc.Block()
        block.__enter__()

        @block.sync
        def _(sp):
            sp.dma_start(weight[:, :], ins["L0_gnn_W"]).then_inc(loaded, 16)
            load_next(sp)

        @block.tensor
        def _(pe):
            def turn_tokens(h):
                pe.wait_ge(norm.xn_ready, h + 1)
                if h.least:
                    pe.wait_ge(xt_ready, h.n)
                for b in range(GB):
                    mm = pe.transpose(tile_of(turn, b), tile_of(xn[h.odd], b), chip.ident)
                mm.then_inc(turn_ready, 1)

            def projection(h):
                pe.wait_ge(xt_ready, h + 1)
                if h.least:
                    pe.wait_ge(ht_ready, h.n)
                pe.matmul(project[:, :], weight[:, :], xt[:, :], start=True, stop=True).then_inc(project_ready, 1)

            def h_and_scores(h):
                pe.wait_ge(ht_ready, h + 1)
                if h.least:
                    pe.wait_ge(hn_ready, h.n)
                for b in range(GB):
                    mm = pe.transpose(tile_of(turn_h, b), tile_of(ht[h.odd], b), chip.ident)
                mm.then_inc(turn_h_ready, 1)
                if h.least:
                    pe.wait_ge(mask_step, h * 3 - 2)
                for b in range(GB):
                    hb = tile_of(ht[h.odd], b)
                    mm = pe.matmul(tile_of(scores, b), hb, hb, start=True, stop=True)
                mm.then_inc(scores_ready, 1)

            def turn_probs(g):
                pe.wait_ge(prob_ready, g + 1)
                if g.least:
                    pe.wait_ge(prob_t_ready, g.n)
                for b in range(GB):
                    mm = pe.transpose(tile_of(turn_p, b), tile_of(prob, b), chip.ident)
                mm.then_inc(turn_p_ready, 1)

            def mixture_of_h(g):
                pe.wait_ge(prob_t_ready, g + 1)
                pe.wait_ge(hn_ready, g + 1)
                if g.least:
                    pe.wait_ge(added, g.n)
                for b in range(GB):
                    mm = pe.matmul(tile_of(mix, b), tile_of(prob_t, b), tile_of(hn[g.odd], b), start=True, stop=True)
                mm.then_inc(mix_ready, 1)

            def group(g, ahead):
                one, two = ahead(1), ahead(2)
                if two:
                    turn_tokens(two)
                turn_probs(g)
                if one:
                    h_and_scores(one)
                if two:
                    projection(two)
                mixture_of_h(g)

            pe.wait_ge(loaded, 16)
            for n in range(2):
                turn_tokens(group_number(n))
                projection(group_number(n))
            h_and_scores(group_number(0))
            over_groups_ahead(pe, group, 2)

        @block.scalar
        def _(scalar):
            def take_turned(h):
                scalar.wait_ge(turn_ready, h + 1)
                if h.least:
                    scalar.wait_ge(project_ready, h.n)
                scalar.activation(xt[:, :], turn[:, :], ACT.Copy).then_inc(xt_ready, 1)

            def take_h(h):
                scalar.wait_ge(project_ready, h + 1)
                if h.least >= 2:
                    scalar.wait_ge(scores_ready, h - 1)
                scalar.activation(ht[h.odd][:, :], project[:, :], ACT.Identity, bias=chip.b_lin).then_inc(ht_ready, 1)

            def take_turned_h(h):
                scalar.wait_ge(turn_h_ready, h + 1)
                if h.least >= 2:
                    scalar.wait_ge(mix_ready, h - 1)
                scalar.activation(hn[h.odd][:, :], turn_h[:, :], ACT.Copy).then_inc(hn_ready, 1)

            def exponentials(g):
                scalar.wait_ge(mask_step, g * 3 + 3)
                if g.least:
                    scalar.wait_ge(turn_p_ready, g.n)
                    scalar.wait_ge(inverse_ready, g.n)
                for b in range(GB):
                    op = scalar.activation(tile_of(prob, b), tile_of(score[g.odd], b), ACT.Exp,
                                           bias=minus_max[g.odd][:, b:b + 1], accum_out=total[:, b:b + 1])
                op.then_inc(prob_ready, 1)

            def take_probs(g):
                scalar.wait_ge(turn_p_ready, g + 1)
                if g.least:
                    scalar.wait_ge(mix_ready, g.n)
                scalar.activation(prob_t[:, :], turn_p[:, :], ACT.Copy).then_inc(prob_t_ready, 1)

            def group(g, ahead):
                one, two = ahead(1), ahead(2)
                exponentials(g)
                if two:
                    take_turned(two)
                take_probs(g)
                if one:
                    take_turned_h(one)
                if two:
                    take_h(two)

            for n in range(2):
                take_turned(group_number(n))
                take_h(group_number(n))
            take_turned_h(group_number(0))
            over_groups_ahead(scalar, group, 2)

        @block.vector
        def _(dve):
            every_graph = chip.adj[:, :].unsqueeze(1).to_broadcast([P, GB, P])

            def mask(h):
                dve.wait_ge(scores_ready, h + 1)
                if h.least:
                    dve.wait_ge(score_ready, h.n)
                dve.tensor_tensor(by_graph(product[:, :]), by_graph(scores[:, :]), every_graph, ALU.mult)\
                    .then_inc(mask_step, 1)
                dve.wait_ge(mask_step, h * 3 + 1)
                dve.tensor_scalar(barred[:, :], product[:, :], 0.0, NEVER, ALU.is_equal, ALU.mult)\
                    .then_inc(mask_step, 1)

            def maximum(h):
                dve.wait_ge(score_ready, h + 1)
                if h.least >= 2:
                    dve.wait_ge(prob_ready, h - 1)
                dve.tensor_reduce(minus_max[h.odd][:, :], by_graph(score[h.odd][:, :]), AX.X, ALU.max, negate=True)\
                    .then_inc(mask_step, 1)

            def add(g):
                dve.wait_ge(prob_ready, g + 1)
                if g.least:
                    dve.wait_ge(added, g.n)
                dve.reciprocal(inverse[:, :], total[:, :]).then_inc(inverse_ready, 1)
                dve.wait_ge(inverse_ready, g + 1)
                dve.wait_ge(mix_ready, g + 1)
                dve.wait_ge(bias_added, g + 1)
                for b in range(GB):
                    xb = graph_of(x, g, b)
                    op = dve.scalar_tensor_tensor(out=xb, in0=tile_of(mix, b), scalar=inverse[:, b:b + 1], in1=xb,
                                                  op0=ALU.mult, op1=ALU.add)
                op.then_inc(added, 1)

            def normalise(h):
                if h.least >= 2:
                    dve.wait_ge(turn_ready, h - 1)
                norm.normalise(dve, h)

            def group(g, ahead):
                one, three = ahead(1), ahead(3)
                if three:
                    norm.moments(dve, three)
                if one:
                    mask(one)
                if three:
                    normalise(three)
                if one:
                    maximum(one)
                add(g)

            for n in range(3):
                norm.moments(dve, group_number(n))
                normalise(group_number(n))
            mask(group_number(0))
            maximum(group_number(0))
            over_groups_ahead(dve, group, 3)

        @block.gpsimd
        def _(pool):
            def bias(g):
                pool.wait_ge(norm.xn_ready, g + 1)
                pool.tensor_tensor(by_graph(group_of(x, g)), by_graph(group_of(x, g)),
                                   chip.tables["L2"]["L0_b"].unsqueeze(1).to_broadcast([P, GB, P]), ALU.add)\
                    .then_inc(bias_added, 1)

            def bar(h):
                pool.wait_ge(mask_step, h * 3 + 2)
                if h.least >= 2:
                    pool.wait_ge(prob_ready, h - 1)
                pool.tensor_tensor(score[h.odd][:, :], product[:, :], barred[:, :], ALU.add).then_inc(score_ready, 1)

            def group(g, ahead):
                if ahead(3):
                    norm.deviation(pool, ahead(3))
                if ahead(1):
                    bar(ahead(1))
                bias(g)

            for n in range(3):
                norm.deviation(pool, group_number(n))
            bar(group_number(0))
            over_groups_ahead(pool, group, 3)

        block.__exit__(None, None, None)


def three_hops(nc, chip, ins, load_next):
    with Phase(nc, "hops") as ph:
        norm = Norm(ph, chip)
        x, xn = chip.x, norm.xn
        weight = ph.sb("weight", [P, 3 * P])
        parts = ph.sb("parts", [P, 3 * P])
        near = [[ph.sb(f"near{i}_{b}", [P, 3 * P]) for b in range(GB)] for i in range(2)]
        gather = [ph.bank(f"gather{b}") for b in range(GB)]
        out = [ph.bank(f"out{i}") for i in range(2)]
        loaded = ph.sem("loaded")
        parts_step = ph.sem("parts_step")
        gather_ready = ph.sem("gather_ready")
        near_ready = ph.sem("near_ready")
        near_ready_v = ph.sem("near_ready_v")
        out_ready = ph.sem("out_ready")
        added = ph.sem("added")
        bias_added = ph.sem("bias_added")
        block = nc.Block()
        block.__enter__()

        @block.sync
        def _(sp):
            sp.dma_start(weight[:, :].rearrange("f (k o) -> f k o", k=3), ins["L3_gnn_W"].rearrange("k f o -> f k o"))\
                .then_inc(loaded, 16)
            load_next(sp)

        @block.tensor
        def _(pe):
            def gathers(h):
                pe.wait_ge(norm.xn_ready, h + 1)
                for b in range(GB):
                    if h.least:
                        pe.wait_ge(near_ready_v if b % 2 else near_ready, h * 2 + b // 2 - 1)
                    pe.matmul(gather[b][:, 0:3 * P], tile_of(xn[h.odd], b), parts[:, :], start=True, stop=True)\
                        .then_inc(gather_ready, 1)

            def outs(g):
                if g.least >= 2:
                    pe.wait_ge(added, g - 1)
                for b in range(GB):
                    pe.wait_ge(near_ready_v if b % 2 else near_ready, g * 2 + b // 2 + 1)
                    for k in range(3):
                        mm = pe.matmul(tile_of(out[g.odd], b), near[g.odd][b][:, k * P:(k + 1) * P],
                                       weight[:, k * P:(k + 1) * P], start=(k == 0), stop=(k == 2))
                    mm.then_inc(out_ready, 1)

            def group(g, ahead):
                if ahead(1):
                    gathers(ahead(1))
                outs(g)

            pe.wait_ge(loaded, 16)
            pe.wait_ge(parts_step, 3)
            gathers(group_number(0))
            over_groups_ahead(pe, group, 1)

        def take(engine, copy, done, g, b):
            engine.wait_ge(gather_ready, g * GB + b + 1)
            if g.least >= 2:
                engine.wait_ge(out_ready, (g - 2) * GB + (b + 1))
            copy(near[g.odd][b][:, :], gather[b][:, 0:3 * P]).then_inc(done, 1)

        @block.scalar
        def _(scalar):
            def group(g, ahead):
                for b in (0, 2):
                    take(scalar, lambda o, i: scalar.activation(o, i, ACT.Copy), near_ready, g, b)

            over_groups_ahead(scalar, group, 0)

        @block.vector
        def _(dve):
            def normalise(h):
                if h.least >= 2:
                    dve.wait_ge(gather_ready, h * GB - GB)
                norm.normalise(dve, h)

            def add(g):
                dve.wait_ge(out_ready, g * GB + GB)
                dve.wait_ge(bias_added, g + 1)
                dve.tensor_tensor(group_of(x, g), group_of(x, g), out[g.odd][:, :], ALU.add).then_inc(added, 1)

            def group(g, ahead):
                two = ahead(2)
                if two:
                    norm.moments(dve, two)
                for b in (1, 3):
                    take(dve, dve.tensor_copy, near_ready_v, g, b)
                if two:
                    normalise(two)
                if g.least:
                    add(g.last())

            for n in range(2):
                norm.moments(dve, group_number(n))
                normalise(group_number(n))
            over_groups_ahead(dve, group, 2)
            add(group_number(NG - 1))

        @block.gpsimd
        def _(pool):
            done = 0
            for k, compare, sign in ((0, ALU.is_equal, 1), (1, ALU.is_gt, 1), (2, ALU.is_gt, -1)):
                pool.affine_select(out=parts[:, k * P:(k + 1) * P], in_=chip.adj_t[:, :], compare_op=compare, fill=0.0,
                                   base=0, pattern=[[-sign, P]], channel_multiplier=sign).then_inc(parts_step, 1)

            def bias(g):
                pool.wait_ge(norm.xn_ready, g + 1)
                pool.tensor_tensor(by_graph(group_of(x, g)), by_graph(group_of(x, g)),
                                   chip.tables["L2"]["L3_b"].unsqueeze(1).to_broadcast([P, GB, P]), ALU.add)\
                    .then_inc(bias_added, 1)

            def group(g, ahead):
                if ahead(2):
                    norm.deviation(pool, ahead(2))
                bias(g)

            for n in range(2):
                norm.deviation(pool, group_number(n))
            over_groups_ahead(pool, group, 2)

        block.__exit__(None, None, None)



def recurrent(nc, chip, ins, load_next):
    with ExitStack() as keep:
        hidden = [keep.enter_context(nc.sbuf_tensor(f"hidden_{n}", [P, NB * P], F32R)) for n in ("high", "low")]
        lstm_w = keep.enter_context(nc.sbuf_tensor("lstm_w", [P, 2 * 16 * P], F32))
        lstm_loaded = keep.enter_context(nc.semaphore("lstm_loaded"))
        convolutions(nc, chip, ins, hidden, lstm_w, lstm_loaded)
        lstms(nc, chip, hidden, lstm_w, lstm_loaded, load_next)
        add_hidden(nc, chip, hidden)


def convolutions(nc, chip, ins, hidden, lstm_w, lstm_loaded):
    with Phase(nc, "conv") as ph:
        norm = Norm(ph, chip)
        x, xn = chip.x, norm.xn
        w0, w1 = ph.sb("w0", [P, P]), ph.sb("w1", [P, P])
        ones = ph.sb("ones", [P, P])
        bias0 = ph.sb("bias0", [P, P])
        near = ph.sb("near", [P, COLS])
        first_sum = ph.sb("first_sum", [P, COLS])
        first = ph.sb("first", [P, COLS])
        second = ph.sb("second", [P, COLS])
        gather, project0, project1, gather1, sums = (ph.bank(n) for n in
                                                     ("gather", "project0", "project1", "gather1", "sums"))
        loaded = ph.sem("loaded")
        ones_set = ph.sem("ones_set")
        sums_ready = ph.sem("sums_ready")
        bias0_ready = ph.sem("bias0_ready")
        gather_ready = ph.sem("gather_ready")
        near_ready = ph.sem("near_ready")
        project0_ready = ph.sem("project0_ready")
        sum0_ready = ph.sem("sum0_ready")
        first_ready = ph.sem("first_ready")
        project1_ready = ph.sem("project1_ready")
        second_ready = ph.sem("second_ready")
        gather1_ready = ph.sem("gather1_ready")
        hidden_ready = ph.sem("hidden_ready")
        hidden_low_ready = ph.sem("hidden_low_ready")
        block = nc.Block()
        block.__enter__()

        @block.sync
        def _(sp):
            sp.dma_start(w0[:, :], ins["L1_gnn_Wg0"]).then_inc(loaded, 16)
            sp.dma_start(w1[:, :], ins["L1_gnn_Wg1"]).then_inc(loaded, 16)
            for n, name in enumerate(("L1_gnn_Wih", "L1_gnn_Whh")):
                sp.dma_start(lstm_w[:, n * 16 * P:(n + 1) * 16 * P].rearrange("h (r d) -> h r d", d=P),
                             ins[name].rearrange("p (t h) d -> h (p t) d", h=P)).then_inc(lstm_loaded, 16)

        @block.gpsimd
        def _(pool):
            pool.memset(ones[:, :], 1.0).then_inc(ones_set, 1)
            for n in range(4):
                norm.deviation(pool, group_number(n))

            def group(g, ahead):
                if ahead(4):
                    norm.deviation(pool, ahead(4))

            over_groups_ahead(pool, group, 4)

        @block.tensor
        def _(pe):
            def gathers(h):
                pe.wait_ge(norm.xn_ready, h + 1)
                if h.least:
                    pe.wait_ge(near_ready, h.n)
                for b in range(GB):
                    mm = pe.matmul(tile_of(gather, b), tile_of(xn[h.odd], b), chip.adj_t[:, :], start=True, stop=True)
                mm.then_inc(gather_ready, 1)

            def first_projection(h):
                pe.wait_ge(near_ready, h + 1)
                if h.least:
                    pe.wait_ge(sum0_ready, h.n)
                pe.matmul(project0[:, :], w0[:, :], near[:, :], start=True, stop=True).then_inc(project0_ready, 1)

            def second_projection(g):
                pe.wait_ge(first_ready, g + 1)
                if g.least:
                    pe.wait_ge(second_ready, g.n)
                for b in range(GB):
                    mm = pe.matmul(tile_of(project1, b), tile_of(first, b), w1[:, :], start=True, stop=True)
                mm.then_inc(project1_ready, 1)

            def second_gathers(g):
                pe.wait_ge(second_ready, g + 1)
                if g.least:
                    pe.wait_ge(hidden_low_ready, g.n)
                for b in range(GB):
                    mm = pe.matmul(tile_of(gather1, b), tile_of(second, b), chip.adj_t[:, :], start=True, stop=True)
                mm.then_inc(gather1_ready, 1)

            def group(g, ahead):
                second_gathers(g)
                for n, stage in ((1, second_projection), (2, first_projection), (3, gathers)):
                    if ahead(n):
                        stage(ahead(n))

            pe.wait_ge(loaded, 32)
            pe.wait_ge(ones_set, 1)
            pe.matmul(sums[:, 0:P], ones[:, :], chip.adj_t[:, :], start=True, stop=True).then_inc(sums_ready, 1)
            gathers(group_number(0))
            first_projection(group_number(0))
            gathers(group_number(1))
            second_projection(group_number(0))
            first_projection(group_number(1))
            gathers(group_number(2))
            over_groups_ahead(pe, group, 3)

        @block.scalar
        def _(scalar):
            def take_near(h):
                scalar.wait_ge(gather_ready, h + 1)
                if h.least:
                    scalar.wait_ge(project0_ready, h.n)
                scalar.activation(near[:, :], gather[:, :], ACT.Copy).then_inc(near_ready, 1)

            def take_first(h):
                scalar.wait_ge(sum0_ready, h + 1)
                if h.least:
                    scalar.wait_ge(project1_ready, h.n)
                scalar.activation(first[:, :], first_sum[:, :], ACT.Relu).then_inc(first_ready, 1)

            def take_hidden(g):
                scalar.wait_ge(gather1_ready, g + 1)
                scalar.activation(group_of(hidden[0], g), gather1[:, :], ACT.Relu).then_inc(hidden_ready, 1)

            def group(g, ahead):
                take_hidden(g)
                if ahead(2):
                    take_first(ahead(2))
                if ahead(3):
                    take_near(ahead(3))

            take_near(group_number(0))
            take_first(group_number(0))
            take_near(group_number(1))
            take_first(group_number(1))
            take_near(group_number(2))
            over_groups_ahead(scalar, group, 3)

        @block.vector
        def _(dve):
            def normalise(h):
                if h.least >= 2:
                    dve.wait_ge(gather_ready, h - 1)
                norm.normalise(dve, h)

            def add_bias0(h):
                dve.wait_ge(project0_ready, h + 1)
                if h.least:
                    dve.wait_ge(first_ready, h.n)
                dve.tensor_tensor(by_graph(first_sum[:, :]), by_graph(project0[:, :]),
                                  bias0[:, :].unsqueeze(1).to_broadcast([P, GB, P]), ALU.add).then_inc(sum0_ready, 1)

            def add_bias1(g):
                dve.wait_ge(project1_ready, g + 1)
                if g.least:
                    dve.wait_ge(gather1_ready, g.n)
                dve.tensor_tensor(by_graph(second[:, :]), by_graph(project1[:, :]),
                                  chip.tables["L2"]["bg1"].unsqueeze(1).to_broadcast([P, GB, P]), ALU.add)\
                    .then_inc(second_ready, 1)

            def low_hidden(g):
                dve.wait_ge(hidden_ready, g + 1)
                dve.scalar_tensor_tensor(out=group_of(hidden[1], g), in0=gather1[:, :], scalar=0.0,
                                         in1=group_of(hidden[0], g).bitcast(F32), op0=ALU.max, op1=ALU.subtract)\
                    .then_inc(hidden_low_ready, 1)

            def group(g, ahead):
                four = ahead(4)
                if four:
                    norm.statistics(dve, four)
                low_hidden(g)
                if ahead(1):
                    add_bias1(ahead(1))
                if four:
                    norm.aggregate(dve, four)
                if ahead(2):
                    add_bias0(ahead(2))
                if four:
                    normalise(four)

            dve.wait_ge(sums_ready, 1)
            dve.tensor_scalar(bias0[:, :], sums[:, 0:P], chip.bg0, None, ALU.mult).then_inc(bias0_ready, 1)
            for n in range(3):
                norm.moments(dve, group_number(n))
                normalise(group_number(n))
            dve.wait_ge(bias0_ready, 1)
            add_bias0(group_number(0))
            add_bias1(group_number(0))
            add_bias0(group_number(1))
            norm.moments(dve, group_number(3))
            normalise(group_number(3))
            over_groups_ahead(dve, group, 4)

        block.__exit__(None, None, None)


LSTMS = ((1, 4), (2, 8), (3, 8), (4, 16))


def lstms(nc, chip, hidden, lstm_w, lstm_loaded, load_next):
    with Phase(nc, "lstm") as ph:
        weight_high = ph.sb("weight_high", [P, 2 * 16 * P], F32R)
        weight_low = ph.sb("weight_low", [P, 2 * 16 * P], F32R)
        gates = [[ph.bank(f"gate{c}_{j}") for j in range(4)] for c in range(2)]
        value = [[ph.sb(f"value{c}_{j}", [P, COLS]) for j in range(4)] for c in range(2)]
        cell = [ph.sb(f"cell{c}", [P, COLS]) for c in range(2)]
        cell_tanh = [ph.sb(f"cell_tanh{c}", [P, COLS]) for c in range(2)]
        state = [ph.sb(f"state{c}", [P, COLS]) for c in range(2)]
        state_high = [ph.sb(f"state_high{c}", [P, COLS], F32R) for c in range(2)]
        state_low = [ph.sb(f"state_low{c}", [P, COLS], F32R) for c in range(2)]
        turned = ph.sem("turned")
        w_high = ph.sem("w_high")
        w_low = ph.sem("w_low")
        gate_ready = ph.sem("gate_ready")
        gate_done = ph.sem("gate_done")
        kept_step = ph.sem("kept_step")
        cell_ready = ph.sem("cell_ready")
        tanh_ready = ph.sem("tanh_ready")
        state_high_ready = ph.sem("state_high_ready")
        state_whole = ph.sem("state_whole")
        state_ready = ph.sem("state_ready")
        block = nc.Block()
        block.__enter__()
        ORDER = (0, 2, 1, 3)

        def gates_of(s):
            return [j for j in ORDER if s or j != 1]

        def over_units(engine, unit):
            units = later = gates_before = 0
            for p, graphs in LSTMS:
                pairs = NB // graphs // 2
                per_pair = 2 * sum(len(gates_of(s)) for s in range(p))

                def two(pair, opening):
                    u, at = pair * (2 * p) + units, pair * per_pair + gates_before
                    more = pair * (2 * p - 2) + later
                    n = 0
                    for s in range(p):
                        for c in range(2):
                            unit(p, graphs, pair, s, c, u + (2 * s + c), more + (2 * s - 2 + c), at + n,
                                 opening and s == 0)
                            n += len(gates_of(s))

                two(0, True)
                with engine.Fori(1, pairs) as pair:
                    two(pair, False)
                units += pairs * 2 * p
                later += pairs * 2 * (p - 1)
                gates_before += pairs * per_pair

        def windows(half, p, graphs, pair, c, s):
            n = P // p
            chunk = hidden[half][:, bass.ds((pair * 2 + c) * (graphs * P), graphs * P)].rearrange("h (b t) -> h b t", t=P)
            return chunk[:, :, s:s + p * (n - 1) + 1:p]

        def columns(buf, p, graphs):
            return buf[:, 0:graphs * (P // p)]

        def as_windows(buf, p, graphs):
            return columns(buf, p, graphs).rearrange("h (b w) -> h b w", b=graphs)

        @block.sync
        def _(sp):
            load_next(sp)

        @block.tensor
        def _(pe):
            pe.wait_ge(lstm_loaded, 32)
            for c in range(8):
                for b in range(GB):
                    mm = pe.transpose(tile_of(gates[c // 4][c % 4], b), tile_of(lstm_w[:, c * COLS:(c + 1) * COLS], b),
                                      chip.ident)
                mm.then_inc(turned, 1)
            pe.wait_ge(w_high, 8)
            pe.wait_ge(w_low, 8)

            def unit(p, graphs, pair, s, c, units, later, gates_before, opening):
                if not (p == 1 and opening):
                    behind = gates_before_last(p, s, c, opening)
                    pe.wait_ge(gate_done, gates_before - behind)
                if opening and p > 1 and c == 0:
                    pe.wait_ge(state_ready, units)
                for j in gates_of(s):
                    w = slice(((p - 1) * 4 + j) * P, ((p - 1) * 4 + j + 1) * P)
                    bank = as_windows(gates[c][j], p, graphs)
                    x_high, x_low = (windows(half, p, graphs, pair, c, s) for half in range(2))
                    pe.matmul(bank, weight_high[:, w], x_high, start=True, stop=False)
                    pe.matmul(bank, weight_high[:, w], x_low, start=False, stop=False)
                    mm = pe.matmul(bank, weight_low[:, w], x_high, start=False, stop=(s == 0))
                    if s == 0:
                        mm.then_inc(gate_ready, 1)
                if s:
                    pe.wait_ge(state_high_ready, units - 1)
                    ws = [slice((16 + (p - 1) * 4 + j) * P, (16 + (p - 1) * 4 + j + 1) * P) for j in range(4)]
                    h_high, h_low = columns(state_high[c], p, graphs), columns(state_low[c], p, graphs)
                    for j in gates_of(s):
                        bank = columns(gates[c][j], p, graphs)
                        pe.matmul(bank, weight_high[:, ws[j]], h_high, start=False, stop=False)
                        pe.matmul(bank, weight_low[:, ws[j]], h_high, start=False, stop=False)
                    pe.wait_ge(state_ready, units - 1)
                    for j in gates_of(s):
                        pe.matmul(columns(gates[c][j], p, graphs), weight_high[:, ws[j]], h_low,
                                  start=False, stop=True).then_inc(gate_ready, 1)

            def gates_before_last(p, s, c, opening):
                if c == 1:
                    return len(gates_of(s))
                if s:
                    return len(gates_of(s - 1))
                return len(gates_of((p - 1) if not opening else (p - 2)))

            over_units(pe, unit)

        @block.scalar
        def _(scalar):
            for c in range(8):
                scalar.wait_ge(turned, c + 1)
                scalar.activation(weight_high[:, c * COLS:(c + 1) * COLS], gates[c // 4][c % 4][:, :], ACT.Copy)\
                    .then_inc(w_high, 1)

            def unit(p, graphs, pair, s, c, units, later, gates_before, opening):
                if not (p == 1 and opening):
                    scalar.wait_ge(state_whole, units - 1)
                for n, j in enumerate(gates_of(s)):
                    scalar.wait_ge(gate_ready, gates_before + (n + 1))
                    scalar.activation(columns(value[c][j], p, graphs), columns(gates[c][j], p, graphs),
                                      ACT.Tanh if j == 2 else ACT.Sigmoid,
                                      bias=chip.lstm_bias[:, (p - 1) * 4 + j:(p - 1) * 4 + j + 1]).then_inc(gate_done, 1)
                scalar.wait_ge(cell_ready, units + 1)
                scalar.activation(columns(cell_tanh[c], p, graphs), columns(cell[c], p, graphs), ACT.Tanh)\
                    .then_inc(tanh_ready, 1)

            over_units(scalar, unit)

        @block.vector
        def _(dve):
            for c in range(8):
                dve.wait_ge(w_high, c + 1)
                cols = slice(c * COLS, (c + 1) * COLS)
                dve.tensor_tensor(weight_low[:, cols], gates[c // 4][c % 4][:, :], weight_high[:, cols].bitcast(F32),
                                  ALU.subtract).then_inc(w_low, 1)

            def unit(p, graphs, pair, s, c, units, later, gates_before, opening):
                def cols(buf):
                    return columns(buf, p, graphs)

                i, f, g, o = (cols(value[c][j]) for j in range(4))
                if not (p == 1 and opening):
                    dve.wait_ge(cell_ready, units - 1)
                    dve.wait_ge(tanh_ready, units - 1)
                if s == 0:
                    dve.wait_ge(gate_done, gates_before + 2)
                    dve.tensor_tensor(cols(cell[c]), i, g, ALU.mult).then_inc(cell_ready, 1)
                else:
                    dve.wait_ge(gate_done, gates_before + 2)
                    dve.tensor_tensor(i, i, g, ALU.mult).then_inc(kept_step, 1)
                    dve.wait_ge(gate_done, gates_before + 3)
                    dve.tensor_tensor(cols(cell[c]), cols(cell[c]), f, ALU.mult).then_inc(kept_step, 1)
                    dve.wait_ge(kept_step, later * 2 + 2)
                    dve.tensor_tensor(cols(cell[c]), cols(cell[c]), i, ALU.add).then_inc(cell_ready, 1)
                dve.wait_ge(tanh_ready, units + 1)
                if s < p - 1:
                    dve.tensor_tensor(cols(state_high[c]), o, cols(cell_tanh[c]), ALU.mult).then_inc(state_high_ready, 1)
                else:
                    dve.tensor_tensor(windows(0, p, graphs, pair, c, s), as_windows(value[c][3], p, graphs),
                                      as_windows(cell_tanh[c], p, graphs), ALU.mult).then_inc(state_high_ready, 1)
                if not (p == 1 and opening):
                    dve.wait_ge(state_ready, units - 1)
                dve.tensor_tensor(cols(state[c]), o, cols(cell_tanh[c]), ALU.mult).then_inc(state_whole, 1)

            over_units(dve, unit)

        @block.gpsimd
        def _(pool):
            def unit(p, graphs, pair, s, c, units, later, gates_before, opening):
                pool.wait_ge(state_whole, units + 1)
                if s < p - 1:
                    pool.tensor_tensor(columns(state_low[c], p, graphs), columns(state[c], p, graphs),
                                       columns(state_high[c], p, graphs).bitcast(F32), ALU.subtract)\
                        .then_inc(state_ready, 1)
                else:
                    pool.tensor_tensor(windows(1, p, graphs, pair, c, s), as_windows(state[c], p, graphs),
                                       windows(0, p, graphs, pair, c, s).bitcast(F32), ALU.subtract)\
                        .then_inc(state_ready, 1)

            over_units(pool, unit)

        block.__exit__(None, None, None)


def add_hidden(nc, chip, hidden):
    with Phase(nc, "fold") as ph:
        copy = [ph.sb(f"copy{i}", [P, COLS]) for i in range(2)]
        turn = [ph.bank(f"turn{i}") for i in range(2)]
        copy_ready = ph.sem("copy_ready")
        turn_ready = ph.sem("turn_ready")
        added = ph.sem("added")
        block = nc.Block()
        block.__enter__()

        @block.gpsimd
        def _(pool):
            def group(g, behind, ahead):
                if g.least >= 2:
                    pool.wait_ge(turn_ready, g - 1)
                pool.tensor_tensor(copy[g.odd][:, :], group_of(hidden[0], g).bitcast(F32),
                                   group_of(hidden[1], g).bitcast(F32), ALU.add).then_inc(copy_ready, 1)

            over_groups_wide(pool, group)

        @block.tensor
        def _(pe):
            def group(g, behind, ahead):
                pe.wait_ge(copy_ready, g + 1)
                if g.least >= 2:
                    pe.wait_ge(added, g - 1)
                for b in range(GB):
                    mm = pe.transpose(tile_of(turn[g.odd], b), tile_of(copy[g.odd], b), chip.ident)
                mm.then_inc(turn_ready, 1)

            over_groups_wide(pe, group)

        @block.vector
        def _(dve):
            def group(g, behind, ahead):
                dve.wait_ge(turn_ready, g + 1)
                dve.tensor_tensor(group_of(chip.x, g), group_of(chip.x, g), turn[g.odd][:, :], ALU.add)\
                    .then_inc(added, 1)

            over_groups_wide(dve, group)

        block.__exit__(None, None, None)



HEADS = 4
EDGES = 256
ET = EDGES // P
ROWS = NB * HEADS
LRELU = 0.2
EDGE_EPS = 1e-8
FAR = -1e30


class Split:

    def __init__(self, nc, tag, chip, keep, raw_count, K):
        self.raw, self.loaded, self.raw_count = chip.raw, chip.raw_loaded, raw_count
        self.high, self.low = (keep.enter_context(nc.sbuf_tensor(f"{tag}_{name}", [P, 2 * K * P], F32R))
                               for name in ("high", "low"))
        self.chunks = 2 * K * P // COLS

    def semaphores(self, ph):
        self.high_ready = ph.sem("split_high")
        self.low_ready = ph.sem("split_low")

    def high_half(self, scalar, c):
        if c == 0:
            scalar.wait_ge(self.loaded, self.raw_count)
        cols = slice(c * COLS, (c + 1) * COLS)
        scalar.activation(self.high[:, cols], self.raw[:, cols], ACT.Copy).then_inc(self.high_ready, 1)

    def low_half(self, pool, c):
        pool.wait_ge(self.high_ready, c + 1)
        cols = slice(c * COLS, (c + 1) * COLS)
        pool.tensor_tensor(self.low[:, cols], self.raw[:, cols], self.high[:, cols].bitcast(F32), ALU.subtract)\
            .then_inc(self.low_ready, 1)


def edges(nc, chip, ins, load_next, split):
    with ExitStack() as keep:
        t = chip.edges
        t.values = keep.enter_context(nc.sbuf_tensor("edge_values", [P, NB * P], F32))
        t.score = keep.enter_context(nc.sbuf_tensor("edge_score", [P, ET, ROWS], F32))
        edge_scores(nc, chip, t, load_next)
        edge_softmax(nc, chip, t, split)
        edge_sums(nc, chip, t)


def edge_storage(nc, keep):
    def kept(name, shape):
        return keep.enter_context(nc.sbuf_tensor(f"edge_{name}", shape, F32))

    t = Chip()
    t.at_src = kept("at_src", [P, EDGES])
    t.at_dst = kept("at_dst", [P, EDGES])
    t.at_both = kept("at_both", [P, EDGES])
    t.src_t = kept("src_t", [P, ET, P])
    t.last_t = kept("last_t", [P, ET, P])
    t.restart = kept("restart", [P, EDGES])
    t.log_adj = kept("log_adj", [P, ET])
    t.heads = kept("heads", [P, HEADS])
    t.weights = kept("weights", [P, 3 * P])
    return t


def edge_tables(nc, chip, ins, t):
    with Phase(nc, "etab") as ph:
        ends = ph.sb("ends", [1, 2 * EDGES], I32)
        endsf = ph.sb("endsf", [1, 2 * EDGES])
        key = ph.sb("key", [1, EDGES])
        ones = ph.sb("ones", [P, P])
        count = ph.sb("count", [P, EDGES])
        own = ph.sb("own", [P, 1])
        heads_at = ph.sb("heads_at", [P, HEADS])
        a_col = ph.sb("a_col", [P, 1])
        raw_w = ph.sb("raw_w", [P, 3 * P])
        key_all = ph.sb("key_all", [P, EDGES])
        key_col = ph.sb("key_col", [P, 3 * ET])
        below = ph.sb("below", [P, ET, EDGES])
        rank = ph.sb("rank", [P, ET])
        perm = ph.sb("perm", [P, ET, EDGES])
        spread = ph.sb("spread", [P, 2 * ET, P])
        sorted_ends = ph.sb("sorted_ends", [P, 2, EDGES])
        is_last = ph.sb("is_last", [P, EDGES])
        dst_t = ph.sb("dst_t", [P, ET, P])
        last_of = ph.sb("last_of", [P, EDGES])
        adj_at = ph.sb("adj_at", [P, ET, P])
        adj_sum = ph.sb("adj_sum", [P, ET])
        banks = [ph.bank(f"bank{i}") for i in range(8)]
        loaded = ph.sem("loaded")
        pool_step = ph.sem("pool_step")
        step = ph.sem("step")
        product = ph.sem("product")
        logged = ph.sem("logged")
        block = nc.Block()
        block.__enter__()

        @block.sync
        def _(sp):
            for n, name in enumerate(("L2_gnn_src", "L2_gnn_dst")):
                sp.dma_start(ends[:, n * EDGES:(n + 1) * EDGES], ins[name].rearrange("(a e) -> a e", a=1))\
                    .then_inc(loaded, 16)
            for n, name in enumerate(("L2_gnn_W_lin", "L2_gnn_W_val", "L2_gnn_W_out")):
                sp.dma_start(tile_of(raw_w, n), ins[name]).then_inc(loaded, 16)
            sp.dma_start(a_col[:, :], ins["L2_gnn_a"].rearrange("h (d a) -> (h d) a", a=1)).then_inc(loaded, 16)

        @block.gpsimd
        def _(pool):
            pool.memset(ones[:, :], 1.0).then_inc(pool_step, 1)
            pool.memset(heads_at[:, :], 1.0).then_inc(pool_step, 1)
            pool.iota(count[:, :], [[1, EDGES]], base=0, channel_multiplier=0, allow_small_or_imprecise_dtypes=True)\
                .then_inc(pool_step, 1)
            pool.iota(own[:, :], [[1, 1]], base=0, channel_multiplier=1, allow_small_or_imprecise_dtypes=True)\
                .then_inc(pool_step, 1)
            pool.wait_ge(pool_step, 4)
            d = P // HEADS
            pool.affine_select(out=heads_at[:, :], in_=heads_at[:, :], compare_op=ALU.is_ge, fill=0.0, base=0,
                               pattern=[[-d, HEADS]], channel_multiplier=1).then_inc(pool_step, 1)
            pool.wait_ge(pool_step, 5)
            pool.affine_select(out=heads_at[:, :], in_=heads_at[:, :], compare_op=ALU.is_gt, fill=0.0, base=d,
                               pattern=[[d, HEADS]], channel_multiplier=-1).then_inc(pool_step, 1)

        @block.vector
        def _(dve):
            done = [0]

            def link(op):
                op.then_inc(step, 1)
                done[0] += 1
                dve.wait_ge(step, done[0])

            dve.wait_ge(loaded, 96)
            dve.wait_ge(pool_step, 6)
            link(dve.tensor_copy(endsf[:, :], ends[:, :]))
            link(dve.scalar_tensor_tensor(out=key[:, :], in0=endsf[:, 0:EDGES], scalar=float(EDGES),
                                          in1=count[0:1, :], op0=ALU.mult, op1=ALU.add))
            assert done[0] == 2
            link(dve.tensor_scalar(t.heads[:, :], heads_at[:, :], a_col[:, 0:1], None, ALU.mult))
            dve.wait_ge(product, 1)
            link(dve.tensor_copy(key_all[:, :], banks[0][:, 0:EDGES]))
            link(dve.tensor_copy(key_col[:, :], banks[1][:, 0:3 * ET]))
            link(dve.tensor_copy(t.weights[:, :], banks[2][:, 0:3 * P]))
            for e in range(ET):
                link(dve.tensor_scalar(below[:, e, :], key_all[:, :], key_col[:, e:e + 1], None, ALU.is_lt))
            link(dve.reduce_sum(rank[:, :], below[:, :, :], AX.X))
            for e in range(ET):
                link(dve.tensor_scalar(perm[:, e, :], count[:, :], rank[:, e:e + 1], None, ALU.is_equal))
            for n in range(2 * ET):
                link(dve.tensor_scalar(spread[:, n, :], ones[:, :], key_col[:, ET + n:ET + n + 1], None, ALU.mult))
            assert done[0] == 15
            dve.wait_ge(product, 2)
            link(dve.tensor_copy(sorted_ends[:, :, :], banks[3][:, :].rearrange("p (n e) -> p n e", n=2)))
            link(dve.tensor_scalar(t.at_src[:, :], sorted_ends[:, 0, :], own[:, 0:1], None, ALU.is_equal))
            link(dve.tensor_scalar(t.at_dst[:, :], sorted_ends[:, 1, :], own[:, 0:1], None, ALU.is_equal))
            link(dve.tensor_tensor(t.at_both[:, :], t.at_src[:, :], t.at_dst[:, :], ALU.add))
            link(dve.memset(is_last[:, :], 1.0))
            link(dve.tensor_tensor(is_last[:, 0:EDGES - 1], sorted_ends[:, 0, 0:EDGES - 1], sorted_ends[:, 0, 1:EDGES],
                                   ALU.not_equal))
            link(dve.memset(t.restart[:, :], 0.0))
            link(dve.tensor_scalar(t.restart[:, 1:EDGES], is_last[:, 0:EDGES - 1], FAR, None, ALU.mult))
            link(dve.tensor_tensor(last_of[:, :], t.at_src[:, :], is_last[:, :], ALU.mult))
            assert done[0] == 24
            dve.wait_ge(product, 3)
            link(dve.tensor_copy(t.src_t[:, :, :], banks[4][:, 0:ET * P].rearrange("p (t n) -> p t n", t=ET)))
            link(dve.tensor_copy(dst_t[:, :, :], banks[5][:, 0:ET * P].rearrange("p (t n) -> p t n", t=ET)))
            link(dve.tensor_copy(t.last_t[:, :, :], banks[6][:, 0:ET * P].rearrange("p (t n) -> p t n", t=ET)))
            link(dve.tensor_tensor(adj_at[:, :, :], banks[7][:, 0:ET * P].rearrange("p (t n) -> p t n", t=ET),
                                   dst_t[:, :, :], ALU.mult))
            link(dve.reduce_sum(adj_sum[:, :], adj_at[:, :, :], AX.X))
            link(dve.tensor_scalar(adj_sum[:, :], adj_sum[:, :], EDGE_EPS, None, ALU.add))
            assert done[0] == 30

        @block.scalar
        def _(scalar):
            scalar.wait_ge(step, 30)
            scalar.activation(t.log_adj[:, :], adj_sum[:, :], ACT.Ln).then_inc(logged, 1)

        @block.tensor
        def _(pe):
            pe.wait_ge(step, 2)
            pe.matmul(banks[0][:, 0:EDGES], ones[0:1, :], key[:, :], start=True, stop=True)
            for e in range(ET):
                for n, row in enumerate((key, endsf, endsf)):
                    at = e * P + (EDGES if n == 2 else 0)
                    pe.matmul(banks[1][:, n * ET + e:n * ET + e + 1], row[:, at:at + P], ones[0:1, 0:1],
                              start=True, stop=True)
            for n in range(3):
                mm = pe.transpose(tile_of(banks[2], n), tile_of(raw_w, n), chip.ident)
            mm.then_inc(product, 1)
            pe.wait_ge(step, 15)
            for n in range(2):
                for e in range(ET):
                    mm = pe.matmul(banks[3][:, n * EDGES:(n + 1) * EDGES], spread[:, n * ET + e, :], perm[:, e, :],
                                   start=(e == 0), stop=(e == ET - 1))
            mm.then_inc(product, 1)
            pe.wait_ge(step, 24)
            for e in range(ET):
                pe.transpose(tile_of(banks[4], e), tile_of(t.at_src, e), chip.ident)
                pe.transpose(tile_of(banks[5], e), tile_of(t.at_dst, e), chip.ident)
                pe.transpose(tile_of(banks[6], e), tile_of(last_of, e), chip.ident)
                mm = pe.matmul(tile_of(banks[7], e), tile_of(t.at_src, e), chip.adj[:, :], start=True, stop=True)
            mm.then_inc(product, 1)

        block.__exit__(None, None, None)


def edge_scores(nc, chip, t, load_next):
    with Phase(nc, "esco") as ph:
        norm = Norm(ph, chip)
        xn = norm.xn
        xt = ph.sb("xt", [P, COLS])
        query = ph.sb("query", [P, COLS])
        small_sum = [ph.sb(f"small_sum{i}", [P, COLS]) for i in range(2)]
        leaky = [ph.sb(f"leaky{i}", [P, COLS]) for i in range(2)]
        turn, queries, values, score = (ph.bank(n) for n in ("turn", "queries", "values", "score"))
        sums = [ph.bank(f"sums{i}") for i in range(2)]
        turn_ready = ph.sem("turn_ready")
        xt_ready = ph.sem("xt_ready")
        query_ready = ph.sem("query_ready")
        value_ready = ph.sem("value_ready")
        query_taken = ph.sem("query_taken")
        value_taken = ph.sem("value_taken")
        sum_ready = ph.sem("sum_ready")
        small_ready = ph.sem("small_ready")
        leaky_ready = ph.sem("leaky_ready")
        score_ready = ph.sem("score_ready")
        score_taken = ph.sem("score_taken")
        block = nc.Block()
        block.__enter__()

        @block.sync
        def _(sp):
            load_next(sp)

        @block.gpsimd
        def _(pool):
            def group(g, ahead):
                if ahead(3):
                    norm.deviation(pool, ahead(3))

            for n in range(3):
                norm.deviation(pool, group_number(n))
            over_groups_ahead(pool, group, 3)

        @block.tensor
        def _(pe):
            def turn_tokens(h):
                pe.wait_ge(norm.xn_ready, h + 1)
                if h.least:
                    pe.wait_ge(xt_ready, h.n)
                for b in range(GB):
                    mm = pe.transpose(tile_of(turn, b), tile_of(xn[h.odd], b), chip.ident)
                mm.then_inc(turn_ready, 1)

            def project(h):
                pe.wait_ge(xt_ready, h + 1)
                if h.least:
                    pe.wait_ge(query_taken, h.n)
                for b in range(GB):
                    mm = pe.matmul(tile_of(queries, b), tile_of(xt, b), t.weights[:, 0:P], start=True, stop=True)
                mm.then_inc(query_ready, 1)
                if h.least:
                    pe.wait_ge(value_taken, h.n)
                for b in range(GB):
                    mm = pe.matmul(tile_of(values, b), tile_of(xt, b), t.weights[:, P:2 * P], start=True, stop=True)
                mm.then_inc(value_ready, 1)

            def sum_ends(h):
                pe.wait_ge(query_taken, h + 1)
                for i in range(2):
                    if h.least:
                        pe.wait_ge(leaky_ready, h * 2 - 1 + i)
                    for b in range(2):
                        mm = pe.matmul(sums[i][:, b * EDGES:(b + 1) * EDGES], tile_of(query, 2 * i + b),
                                       t.at_both[:, :], start=True, stop=True)
                    mm.then_inc(sum_ready, 1)

            def scores(g):
                if g.least:
                    pe.wait_ge(score_taken, g.n)
                for b in range(GB):
                    if b % 2 == 0:
                        pe.wait_ge(leaky_ready, g * 2 + b // 2 + 1)
                    for e in range(ET):
                        at = (b % 2) * EDGES + e * P
                        mm = pe.matmul(score[:, (e * GB + b) * HEADS:(e * GB + b + 1) * HEADS],
                                       leaky[b // 2][:, at:at + P], t.heads[:, :], start=True, stop=True)
                mm.then_inc(score_ready, 1)

            def group(g, ahead):
                one, two = ahead(1), ahead(2)
                if two:
                    turn_tokens(two)
                scores(g)
                if one:
                    sum_ends(one)
                if two:
                    project(two)

            turn_tokens(group_number(0))
            project(group_number(0))
            turn_tokens(group_number(1))
            sum_ends(group_number(0))
            project(group_number(1))
            over_groups_ahead(pe, group, 2)

        @block.scalar
        def _(scalar):
            def take_turned(h):
                scalar.wait_ge(turn_ready, h + 1)
                if h.least:
                    scalar.wait_ge(value_ready, h.n)
                scalar.activation(xt[:, :], turn[:, :], ACT.Copy).then_inc(xt_ready, 1)

            def take_query(h):
                scalar.wait_ge(query_ready, h + 1)
                if h.least:
                    scalar.wait_ge(sum_ready, h * 2)
                scalar.activation(query[:, :], queries[:, :], ACT.Copy).then_inc(query_taken, 1)

            def small(h):
                for i in range(2):
                    scalar.wait_ge(sum_ready, h * 2 + i + 1)
                    if h.least:
                        scalar.wait_ge(leaky_ready, h * 2 - 1 + i)
                    scalar.activation(small_sum[i][:, :], sums[i][:, :], ACT.Copy, scale=LRELU).then_inc(small_ready, 1)

            def group(g, ahead):
                one, two = ahead(1), ahead(2)
                if two:
                    take_turned(two)
                if one:
                    small(one)
                if two:
                    take_query(two)

            take_turned(group_number(0))
            take_query(group_number(0))
            take_turned(group_number(1))
            small(group_number(0))
            take_query(group_number(1))
            over_groups_ahead(scalar, group, 2)

        @block.vector
        def _(dve):
            def normalise(h):
                if h.least >= 2:
                    dve.wait_ge(turn_ready, h - 1)
                norm.normalise(dve, h)

            def take_values(h):
                dve.wait_ge(value_ready, h + 1)
                dve.tensor_copy(group_of(t.values, h), values[:, :]).then_inc(value_taken, 1)

            def leak(h):
                for i in range(2):
                    dve.wait_ge(small_ready, h * 2 + i + 1)
                    if h.least:
                        dve.wait_ge(score_ready, h.n)
                    dve.tensor_tensor(leaky[i][:, :], sums[i][:, :], small_sum[i][:, :], ALU.max)\
                        .then_inc(leaky_ready, 1)

            def take_scores(g):
                dve.wait_ge(score_ready, g + 1)
                n = GB * HEADS
                for e in range(ET):
                    op = dve.tensor_scalar(t.score[:, e, bass.ds(g * n, n)], score[:, e * n:(e + 1) * n],
                                           t.log_adj[:, e:e + 1], None, ALU.add)
                op.then_inc(score_taken, 1)

            def group(g, ahead):
                one, two, three = ahead(1), ahead(2), ahead(3)
                if three:
                    norm.moments(dve, three)
                take_scores(g)
                if three:
                    normalise(three)
                if one:
                    leak(one)
                if two:
                    take_values(two)

            for n in range(3):
                norm.moments(dve, group_number(n))
                normalise(group_number(n))
            take_values(group_number(0))
            leak(group_number(0))
            take_values(group_number(1))
            over_groups_ahead(dve, group, 3)

        block.__exit__(None, None, None)


def edge_softmax(nc, chip, t, split):
    with Phase(nc, "esof") as ph:
        split.semaphores(ph)
        rows = ph.sb("rows", [P, 2, EDGES])
        running = ph.sb("running", [P, 2, EDGES])
        running_t = ph.sb("running_t", [P, ET, ROWS])
        node_max = ph.sb("node_max", [P, ROWS])
        shifted = ph.sb("shifted", [P, ET, ROWS])
        expd = ph.sb("expd", [P, ET, ROWS])
        node_sum = ph.sb("node_sum", [P, ROWS])
        edge_inv = ph.sb("edge_inv", [P, ET, ROWS])
        turned, back, of_node, of_edge, sum_node, sum_edge = (ph.bank(n) for n in (
            "turned", "back", "of_node", "of_edge", "sum_node", "sum_edge"))
        product = ph.sem("product")
        step = ph.sem("step")
        exp_ready = ph.sem("exp_ready")
        block = nc.Block()
        block.__enter__()

        @block.tensor
        def _(pe):
            for r in range(2):
                for e in range(ET):
                    mm = pe.transpose(turned[:, r * EDGES + e * P:r * EDGES + (e + 1) * P],
                                      t.score[:, e, r * P:(r + 1) * P], chip.ident)
            mm.then_inc(product, 1)
            pe.wait_ge(step, 3)
            for r in range(2):
                for e in range(ET):
                    mm = pe.transpose(back[:, e * ROWS + r * P:e * ROWS + (r + 1) * P],
                                      running[:, r, e * P:(e + 1) * P], chip.ident)
            mm.then_inc(product, 1)
            pe.wait_ge(step, 4)
            for e in range(ET):
                mm = pe.matmul(of_node[:, 0:ROWS], t.last_t[:, e, :], running_t[:, e, :], start=(e == 0),
                               stop=(e == ET - 1))
            mm.then_inc(product, 1)
            pe.wait_ge(step, 5)
            for e in range(ET):
                mm = pe.matmul(of_edge[:, e * ROWS:(e + 1) * ROWS], tile_of(t.at_src, e), node_max[:, :],
                               start=True, stop=True)
            mm.then_inc(product, 1)
            pe.wait_ge(exp_ready, 1)
            for e in range(ET):
                mm = pe.matmul(sum_node[:, 0:ROWS], t.src_t[:, e, :], expd[:, e, :], start=(e == 0), stop=(e == ET - 1))
            mm.then_inc(product, 1)
            pe.wait_ge(step, 7)
            for e in range(ET):
                mm = pe.matmul(sum_edge[:, e * ROWS:(e + 1) * ROWS], tile_of(t.at_src, e), node_sum[:, :],
                               start=True, stop=True)
            mm.then_inc(product, 1)

        @block.vector
        def _(dve):
            def tiles(bank):
                return bank[:, :].rearrange("p (t r) -> p t r", t=2)

            dve.wait_ge(product, 1)
            dve.tensor_copy(rows[:, :, :], tiles(turned)).then_inc(step, 1)
            dve.wait_ge(step, 1)
            for r in range(2):
                dve.tensor_tensor_scan(running[:, r, :], t.restart[:, :], rows[:, r, :], FAR, ALU.add, ALU.max)\
                    .then_inc(step, 1)
            dve.wait_ge(product, 2)
            dve.tensor_copy(running_t[:, :, :], tiles(back)).then_inc(step, 1)
            dve.wait_ge(product, 3)
            dve.tensor_copy(node_max[:, :], of_node[:, 0:ROWS]).then_inc(step, 1)
            dve.wait_ge(product, 4)
            dve.tensor_tensor(shifted[:, :, :], t.score[:, :, :], tiles(of_edge), ALU.subtract).then_inc(step, 1)
            dve.wait_ge(product, 5)
            dve.tensor_copy(node_sum[:, :], sum_node[:, 0:ROWS]).then_inc(step, 1)
            dve.wait_ge(product, 6)
            dve.reciprocal(edge_inv[:, :, :], tiles(sum_edge)).then_inc(step, 1)
            dve.wait_ge(step, 8)
            dve.tensor_tensor(t.score[:, :, :], expd[:, :, :], edge_inv[:, :, :], ALU.mult).then_inc(step, 1)

        @block.scalar
        def _(scalar):
            for c in range(split.chunks // 2):
                split.high_half(scalar, c)
            scalar.wait_ge(step, 6)
            scalar.activation(expd[:, :, :], shifted[:, :, :], ACT.Exp).then_inc(exp_ready, 1)
            for c in range(split.chunks // 2, split.chunks):
                split.high_half(scalar, c)

        @block.gpsimd
        def _(pool):
            for c in range(split.chunks):
                split.low_half(pool, c)

        block.__exit__(None, None, None)


def edge_sums(nc, chip, t):
    with Phase(nc, "esum") as ph:
        weighed = [[ph.sb(f"weighed{i}_{e}", [P, COLS]) for e in range(ET)] for i in range(2)]
        summed = ph.sb("summed", [P, COLS])
        at_edge = [[ph.bank(f"at_edge{i}_{e}") for e in range(ET)] for i in range(2)]
        sums, out = ph.bank("sums"), ph.bank("out")
        at_edge_ready = ph.sem("at_edge_ready")
        weighed_ready = ph.sem("weighed_ready")
        sums_ready = ph.sem("sums_ready")
        summed_ready = ph.sem("summed_ready")
        out_ready = ph.sem("out_ready")
        added = ph.sem("added")
        block = nc.Block()
        block.__enter__()

        @block.tensor
        def _(pe):
            def gathers(h):
                for e in range(ET):
                    if h.least >= 2:
                        pe.wait_ge(weighed_ready, (h - 2) * ET + (e + 1))
                    pe.matmul(at_edge[h.odd][e][:, :], tile_of(t.at_dst, e), group_of(t.values, h), start=True, stop=True)\
                        .then_inc(at_edge_ready, 1)

            def segment_sums(g):
                pe.wait_ge(weighed_ready, g * ET + ET)
                if g.least:
                    pe.wait_ge(summed_ready, g.n)
                for b in range(GB):
                    for e in range(ET):
                        mm = pe.matmul(tile_of(sums, b), tile_of(weighed[g.odd][e], b), t.src_t[:, e, :], start=(e == 0),
                                       stop=(e == ET - 1))
                mm.then_inc(sums_ready, 1)

            def outs(g):
                pe.wait_ge(summed_ready, g + 1)
                if g.least:
                    pe.wait_ge(added, g.n)
                for b in range(GB):
                    mm = pe.matmul(tile_of(out, b), tile_of(summed, b), t.weights[:, 2 * P:3 * P], start=True, stop=True)
                mm.then_inc(out_ready, 1)

            def group(g, ahead):
                segment_sums(g)
                if ahead(2):
                    gathers(ahead(2))
                outs(g)

            gathers(group_number(0))
            gathers(group_number(1))
            over_groups_ahead(pe, group, 2)

        @block.scalar
        def _(scalar):
            def group(g, ahead):
                scalar.wait_ge(sums_ready, g + 1)
                if g.least:
                    scalar.wait_ge(out_ready, g.n)
                scalar.activation(summed[:, :], sums[:, :], ACT.Copy).then_inc(summed_ready, 1)

            over_groups_ahead(scalar, group, 0)

        @block.vector
        def _(dve):
            n = GB * HEADS

            def weigh(h):
                for e in range(ET):
                    dve.wait_ge(at_edge_ready, h * ET + e + 1)
                    if h.least >= 2:
                        dve.wait_ge(sums_ready, h - 1)
                    dve.tensor_tensor(weighed[h.odd][e][:, :].rearrange("e (r d) -> e r d", r=n),
                                      at_edge[h.odd][e][:, :].rearrange("e (r d) -> e r d", r=n),
                                      t.score[:, e, bass.ds(h * n, n)].unsqueeze(2).to_broadcast([P, n, P // HEADS]),
                                      ALU.mult).then_inc(weighed_ready, 1)

            def add(g):
                dve.wait_ge(out_ready, g + 1)
                dve.tensor_tensor(group_of(chip.x, g), group_of(chip.x, g), out[:, :], ALU.add).then_inc(added, 1)

            def group(g, ahead):
                if ahead(2):
                    weigh(ahead(2))
                add(g)

            weigh(group_number(0))
            weigh(group_number(1))
            over_groups_ahead(dve, group, 2)

        block.__exit__(None, None, None)

class Chip:
    pass


def setup(nc, chip, ins, keep, x_from):
    rows_of = [("L0_b1", ins["L0_ffn_b1"].rearrange("e (t h) -> (e t) h", h=P), 32),
               ("L1_b1", ins["L1_ffn_b1"], 8),
               ("L2_b1", ins["L2_ffn_b1"].rearrange("e (t h) -> (e t) h", h=P), 32),
               ("L3_b1", ins["L3_ffn_b1"].rearrange("e (t h) -> (e t) h", h=P), 16),
               ("bih", ins["L1_gnn_bih"].rearrange("p (t h) -> (p t) h", h=P), 16),
               ("b_lin", ins["L0_gnn_b_lin"].rearrange("(a d) -> a d", a=1), 1),
               ("bg0", ins["L1_gnn_bg0"].rearrange("(a d) -> a d", a=1), 1),
               ("bhh", ins["L1_gnn_bhh"].rearrange("p (t h) -> (p t) h", h=P), 16)]
    at = {}
    n_rows = 0
    for name, _, n in rows_of:
        at[name] = n_rows
        n_rows += n
    wide_of = [("L0_b", ins["L0_gnn_b"], P), ("bg1", ins["L1_gnn_bg1"], P), ("gamma", ins["L2_ffn_gamma"], P),
               ("beta", ins["L2_ffn_beta"], P), ("L3_b", ins["L3_gnn_bias"], P), ("L0_bg", ins["L0_ffn_bg"], 8),
               ("L2_bg", ins["L2_ffn_gate_b"], 16), ("L3_bg", ins["L3_ffn_gate_b"], 8)]
    wide_at = {}
    n_wide = 0
    for name, _, n in wide_of:
        wide_at[name] = n_wide
        n_wide += n
    b2_of = [("L0", ins["L0_ffn_b2"], 8), ("L1", ins["L1_ffn_b2"], 8), ("L2", ins["L2_ffn_b2"], 16),
             ("L3", ins["L3_ffn_b2"], 8)]

    def kept(name, shape, dt=F32):
        return keep.enter_context(nc.sbuf_tensor(name, shape, dt))

    chip.ident = kept("ident", [P, P])[:, :]
    chip.ident_r = kept("ident_r", [P, P], F32R)[:, :]
    chip.ident_bf = kept("ident_bf", [P, P], BF16)
    chip.numbers = kept("numbers", [P, 16])
    chip.minus_half = kept("minus_half", [P, GB])
    chip.eps = kept("eps", [P, GB])
    chip.adj = kept("adj_rows", [P, P])
    chip.adj_t = kept("adj_t", [P, P])
    chip.columns = kept("columns", [P, n_rows])
    chip.gate_cols = kept("gate_cols", [P, 16 + 16 + 8])
    chip.lstm_bias = kept("lstm_bias", [P, 16])
    chip.wide = kept("wide", [P, n_wide])
    chip.zero_bias = kept("zero_bias", [P, 8])
    b2_tiles = [kept(f"b2_rows{n}", [P, P]) for n in range(2)]
    b2_rows = {"L0": b2_tiles[0][0:24, :], "L1": b2_tiles[0][32:56, :], "L3": b2_tiles[0][64:88, :],
               "L2": b2_tiles[1][0:48, :]}

    with Phase(nc, "setup") as ph:
        rows = ph.sb("rows", [n_rows, P])
        gate_rows = ph.sb("gate_rows", [16, P])
        wide_row = ph.sb("wide_row", [1, n_wide])
        ones = ph.sb("ones", [1, P])
        turned, gates_turned, adj_turned = ph.bank("turned"), ph.bank("gates_turned"), ph.bank("adj_turned")
        spread = [ph.bank("spread0"), ph.bank("spread1")]
        loaded = ph.sem("loaded")
        ident_zero = ph.sem("ident_zero")
        ident_step = ph.sem("ident_step")
        ones_set = ph.sem("ones_set")
        turn_done = ph.sem("turn_done")
        columns_ready = ph.sem("columns_ready")
        N_LOADS = len(rows_of) + 2 + 2 + len(wide_of) + len(b2_of) + 1

        block = nc.Block()
        block.__enter__()

        @block.sync
        def _(sp):
            for name, src, n in rows_of:
                sp.dma_start(rows[at[name]:at[name] + n, :], src).then_inc(loaded, 16)
            sp.dma_start(gate_rows[0:8, :], ins["L0_ffn_Wg"]).then_inc(loaded, 16)
            sp.dma_start(gate_rows[8:16, :], ins["L1_ffn_router_w"]).then_inc(loaded, 16)
            sp.dma_start(chip.gate_cols[:, 16:32], ins["L2_ffn_gate_w"]).then_inc(loaded, 16)
            sp.dma_start(chip.gate_cols[:, 32:40], ins["L3_ffn_gate_w"]).then_inc(loaded, 16)
            sp.dma_start(chip.adj[:, :], ins["adj"]).then_inc(loaded, 16)
            for name, src, n in wide_of:
                sp.dma_start(wide_row[:, wide_at[name]:wide_at[name] + n],
                             src.rearrange("(a d) -> a d", a=1)).then_inc(loaded, 16)
            sp.wait_ge(loaded, 16 * N_LOADS)

        @block.scalar
        def _(scalar):
            for name, src, E in b2_of:
                scalar.dma_start(b2_rows[name], src.unsqueeze(0).to_broadcast([3, E, P])).then_inc(loaded, 16)
            for c in range(4):
                graphs = slice(c * NB // 4, (c + 1) * NB // 4)
                scalar.dma_start(chip.x[:, c * NB * P // 4:(c + 1) * NB * P // 4].rearrange("n (b d) -> n b d", d=P),
                                 x_from[graphs].rearrange("b n d -> n b d")).then_inc(chip.x_loaded, 16)

        @block.gpsimd
        def _(pool):
            pool.memset(chip.ident, 0.0).then_inc(ident_zero, 1)
            pool.memset(chip.ident_bf[:, :], 0.0).then_inc(ident_zero, 1)
            pool.wait_ge(ident_zero, 2)
            for m in (chip.ident, chip.ident_bf[:, :]):
                pool.affine_select(out=m, in_=m, compare_op=ALU.not_equal, fill=1.0, base=0,
                                   pattern=[[-1, P]], channel_multiplier=1).then_inc(ident_step, 1)
            pool.wait_ge(ident_step, 1)
            pool.tensor_copy(chip.ident_r, chip.ident).then_inc(ident_step, 1)
            pool.iota(chip.numbers[:, :], [[1, 16]], base=0, channel_multiplier=0,
                      allow_small_or_imprecise_dtypes=True).then_inc(ident_step, 1)
            pool.memset(chip.minus_half[:, :], -0.5).then_inc(ident_step, 1)
            pool.memset(chip.zero_bias[:, :], 0.0).then_inc(ident_step, 1)
            pool.memset(chip.eps[:, :], EPS).then_inc(ident_step, 1)
            pool.memset(ones[:, :], 1.0).then_inc(ones_set, 1)

        @block.tensor
        def _(pe):
            pe.wait_ge(loaded, 16 * N_LOADS)
            pe.wait_ge(ident_step, 7)
            pe.wait_ge(ones_set, 1)
            pe.transpose(turned[:, 0:n_rows], rows[:, :], chip.ident[0:n_rows, 0:n_rows]).then_inc(turn_done, 1)
            pe.transpose(gates_turned[:, 0:16], gate_rows[:, :], chip.ident[0:16, 0:16]).then_inc(turn_done, 1)
            pe.transpose(adj_turned[:, 0:P], chip.adj[:, :], chip.ident).then_inc(turn_done, 1)
            pe.matmul(spread[0][:, :], ones[:, :], wide_row[:, 0:COLS], start=True, stop=True).then_inc(turn_done, 1)
            pe.matmul(spread[1][:, 0:n_wide - COLS], ones[:, :], wide_row[:, COLS:n_wide], start=True, stop=True)\
                .then_inc(turn_done, 1)

        @block.vector
        def _(dve):
            dve.wait_ge(turn_done, 5)
            dve.tensor_copy(chip.columns[:, :], turned[:, 0:n_rows]).then_inc(columns_ready, 1)
            dve.tensor_copy(chip.gate_cols[:, 0:16], gates_turned[:, 0:16])
            dve.tensor_copy(chip.adj_t[:, :], adj_turned[:, 0:P])
            dve.tensor_copy(chip.wide[:, 0:COLS], spread[0][:, :])
            dve.tensor_copy(chip.wide[:, COLS:n_wide], spread[1][:, 0:n_wide - COLS])
            dve.wait_ge(columns_ready, 1)
            dve.tensor_tensor(chip.lstm_bias[:, :], chip.columns[:, at["bih"]:at["bih"] + 16],
                              chip.columns[:, at["bhh"]:at["bhh"] + 16], ALU.add)

        block.__exit__(None, None, None)

    def table(b1, n_b1, b2, E, gates, bias):
        return {"b1": chip.columns[:, at[b1]:at[b1] + n_b1], "b2": b2_rows[b2], "gates": chip.gate_cols[:, gates:gates + E],
                "gate_bias": chip.zero_bias[:, 0:E] if bias is None else chip.wide[:, wide_at[bias]:wide_at[bias] + E]}

    chip.tables = {"L0": table("L0_b1", 32, "L0", 8, 0, "L0_bg"), "L1": table("L1_b1", 8, "L1", 8, 8, None),
                   "L2": table("L2_b1", 32, "L2", 16, 16, "L2_bg"), "L3": table("L3_b1", 16, "L3", 8, 32, "L3_bg")}
    for name in ("gamma", "beta", "L0_b", "bg1", "L3_b"):
        chip.tables["L2"][name] = chip.wide[:, wide_at[name]:wide_at[name] + P]
    chip.b_lin = chip.columns[:, at["b_lin"]:at["b_lin"] + 1]
    chip.bg0 = chip.columns[:, at["bg0"]:at["bg0"] + 1]


def load_experts(engine, chip, w1, w2, turned):
    tiles = w1.shape[0] * w1.shape[2] // P if not turned else w1.shape[0] * w1.shape[1] // P
    first = chip.raw[:, 0:tiles * P].rearrange("p (e f) -> p e f", e=w1.shape[0])
    second = chip.raw[:, tiles * P:2 * tiles * P]
    if turned:
        first = chip.raw[:, 0:tiles * P].rearrange("p (r f) -> p r f", f=P)
        engine.dma_start(first, w1.rearrange("e (t h) d -> h (e t) d", h=P)).then_inc(chip.raw_loaded, 16)
        second = second.rearrange("p (e f) -> p e f", e=w2.shape[0])
        engine.dma_start(second, w2.rearrange("e d h -> d e h")).then_inc(chip.raw_loaded, 16)
    else:
        engine.dma_start(first, w1.rearrange("e d h -> d e h")).then_inc(chip.raw_loaded, 16)
        second = second.rearrange("p (r f) -> p r f", f=P)
        engine.dma_start(second, w2.rearrange("e (t h) d -> h (e t) d", h=P)).then_inc(chip.raw_loaded, 16)


EXPERTS = {"L0": ("L0_ffn_W1", "L0_ffn_W2", 8, 4, ACT.Relu, "pair", "plain", True),
           "L1": ("L1_ffn_w1", "L1_ffn_w2", 8, 1, ACT.Gelu, "renormed", "normed", False),
           "L2": ("L2_ffn_w1", "L2_ffn_w2", 16, 2, ACT.Relu, "pair", "layernorm", False),
           "L3": ("L3_ffn_W1", "L3_ffn_W2", 8, 2, ACT.Gelu, "probs", "plain", False)}


GRAPH_LAYERS = {"attention": attention, "recurrent": recurrent, "three_hops": three_hops}


def program(nc, ins, out):
    with ExitStack() as keep:
        chip = Chip()
        chip.x = keep.enter_context(nc.sbuf_tensor("x_all", [P, NB * P], F32))
        chip.x_loaded = keep.enter_context(nc.semaphore("x_loaded"))
        chip.raw_loaded = keep.enter_context(nc.semaphore("raw_loaded"))
        chip.stored = keep.enter_context(nc.semaphore("stored"))
        setup(nc, chip, ins, keep, ins["x"])
        chip.edges = edge_storage(nc, keep)
        edge_tables(nc, chip, ins, chip.edges)
        with nc.Block() as block:
            @block.vector
            def _(dve):
                dve.wait_ge(chip.x_loaded, 64)
        for n, (graph_layer, experts) in enumerate(zip(("attention", "recurrent", "edges", "three_hops"),
                                                       ("L0", "L1", "L2", "L3"))):
            w1, w2, E, HT, act, weighting, residual, turned = EXPERTS[experts]
            raw = nc.sbuf_tensor(f"raw_experts{n}", [P, 2 * E * HT * P], F32, side="right")
            chip.raw = raw.__enter__()
            loads = 32 * (n + 1)

            def load(engine, w1=w1, w2=w2, turned=turned):
                load_experts(engine, chip, ins[w1], ins[w2], turned)

            with ExitStack() as halves:
                if graph_layer == "edges":
                    split = Split(nc, f"split{n}", chip, halves, loads, E * HT)
                    edges(nc, chip, ins, load, split)
                    high, low = split.high, split.low
                else:
                    GRAPH_LAYERS[graph_layer](nc, chip, ins, load)
                    high, low = split_experts(nc, f"split{n}", chip, halves, loads, E * HT, turned)
                raw.__exit__(None, None, None)
                mixture(nc, f"mix{n}", chip, (high, low), chip.tables[experts], E, HT, act, weighting, residual,
                        out if experts == "L3" else None)


_INS = ['x', 'adj', 'L0_gnn_W', 'L0_gnn_b_lin', 'L0_gnn_b', 'L0_ffn_Wg', 'L0_ffn_bg', 'L0_ffn_W1', 'L0_ffn_b1',
        'L0_ffn_W2', 'L0_ffn_b2', 'L1_gnn_Wg0', 'L1_gnn_bg0', 'L1_gnn_Wg1', 'L1_gnn_bg1', 'L1_gnn_Wih',
        'L1_gnn_Whh', 'L1_gnn_bih', 'L1_gnn_bhh', 'L1_ffn_router_w', 'L1_ffn_w1', 'L1_ffn_b1', 'L1_ffn_w2',
        'L1_ffn_b2', 'L2_gnn_W_lin', 'L2_gnn_W_val', 'L2_gnn_a', 'L2_gnn_W_out', 'L2_gnn_src', 'L2_gnn_dst',
        'L2_ffn_gate_w', 'L2_ffn_gate_b', 'L2_ffn_w1', 'L2_ffn_b1', 'L2_ffn_w2', 'L2_ffn_b2', 'L2_ffn_gamma',
        'L2_ffn_beta', 'L3_gnn_W', 'L3_gnn_bias', 'L3_ffn_gate_w', 'L3_ffn_gate_b', 'L3_ffn_W1', 'L3_ffn_b1',
        'L3_ffn_W2', 'L3_ffn_b2']


def kernel(**inputs):
    import numpy as _np
    import concourse.bacc as _bacc
    from concourse import mybir as _mybir
    from concourse.bass_utils import run_bass_kernel_spmd as _run

    nc = _bacc.Bacc("TRN2", target_bir_lowering=False, num_devices=1)
    arrays, ins = {}, {}
    for name in _INS:
        a = _np.ascontiguousarray(inputs[name])
        arrays[f"in_{name}_dram"] = a
        ins[name] = nc.dram_tensor(f"in_{name}_dram", a.shape, _mybir.dt.from_np(a.dtype), kind="ExternalInput").ap()
    out = nc.dram_tensor("out_0_dram", (NB, P, P), _mybir.dt.float32, kind="ExternalOutput").ap()
    program(nc, ins, out)
    r = _run(nc, [arrays], core_ids=[0])
    return r.results[0]["out_0_dram"]
```
